# Optimizing a Trainium2 kernel written in Bass

```python
import numpy as np
import jax
import jax.numpy as jnp

def _softmax(x, axis=-1):
    return jax.nn.softmax(x, axis=axis)

def _gelu(x):
    return jax.nn.gelu(x, approximate=True)

def _silu(x):
    return jax.nn.silu(x)

def _sigmoid(x):
    return jax.nn.sigmoid(x)

def _layernorm(x, axis=-1, eps=1e-05):
    m = jnp.mean(x, axis=axis, keepdims=True)
    v = jnp.var(x, axis=axis, keepdims=True)
    return (x - m) / jnp.sqrt(v + eps)

def _scatter_add(tgt, idx, src, axis=0):
    return tgt.at[idx].add(src)

def _segment_sum(src, seg, n):
    return jax.ops.segment_sum(src, seg, n)
kernel_name = 'mk_decoder_preln_d1_seqx_r4_d7d0c3'

def setup_inputs(seed: int=0):
    np.random.seed(seed)
    _w = jnp.asarray

    def _rec_inputs():
        import jax
        import jax.numpy as jnp
        _rk = jax.random.key(seed)
        x = -0.0003929 + 0.9999 * jax.random.normal(jax.random.fold_in(_rk, 1), (16, 256, 256), jnp.float32)
        _lenS = 256 - jax.random.randint(jax.random.fold_in(_rk, 7), (16,), 0, max(1, 256 // 4) + 1, jnp.int32)
        _lenS2 = 256 - jax.random.randint(jax.random.fold_in(_rk, 8), (16,), 0, max(1, 256 // 4) + 1, jnp.int32)
        _ctx_1024P = jax.random.normal(jax.random.fold_in(_rk, 11), (16, 16, 256), jnp.float32)
        _ctx_1024c = jax.random.dirichlet(jax.random.fold_in(_rk, 511), 0.3 * jnp.ones((16,), jnp.float32), (16, 256))
        _ctx_1024t = jnp.einsum('bsk,bkd->bsd', _ctx_1024c, _ctx_1024P)
        _ctx_1024t = _ctx_1024t * jax.lax.rsqrt(jnp.mean(jnp.square(_ctx_1024t)) + 1e-12) * 0.953939
        ctx_1024 = 2.81802e-05 + 1.00001 * (_ctx_1024t + 0.3 * jax.random.normal(jax.random.fold_in(_rk, 611), (16, 256, 256), jnp.float32))
        return (x, ctx_1024)
    x, ctx_1024 = _rec_inputs()

    def _L0_attn_setup():
        import jax, jax.numpy as jnp
        import numpy as np
        from functools import partial
        LN_EPS = 1000000.0
        FEAT_EPS = 1e-06

        def _layernorm(x, gamma, beta):
            mu = jnp.mean(x, axis=-1, keepdims=True)
            var = jnp.var(x, axis=-1, keepdims=True)
            return gamma * (x - mu) / jnp.sqrt(var + LN_EPS) + beta

        def _phi(x, omega):
            m = omega.shape[0]
            proj = jnp.einsum('bhsd,md->bhsm', x, omega)
            z = proj - 0.5 * jnp.sum(x * x, axis=-1, keepdims=True)
            z = z - jnp.max(z, axis=-1, keepdims=True)
            return jnp.exp(z) / jnp.sqrt(jnp.asarray(m, x.dtype)) + FEAT_EPS

        def _forward(batch, Wq, Wk, Wv, Wo, omega, W1, b1, W2, b2, gamma, beta):
            B, S, D = batch.shape
            M, dh = omega.shape
            H = D // dh
            scale = dh ** (-0.25)

            def heads(W):
                return (batch @ W).reshape(B, S, H, dh).transpose(0, 2, 1, 3)
            q = heads(Wq) * scale
            k = heads(Wk) * scale
            v = heads(Wv)
            qp = _phi(q, omega)
            kp = _phi(k, omega)
            qs = qp.transpose(2, 0, 1, 3)
            ks = kp.transpose(2, 0, 1, 3)
            vs = v.transpose(2, 0, 1, 3)

            def step(carry, qkv):
                S_kv, s_k = carry
                qt, kt, vt = qkv
                S_kv = S_kv + kt[..., :, None] * vt[..., None, :]
                s_k = s_k + kt
                num = jnp.einsum('bhm,bhmd->bhd', qt, S_kv)
                den = jnp.einsum('bhm,bhm->bh', qt, s_k)
                return ((S_kv, s_k), num / (den[..., None] + FEAT_EPS))
            carry0 = (jnp.zeros((B, H, M, dh), batch.dtype), jnp.zeros((B, H, M), batch.dtype))
            _, outs = jax.lax.scan(step, carry0, (qs, ks, vs))
            attn = outs.transpose(1, 0, 2, 3).reshape(B, S, D) @ Wo
            h = _layernorm(batch + attn, gamma, beta)
            out = jnp.maximum(h @ W1 + b1, 0.0) @ W2 + b2
            return out
        key = jax.random.key(seed)
        ks = jax.random.split(key, 8)
        B, S, D, H, dh, M, DFF = (4, 256, 256, 16, 64, 128, 1024)
        w = 0.02
        return {'batch': jax.random.normal(ks[0], (B, S, D), jnp.float32), 'Wq': jax.random.normal(ks[1], (D, D), jnp.float32) * w, 'Wk': jax.random.normal(ks[2], (D, D), jnp.float32) * w, 'Wv': jax.random.normal(ks[3], (D, D), jnp.float32) * w, 'Wo': jax.random.normal(ks[4], (D, D), jnp.float32) * w, 'omega': jax.random.normal(ks[5], (M, dh), jnp.float32), 'W1': jax.random.normal(ks[6], (D, DFF), jnp.float32) * w, 'b1': jnp.zeros((DFF,), jnp.float32), 'W2': jax.random.normal(ks[7], (DFF, D), jnp.float32) * w, 'b2': jnp.zeros((D,), jnp.float32), 'gamma': jnp.ones((D,), jnp.float32), 'beta': jnp.zeros((D,), jnp.float32)}
    _L0_attn_all = _L0_attn_setup()
    _L0_attn_in = {k: v for k, v in _L0_attn_all.items() if k in ('Wq', 'Wk', 'Wv', 'Wo', 'omega', 'W1', 'b1', 'W2', 'b2', 'gamma', 'beta')}
    del _L0_attn_all

    def _L0_xattn_setup():
        import jax, jax.numpy as jnp
        import numpy as np
        DIM = 256
        key = jax.random.key(seed)
        ks = jax.random.split(key, 9)
        B, S, D = (8, 512, DIM)
        inv = 1.0 / np.sqrt(D)
        return {'image_emb': jax.random.normal(ks[0], (B, S, D), dtype=jnp.float32), 'text_emb': jax.random.normal(ks[1], (B, S, D), dtype=jnp.float32), 'edge_index': jax.random.randint(ks[2], (2, 16), 0, 512, dtype=jnp.int64), 'Wq': jax.random.normal(ks[3], (D, D), dtype=jnp.float32) * inv, 'bq': jnp.zeros((D,), dtype=jnp.float32), 'Wk': jax.random.normal(ks[4], (D, D), dtype=jnp.float32) * inv, 'bk': jnp.zeros((D,), dtype=jnp.float32), 'Wv': jax.random.normal(ks[5], (D, D), dtype=jnp.float32) * inv, 'bv': jnp.zeros((D,), dtype=jnp.float32)}
    _L0_xattn_all = _L0_xattn_setup()
    _L0_xattn_in = {k: v for k, v in _L0_xattn_all.items() if k in ('edge_index', 'Wq', 'bq', 'Wk', 'bk', 'Wv', 'bv')}
    del _L0_xattn_all

    def _L0_ffn_setup():
        import jax, jax.numpy as jnp
        import numpy as np
        E = 16
        K = 2
        DIM = 256
        INTER = 176
        B, S = (4, 256)
        key = jax.random.key(seed)
        ks = jax.random.split(key, 5)
        x = jax.random.normal(ks[0], (B, S, DIM), dtype=jnp.float32)
        Wg = jax.random.normal(ks[1], (E, DIM), dtype=jnp.float32) * 0.02
        W1 = jax.random.normal(ks[2], (E, DIM, INTER), dtype=jnp.float32) * 0.02
        W3 = jax.random.normal(ks[3], (E, DIM, INTER), dtype=jnp.float32) * 0.02
        W2 = jax.random.normal(ks[4], (E, INTER, DIM), dtype=jnp.float32) * 0.02
        return {'x': x, 'Wg': Wg, 'W1': W1, 'W2': W2, 'W3': W3}
    _L0_ffn_all = _L0_ffn_setup()
    _L0_ffn_in = {k: v for k, v in _L0_ffn_all.items() if k in ('Wg', 'W1', 'W2', 'W3')}
    del _L0_ffn_all
    return {'x': x, 'ctx_1024': ctx_1024, 'L0_attn_Wq': _L0_attn_in['Wq'], 'L0_attn_Wk': _L0_attn_in['Wk'], 'L0_attn_Wv': _L0_attn_in['Wv'], 'L0_attn_Wo': _L0_attn_in['Wo'], 'L0_attn_omega': _L0_attn_in['omega'], 'L0_attn_W1': _L0_attn_in['W1'], 'L0_attn_b1': _L0_attn_in['b1'], 'L0_attn_W2': _L0_attn_in['W2'], 'L0_attn_b2': _L0_attn_in['b2'], 'L0_attn_gamma': _L0_attn_in['gamma'], 'L0_attn_beta': _L0_attn_in['beta'], 'L0_xattn_edge_index': _L0_xattn_in['edge_index'], 'L0_xattn_Wq': _L0_xattn_in['Wq'], 'L0_xattn_bq': _L0_xattn_in['bq'], 'L0_xattn_Wk': _L0_xattn_in['Wk'], 'L0_xattn_bk': _L0_xattn_in['bk'], 'L0_xattn_Wv': _L0_xattn_in['Wv'], 'L0_xattn_bv': _L0_xattn_in['bv'], 'L0_ffn_Wg': _L0_ffn_in['Wg'], 'L0_ffn_W1': _L0_ffn_in['W1'], 'L0_ffn_W2': _L0_ffn_in['W2'], 'L0_ffn_W3': _L0_ffn_in['W3']}

def reference(x, ctx_1024, L0_attn_Wq, L0_attn_Wk, L0_attn_Wv, L0_attn_Wo, L0_attn_omega, L0_attn_W1, L0_attn_b1, L0_attn_W2, L0_attn_b2, L0_attn_gamma, L0_attn_beta, L0_xattn_edge_index, L0_xattn_Wq, L0_xattn_bq, L0_xattn_Wk, L0_xattn_bk, L0_xattn_Wv, L0_xattn_bv, L0_ffn_Wg, L0_ffn_W1, L0_ffn_W2, L0_ffn_W3):
    import jax
    import jax.numpy as jnp

    def _L0_attn_ref(batch, Wq, Wk, Wv, Wo, omega, W1, b1, W2, b2, gamma, beta):
        import jax, jax.numpy as jnp
        import numpy as np
        from functools import partial
        LN_EPS = 1000000.0
        FEAT_EPS = 1e-06

        def _layernorm(x, gamma, beta):
            mu = jnp.mean(x, axis=-1, keepdims=True)
            var = jnp.var(x, axis=-1, keepdims=True)
            return gamma * (x - mu) / jnp.sqrt(var + LN_EPS) + beta

        def _phi(x, omega):
            m = omega.shape[0]
            proj = jnp.einsum('bhsd,md->bhsm', x, omega)
            z = proj - 0.5 * jnp.sum(x * x, axis=-1, keepdims=True)
            z = z - jnp.max(z, axis=-1, keepdims=True)
            return jnp.exp(z) / jnp.sqrt(jnp.asarray(m, x.dtype)) + FEAT_EPS

        def _forward(batch, Wq, Wk, Wv, Wo, omega, W1, b1, W2, b2, gamma, beta):
            B, S, D = batch.shape
            M, dh = omega.shape
            H = D // dh
            scale = dh ** (-0.25)

            def heads(W):
                return (batch @ W).reshape(B, S, H, dh).transpose(0, 2, 1, 3)
            q = heads(Wq) * scale
            k = heads(Wk) * scale
            v = heads(Wv)
            qp = _phi(q, omega)
            kp = _phi(k, omega)
            qs = qp.transpose(2, 0, 1, 3)
            ks = kp.transpose(2, 0, 1, 3)
            vs = v.transpose(2, 0, 1, 3)

            def step(carry, qkv):
                S_kv, s_k = carry
                qt, kt, vt = qkv
                S_kv = S_kv + kt[..., :, None] * vt[..., None, :]
                s_k = s_k + kt
                num = jnp.einsum('bhm,bhmd->bhd', qt, S_kv)
                den = jnp.einsum('bhm,bhm->bh', qt, s_k)
                return ((S_kv, s_k), num / (den[..., None] + FEAT_EPS))
            carry0 = (jnp.zeros((B, H, M, dh), batch.dtype), jnp.zeros((B, H, M), batch.dtype))
            _, outs = jax.lax.scan(step, carry0, (qs, ks, vs))
            attn = outs.transpose(1, 0, 2, 3).reshape(B, S, D) @ Wo
            h = _layernorm(batch + attn, gamma, beta)
            out = jnp.maximum(h @ W1 + b1, 0.0) @ W2 + b2
            return out
        return _forward(batch, Wq, Wk, Wv, Wo, omega, W1, b1, W2, b2, gamma, beta)

    def _L0_xattn_ref(image_emb, text_emb, edge_index, Wq, bq, Wk, bk, Wv, bv):
        import jax, jax.numpy as jnp
        import numpy as np
        DIM = 256
        D = image_emb.shape[-1]
        scale = D ** (-0.5)
        q = jnp.einsum('bsd,ed->bse', image_emb, Wq) + bq
        k = jnp.einsum('bsd,ed->bse', text_emb, Wk) + bk
        v = jnp.einsum('bsd,ed->bse', text_emb, Wv) + bv
        scores = jnp.einsum('bqd,bkd->bqk', q, k) * scale
        probs = jax.nn.softmax(scores, axis=-1)
        attended = jnp.einsum('bqk,bkd->bqd', probs, v)
        return attended

    def _L0_ffn_ref(x, Wg, W1, W2, W3):
        import jax, jax.numpy as jnp
        import numpy as np
        E = 16
        K = 2
        DIM = 256
        INTER = 176
        B, S = (4, 256)
        Bb, Ss, D = x.shape
        xf = x.reshape(-1, D)
        logits = xf @ Wg.T
        probs = jax.nn.softmax(logits, axis=-1)
        topw, topi = jax.lax.top_k(probs, K)
        topw = topw / topw.sum(axis=-1, keepdims=True)
        gates = (jax.nn.one_hot(topi, E, dtype=xf.dtype) * topw[..., None]).sum(axis=1)
        out = jnp.zeros_like(xf)
        for e in range(E):
            h = jax.nn.silu(xf @ W1[e]) * (xf @ W3[e])
            out = out + gates[:, e:e + 1] * (h @ W2[e])
        return out.reshape(Bb, Ss, D)
    x = x + _L0_attn_ref(_layernorm(x, axis=-1), L0_attn_Wq, L0_attn_Wk, L0_attn_Wv, L0_attn_Wo, L0_attn_omega, L0_attn_W1, L0_attn_b1, L0_attn_W2, L0_attn_b2, L0_attn_gamma, L0_attn_beta)
    x = x + _L0_xattn_ref(_layernorm(x, axis=-1), ctx_1024, L0_xattn_edge_index, L0_xattn_Wq, L0_xattn_bq, L0_xattn_Wk, L0_xattn_bk, L0_xattn_Wv, L0_xattn_bv)
    x = x + _L0_ffn_ref(_layernorm(x, axis=-1), L0_ffn_Wg, L0_ffn_W1, L0_ffn_W2, L0_ffn_W3)
    return x

_drawn_inputs = setup_inputs


def setup_inputs(seed=0):
    import zlib

    import numpy as np

    out = dict(_drawn_inputs(seed))
    spreads = {'L0_attn_b1': (0.0, 0.1),
     'L0_attn_b2': (0.0, 0.1),
     'L0_attn_gamma': (1.0, 0.6),
     'L0_attn_beta': (0.0, 0.647),
     'L0_xattn_bq': (0.0, 0.397),
     'L0_xattn_bk': (0.0, 0.8),
     'L0_xattn_bv': (0.0, 0.1)}
    factors = {'L0_attn_Wq': 8.0,
     'L0_attn_Wk': 8.0,
     'L0_attn_Wv': 8.0,
     'L0_attn_Wo': 8.0,
     'L0_attn_omega': 8.0,
     'L0_attn_W1': 4.915,
     'L0_ffn_Wg': 6.964,
     'L0_ffn_W1': 6.56,
     'L0_ffn_W2': 6.5,
     'L0_ffn_W3': 6.524}
    for name, (base, spread) in spreads.items():
        noise = np.random.default_rng([zlib.crc32(name.encode()), seed]).standard_normal(out[name].shape)
        drawn = base * np.exp(spread * noise) if base else spread * noise
        out[name] = jnp.asarray(drawn.astype(out[name].dtype))
    for name, factor in factors.items():
        out[name] = (out[name] * factor).astype(out[name].dtype)
    return out
```

```python
from contextlib import ExitStack

import concourse.bass as bass
from concourse import mybir

F32 = mybir.dt.float32
I32 = mybir.dt.int32
ALU = mybir.AluOpType
ACT = mybir.ActivationFunctionType
AX_X = mybir.AxisListType.X

P = 128
LN_EPS = 1e-5
ATTN_LN_EPS = 1e6
FEAT_EPS = 1e-6


def decoder(nc, x, ctxT, WqT, WkT, Wv, Wo, omegaT, W1, b1, W2, b2, gamma, beta,
            xWqT, xbq, xWkT, xbk, xWvT, xbv, WgT, E1, E3, E2, out):
    NSEQ, S, D = x.shape
    DC = D // P
    TS = S // P
    NT = NSEQ * TS
    DH, M = omegaT.shape
    H = D // DH
    FF = W1.shape[1]
    FC = FF // P
    NE = WgT.shape[1]
    INTER = E1.shape[2]
    IR = INTER - P
    TOPK = 2
    SLOT_TILES = NT * TOPK + NE
    NASSIGN = NT * P * TOPK
    SCORE_SCALE = float(D) ** -0.5
    PHI_SCALE = float(M) ** -0.5
    V1W = DH + 1
    ATW = S + P
    assert DC == 2 and TS == 2 and H * P == 512 and M == P and FC == 8

    xn3_dram = nc.dram_tensor("xn3_rows", (NT * P, D), F32, kind="Internal").ap()
    y_dram = nc.dram_tensor("expert_rows", (NASSIGN + SLOT_TILES * P, D), F32, kind="Internal").ap()

    x_v = x.rearrange("b (t p) d -> p (b t) d", p=P)
    out_v = out.rearrange("b (t p) d -> p (b t) d", p=P)
    ctx_v = ctxT.rearrange("b (c p) s -> p b c s", p=P)
    xn3_v = xn3_dram.rearrange("(t p) d -> p t d", p=P)
    y_v = y_dram[0:NASSIGN, :].rearrange("(t p j) d -> p t (j d)", p=P, j=TOPK)

    with ExitStack() as stack:
        def sb(name, shape, dt=F32):
            return stack.enter_context(nc.sbuf_tensor(name, shape, dt))

        def sem(name):
            return stack.enter_context(nc.semaphore(name))

        X = sb("X", [P, NT, D])
        wq_sb = sb("wq_sb", [P, DC, H * M])
        wk_sb = sb("wk_sb", [P, DC, H * M])
        wv_sb = sb("wv_sb", [P, DC, D])
        wo_sb = sb("wo_sb", [P, DC, D])
        w1_sb = sb("w1_sb", [P, DC, FF])
        w2_sb = sb("w2_sb", [P, FC, D])
        xwq_sb = sb("xwq_sb", [P, DC, D])
        xwk_sb = sb("xwk_sb", [P, DC, D])
        xwv_sb = sb("xwv_sb", [P, DC, D])
        wg_sb = sb("wg_sb", [P, DC, NE])
        e13_sb = sb("e13_sb", [P, DC, NE, 2 * INTER])
        b1_sb = sb("b1_sb", [P, FC])
        gam_sb = sb("gam_sb", [P, DC])
        bet_sb = sb("bet_sb", [P, DC])
        bq_sb = sb("bq_sb", [P, DC])
        bk_sb = sb("bk_sb", [P, DC])
        b2_sb = sb("b2_sb", [P, D])
        bv_sb = sb("bv_sb", [P, D])
        ident = sb("ident", [P, P])
        mask = sb("mask", [P, ATW])
        before = sb("before", [P, P])
        ones = sb("ones", [P, P])
        halfneg = sb("halfneg", [P, TS])
        eps_ln = sb("eps_ln", [P, TS])
        eps_attn = sb("eps_attn", [P, TS])
        feat_eps = sb("feat_eps", [P, 1])
        iota_slot = sb("iota_slot", [P, P])
        iota_tile = sb("iota_tile", [P, SLOT_TILES])
        iota_back = sb("iota_back", [P, NE])
        assign_no = sb("assign_no", [P, NT, TOPK])
        dump_no = sb("dump_no", [P, SLOT_TILES])

        wide = sb("wide", [P, 2 * NE * D])
        e2a_sb = wide[:, 0:NE * D].rearrange("p (e d) -> p e d", e=NE)
        e2b_sb = wide[:, NE * D:2 * NE * D].rearrange("p (e d) -> p e d", e=NE)
        at = 0
        phi = wide[:, at:at + 4 * H * M].rearrange("p (g h m) -> p g h m", g=4, h=H)
        at += 4 * H * M
        qpT = wide[:, at:at + H * S].rearrange("p (h s) -> p h s", h=H)
        at += H * S
        kpT = wide[:, at:at + H * S].rearrange("p (h s) -> p h s", h=H)
        at += H * S
        aT = wide[:, at:at + H * ATW].rearrange("p (h s) -> p h s", h=H)
        at += H * ATW
        fT = wide[:, at:at + FC * S].rearrange("p (f s) -> p f s", f=FC)
        at += FC * S
        assert at <= 2 * NE * D

        narrow = sb("narrow", [P, 17 * 512 + TS * H * V1W])
        place = [0]

        def carve(n):
            place[0] += n
            return narrow[:, place[0] - n:place[0]]

        def tile2():
            return carve(2 * 256).rearrange("p (a b) -> p a b", a=2)

        xn_next, xn, xnT, attn, attnT, y, hT = (tile2() for _ in range(7))
        xn2, xn2T, kT, qT, v2, pr, prT, xn3, xn3T, ctx = (tile2() for _ in range(10))
        v1 = carve(TS * H * V1W).rearrange("p (t h d) -> p t h d", t=TS, h=H)
        place[0] = 0
        oh1, oh2, oh, masked, tmp_a, tmp_b, tot = (carve(NT * NE).rearrange("p (t e) -> p t e", e=NE) for _ in range(7))
        HB = 4
        hot_slot = carve(HB * P).rearrange("p (u s) -> p u s", u=HB)
        hot_tile = carve(HB * SLOT_TILES).rearrange("p (u s) -> p u s", u=HB)
        early = carve(SLOT_TILES * NE).rearrange("p (s e) -> p s e", e=NE)
        place[0] = 0
        GB = 8
        PER = 16 // GB
        LAG = 2
        xg = carve(GB * D).rearrange("p (u d) -> p u d", u=GB)
        yg = carve(GB * D).rearrange("p (u d) -> p u d", u=GB)
        xgT = carve(2 * D).rearrange("p (u c s) -> p u c s", u=2, c=DC)
        silu = carve(2 * INTER).rearrange("p (u i) -> p u i", u=2)
        hid = carve(2 * INTER).rearrange("p (u i) -> p u i", u=2)
        hidT = carve(2 * 2 * P).rearrange("p (u c s) -> p u c s", u=2, c=2)
        place[0] = 0
        YB = 4
        yl = carve(YB * TS * TOPK * D).rearrange("p (u t j d) -> p u t j d", u=YB, t=TS, j=TOPK)

        logits = sb("logits", [P, NT, NE])
        stat = sb("stat", [P, 4, TS, 6])
        mv = sb("mv", [P, 4, TS, 2])
        veps = sb("veps", [P, 4, TS])
        rstd = sb("rstd", [P, 4, TS])
        nmax = sb("nmax", [P, 4, H])
        den = sb("den", [P, TS, H])
        rden = sb("rden", [P, TS, H])
        snmax = sb("snmax", [P, TS])
        ssum = sb("ssum", [P, TS])
        rsum = sb("rsum", [P, TS])
        best1, best2, pick1, pick2, gap, egap, gden, gate1, gate2 = (sb(n, [P, NT]) for n in (
            "best1", "best2", "pick1", "pick2", "gap", "egap", "gden", "gate1", "gate2"))
        need_i, need_s = sb("need_i", [P, NE], I32), sb("need_s", [P, NE], I32)
        need, cum_a, cum_b, base = (sb(n, [P, NE]) for n in ("need", "cum_a", "cum_b", "base"))
        slot = sb("slot", [P, NT, TOPK])
        slot_i, slot_hi_i, slot_lo_i = (sb(n, [P, NT, TOPK], I32) for n in ("slot_i", "slot_hi_i", "slot_lo_i"))
        slot_hi, slot_lo = sb("slot_hi", [P, NT, TOPK]), sb("slot_lo", [P, NT, TOPK])
        table, empty, scat_f, gath_f = (sb(n, [P, SLOT_TILES]) for n in ("table", "empty", "scat_f", "gath_f"))
        scat_i, gath_i, gath_j = (sb(n, [P, SLOT_TILES], I32) for n in ("scat_i", "gath_i", "gath_j"))
        expert_f = sb("expert_f", [P, SLOT_TILES])
        expert_i = sb("expert_i", [1, SLOT_TILES], I32)
        gidx = sb("gidx", [P, GB], I32)
        sidx = sb("sidx", [P, GB], I32)

        ps = stack.enter_context(nc.psum_tensor("ps", [P, 8, 512], F32))

        fuse_loaded, attn_loaded, ffn_loaded, cross_loaded = (sem(n) for n in (
            "fuse_loaded", "attn_loaded", "ffn_loaded", "cross_loaded"))
        em_loaded, e2_loaded = sem("em_loaded"), sem("e2_loaded")
        x_loaded, ctx_loaded, xn3_stored = sem("x_loaded"), sem("ctx_loaded"), sem("xn3_stored")
        blank, const_ready = sem("blank"), sem("const_ready")
        fused_ps, fused_ready = sem("fused_ps"), sem("fused_ready")
        stat_ready = [sem(f"stat{n}_ready") for n in range(4)]
        mv_ready = [sem(f"mv{n}_ready") for n in range(4)]
        veps_ready = [sem(f"veps{n}_ready") for n in range(4)]
        rstd_ready = [sem(f"rstd{n}_ready") for n in range(4)]
        xn_kept = sem("xn_kept")
        xn_ready, z_ready, xn2_ready, xn3_ready = sem("xn_ready"), sem("z_ready"), sem("xn2_ready"), sem("xn3_ready")
        xnT_ps, xnT_ready = sem("xnT_ps"), sem("xnT_ready")
        proj_ps, nmax_ready, phi_ready = sem("proj_ps"), sem("nmax_ready"), sem("phi_ready")
        v_ps, v1_ready = sem("v_ps"), sem("v1_ready")
        qpT_ps, qpT_ready, kpT_ps, kpT_ready = sem("qpT_ps"), sem("qpT_ready"), sem("kpT_ps"), sem("kpT_ready")
        aT_ps, aT_ready = sem("aT_ps"), sem("aT_ready")
        num_ps, den_ready, rden_ready, attn_ready = sem("num_ps"), sem("den_ready"), sem("rden_ready"), sem("attn_ready")
        attnT_ps, attnT_ready = sem("attnT_ps"), sem("attnT_ready")
        wo_ps, y_ready = sem("wo_ps"), sem("y_ready")
        zT_ps, hT_ready = sem("zT_ps"), sem("hT_ready")
        w1_ps, relu_act_ready, relu_dve_ready = sem("w1_ps"), sem("relu_act_ready"), sem("relu_dve_ready")
        w2_ps, xb2_ready, x1_ready = sem("w2_ps"), sem("xb2_ready"), sem("x1_ready")
        xn2T_ps, xn2T_ready = sem("xn2T_ps"), sem("xn2T_ready")
        k_ps, kT_ready, q_ps, qT_ready = sem("k_ps"), sem("kT_ready"), sem("q_ps"), sem("qT_ready")
        score_ps, snmax_ready, pr_ready, rsum_ready = sem("score_ps"), sem("snmax_ready"), sem("pr_ready"), sem("rsum_ready")
        v2_ps, v2_ready, prT_ps, prT_ready = sem("v2_ps"), sem("v2_ready"), sem("prT_ps"), sem("prT_ready")
        av_ps, xbv_ready, x2_ready = sem("av_ps"), sem("xbv_ready"), sem("x2_ready")
        xn3T_ps, xn3T_ready = sem("xn3T_ps"), sem("xn3T_ready")
        logit_ps, logit_ready = sem("logit_ps"), sem("logit_ready")
        routed = sem("routed")
        gap_ready, egap_ready, oh_ready, rank_ps, hot_ready, table_ps, plan_ready = (sem(n) for n in (
            "gap_ready", "egap_ready", "oh_ready", "rank_ps", "hot_ready", "table_ps", "plan_ready"))
        gidx_ready, sidx_ready = sem("gidx_ready"), sem("sidx_ready")
        gathered = [sem(f"gathered{u}") for u in range(GB)]
        scattered = [sem(f"scattered{u}") for u in range(GB)]
        xgT_ps, xgT_ready, e13_ps, silu_ready, hid_ready, hidT_ps, hidT_ready, e2_ps, yg_ready = (sem(n) for n in (
            "xgT_ps", "xgT_ready", "e13_ps", "silu_ready", "hid_ready", "hidT_ps", "hidT_ready", "e2_ps", "yg_ready"))
        y_loaded = [sem(f"y_loaded{u}") for u in range(YB)]
        part_ready, sum_ready, out_stored = sem("part_ready"), sem("sum_ready"), sem("out_stored")
        held = sem("held")

        N_CONST = 14

        def hold(eng, s, value):
            eng.wait_ge(s, value)
            eng.sem_inc(held)

        def in_turns(eng, turn):
            for i in range(3):
                turn(i, i, i - 1 if i >= 1 else None, i - 2 if i >= 2 else None, i + 1)
            with eng.Fori(3, NSEQ - 1) as i:
                turn(i, i, i - 1, i - 2, i + 1)
            turn(NSEQ - 1, NSEQ - 1, NSEQ - 2, NSEQ - 3, None)
            turn(NSEQ, None, NSEQ - 1, NSEQ - 2, None)
            turn(NSEQ + 1, None, None, NSEQ - 1, None)

        def in_groups(step, eng):
            for u in range(GB):
                step(u, u, False)
            with eng.Fori(1, SLOT_TILES // GB - 1) as g:
                for u in range(GB):
                    step(g * GB + u, u, False)
            for u in range(GB):
                step(SLOT_TILES - GB + u, u, True)

        def first(n):
            return isinstance(n, int) and n == 0

        def tiles_of(seq):
            return bass.ds(seq * TS, TS)

        block = stack.enter_context(nc.Block())

        @block.sync
        def _(sp):
            def load(dst, src, s):
                sp.dma_start(dst, src).then_inc(s, 16)

            def load_x(n):
                if not first(n):
                    sp.wait_ge(x_loaded, n * 16)
                sp.dma_start(X[:, tiles_of(n), :], x_v[:, tiles_of(n), :]).then_inc(x_loaded, 16)

            load_x(0)
            stage = e13_sb[:, :, :, :].rearrange("p c e i -> p (c e i)")
            load(stage[0:DH, 0:H * D].rearrange("p (h d) -> p h d", h=H), WqT.rearrange("(h e) d -> e h d", h=H), fuse_loaded)
            load(stage[0:DH, H * D:2 * H * D].rearrange("p (h d) -> p h d", h=H), WkT.rearrange("(h e) d -> e h d", h=H), fuse_loaded)
            load(stage[0:DH, 2 * H * D:2 * H * D + M], omegaT, fuse_loaded)
            load(wv_sb[:, :, :], Wv.rearrange("(c p) n -> p c n", p=P), attn_loaded)
            load(wo_sb[:, :, :], Wo.rearrange("(c p) n -> p c n", p=P), attn_loaded)
            load(gam_sb[:, :], gamma, attn_loaded)
            load(bet_sb[:, :], beta, attn_loaded)
            load(w1_sb[:, :, :], W1.rearrange("(c p) n -> p c n", p=P), ffn_loaded)
            load(b1_sb[:, :], b1, ffn_loaded)
            load(w2_sb[:, :, :], W2.rearrange("(c p) n -> p c n", p=P), ffn_loaded)
            load(b2_sb[:, :], b2.partition_broadcast(P), ffn_loaded)
            load(xwq_sb[:, :, :], xWqT.rearrange("(c p) n -> p c n", p=P), cross_loaded)
            load(xwk_sb[:, :, :], xWkT.rearrange("(c p) n -> p c n", p=P), cross_loaded)
            load(xwv_sb[:, :, :], xWvT.rearrange("(c p) n -> p c n", p=P), cross_loaded)
            load(bq_sb[:, :], xbq, cross_loaded)
            load(bk_sb[:, :], xbk, cross_loaded)
            load(bv_sb[:, :], xbv.partition_broadcast(P), cross_loaded)
            load(wg_sb[:, :, :], WgT.rearrange("(c p) n -> p c n", p=P), cross_loaded)
            load(ctx, ctx_v[:, 0, :, :], ctx_loaded)
            sp.wait_ge(fused_ps, 4)
            for c in range(DC):
                for n, w in enumerate((E1, E3)):
                    load(e13_sb[:, c, :, n * INTER:(n + 1) * INTER],
                         w[:, c * P:(c + 1) * P, :].rearrange("e p i -> p e i"), em_loaded)

            def turn(i, a, f, b, nxt):
                if nxt is not None:
                    load_x(nxt)
                if b is not None:
                    if not (isinstance(b, int) and b == NSEQ - 1):
                        sp.wait_ge(v2_ps, b + 1)
                        sp.dma_start(ctx, ctx_v[:, bass.ds(b + 1, 1), :, :]
                                     .rearrange("p b c s -> p (b c) s")).then_inc(ctx_loaded, 16)
                    sp.wait_ge(xn3_ready, b + 1)
                    sp.dma_start(xn3_v[:, tiles_of(b), :], xn3).then_inc(xn3_stored, 16)

            in_turns(sp, turn)
            sp.wait_ge(w2_ps, NSEQ)
            sp.wait_ge(num_ps, NSEQ)
            load(e2a_sb, E2[:, 0:P, :].rearrange("e p d -> p e d"), e2_loaded)
            load(e2b_sb[0:IR], E2[:, P:INTER, :].rearrange("e p d -> p e d"), e2_loaded)

            for u in range(GB):
                sp.wait_ge(scattered[u], 16 * (SLOT_TILES // GB))
            sp.wait_ge(yg_ready, SLOT_TILES)

            def fetch(n, u):
                if not (isinstance(n, int) and n < YB):
                    sp.wait_ge(sum_ready, n - YB + 1)
                sp.dma_start(yl[:, u].rearrange("p t j d -> p t (j d)"), y_v[:, tiles_of(n), :])\
                    .then_inc(y_loaded[u], 16)

            for u in range(YB):
                fetch(u, u)
            with sp.Fori(1, NSEQ // YB) as g:
                for u in range(YB):
                    fetch(g * YB + u, u)

        @block.gpsimd
        def _(pool):
            pool.memset(ones[:, :], 1.0).then_inc(blank, 1)
            pool.memset(halfneg[:, :], -0.5).then_inc(const_ready, 1)
            pool.memset(eps_ln[:, :], LN_EPS).then_inc(const_ready, 1)
            pool.memset(eps_attn[:, :], ATTN_LN_EPS).then_inc(const_ready, 1)
            pool.memset(feat_eps[:, :], FEAT_EPS).then_inc(const_ready, 1)
            pool.memset(v1[:, :, :, DH:V1W], 1.0).then_inc(const_ready, 1)
            pool.memset(mask[:, :], 1.0).then_inc(blank, 1)
            pool.wait_ge(blank, 2)
            pool.affine_select(out=ident[:, :], in_=ones[:, :], compare_op=ALU.is_equal, fill=0.0, base=0,
                               pattern=[[-1, P]], channel_multiplier=1).then_inc(const_ready, 1)
            pool.affine_select(out=before[:, :], in_=ones[:, :], compare_op=ALU.is_gt, fill=0.0, base=0,
                               pattern=[[1, P]], channel_multiplier=-1).then_inc(const_ready, 1)
            for lo in (0, S):
                pool.affine_select(out=mask[:, lo:lo + P], in_=mask[:, lo:lo + P], compare_op=ALU.is_ge, fill=0.0,
                                   base=0, pattern=[[1, P]], channel_multiplier=-1).then_inc(const_ready, 1)
            fl = {"allow_small_or_imprecise_dtypes": True}
            pool.iota(iota_slot[:, :], pattern=[[1, P]], base=0, channel_multiplier=0, **fl).then_inc(const_ready, 1)
            pool.iota(iota_tile[:, :], pattern=[[1, SLOT_TILES]], base=0, channel_multiplier=0, **fl)\
                .then_inc(const_ready, 1)
            pool.iota(iota_back[:, :], pattern=[[-1, NE]], base=NE, channel_multiplier=0, **fl)\
                .then_inc(const_ready, 1)
            pool.iota(assign_no[:, :, :], pattern=[[P * TOPK, NT], [1, TOPK]], base=1, channel_multiplier=TOPK, **fl)\
                .then_inc(const_ready, 1)
            pool.iota(dump_no[:, :], pattern=[[P, SLOT_TILES]], base=NASSIGN + 1, channel_multiplier=1, **fl)\
                .then_inc(const_ready, 1)
            pool.wait_ge(const_ready, N_CONST)
            pool.wait_ge(ffn_loaded, 16 * 4)
            pool.wait_ge(cross_loaded, 16 * 7)

            def root(n, seq, eps):
                pool.wait_ge(mv_ready[n], seq + 1)
                pool.tensor_tensor(veps[:, n, :], mv[:, n, :, 1], eps[:, :], ALU.add).then_inc(veps_ready[n], 1)
                pool.wait_ge(veps_ready[n], seq + 1)
                pool.tensor_tensor(rstd[:, n, :], veps[:, n, :], halfneg[:, :], ALU.pow).then_inc(rstd_ready[n], 1)

            def add_bias(seq, row, after, done):
                hold(pool, after, seq + 1)
                xs = X[:, tiles_of(seq), :]
                pool.tensor_tensor(xs, xs, row[:, :].unsqueeze(1).broadcast_to([P, TS, D]), ALU.add).then_inc(done, 1)

            def turn(i, a, f, b, nxt):
                if a is not None:
                    hold(pool, xn_ready, a + 1)
                    if not first(a):
                        hold(pool, y_ready, a)
                    pool.tensor_copy(xn, xn_next).then_inc(xn_kept, 1)
                    add_bias(a, b2_sb, xn_ready, xb2_ready)
                if nxt is not None:
                    root(0, nxt, eps_ln)
                if b is not None:
                    add_bias(b, bv_sb, xn2_ready, xbv_ready)
                    root(3, b, eps_ln)
                if f is not None:
                    root(2, f, eps_ln)
                if a is not None:
                    root(1, a, eps_attn)

            root(0, 0, eps_ln)
            in_turns(pool, turn)

            pool.wait_ge(plan_ready, 1)
            pool.wait_ge(xn3_stored, 16 * NSEQ)

            def gather(s, u):
                if not (isinstance(s, int) and s < GB):
                    hold(pool, xgT_ps, s - GB + 1)
                pool.tensor_copy(gidx[:, u:u + 1], gath_i[:, bass.ds(s, 1)]).then_inc(gidx_ready, 1)
                hold(pool, gidx_ready, s + 1)
                pool.indirect_dma_start(xg[:, u, :], None, xn3_dram, bass.IndirectOffsetOnAxis(gidx[:, u:u + 1], 0))\
                    .then_inc(gathered[u], 16)

            def scatter(s, u):
                if not (isinstance(s, int) and s < GB):
                    hold(pool, scattered[u], (s - u) * PER)
                pool.tensor_copy(sidx[:, u:u + 1], scat_i[:, bass.ds(s, 1)]).then_inc(sidx_ready, 1)
                hold(pool, sidx_ready, s + 1)
                hold(pool, yg_ready, s + 1)
                pool.indirect_dma_start(y_dram, bass.IndirectOffsetOnAxis(sidx[:, u:u + 1], 0), yg[:, u, :], None)\
                    .then_inc(scattered[u], 16)

            for s in range(GB):
                gather(s, s)

            def slot_tiles(s, u, last):
                if not last:
                    gather(s + GB, u)
                if not (isinstance(s, int) and s < LAG):
                    scatter(s - LAG, (u - LAG) % GB)

            in_groups(slot_tiles, pool)
            for u in range(GB - LAG, GB):
                scatter(SLOT_TILES - GB + u, u)
            for u in range(GB):
                pool.wait_ge(scattered[u], 16 * (SLOT_TILES // GB))

        @block.tensor
        def _(pe):
            def mm(out_, lhsT, rhs, start=True, stop=True):
                return pe.matmul(out_, lhsT, rhs, start=start, stop=stop)

            def turn_tiles(bank, src):
                for c in range(DC):
                    for t in range(TS):
                        lo = c * S + t * P
                        last = pe.transpose(ps[:, bank, lo:lo + P], src[:, t, c * P:(c + 1) * P], ident[:, :])
                return last

            def by_token(bank, srcT, w, n):
                for t in range(TS):
                    for c in range(DC):
                        last = mm(ps[:, bank, t * n:(t + 1) * n], srcT[:, c, t * P:(t + 1) * P], w[:, c, 0:n],
                                  c == 0, c == DC - 1)
                return last

            def by_feature(bank, srcT, w):
                for e in range(DC):
                    for c in range(DC):
                        last = mm(ps[:, bank, e * S:(e + 1) * S], w[:, c, e * P:(e + 1) * P], srcT[:, c, :],
                                  c == 0, c == DC - 1)
                return last

            pe.wait_ge(fuse_loaded, 16 * 3)
            pe.wait_ge(const_ready, N_CONST)
            stage = e13_sb[:, :, :, :].rearrange("p c e i -> p (c e i)")
            for n in range(2):
                for c in range(DC):
                    for h in range(H):
                        lo = n * H * D + h * D + c * P
                        last = mm(ps[:, 2 * n + c, h * M:(h + 1) * M], stage[0:DH, lo:lo + P],
                                  stage[0:DH, 2 * H * D:2 * H * D + M])
                    last.then_inc(fused_ps, 1)
            pe.wait_ge(fused_ready, 4)
            pe.wait_ge(attn_loaded, 16 * 4)

            def turn(i, a, f, b, nxt):
                if a is not None:
                    pe.wait_ge(xn_ready, a + 1)
                    turn_tiles(5, xn_next).then_inc(xnT_ps, 1)
                if b is not None:
                    if first(b):
                        pe.wait_ge(cross_loaded, 16 * 7)
                    else:
                        pe.wait_ge(logit_ready, b)
                    pe.wait_ge(xn2_ready, b + 1)
                    turn_tiles(6, xn2).then_inc(xn2T_ps, 1)
                    pe.wait_ge(ctx_loaded, (b + 1) * 16)
                    by_feature(7, ctx, xwk_sb).then_inc(k_ps, 1)
                if a is not None:
                    pe.wait_ge(xnT_ready, a + 1)
                    by_token(5, xnT, wv_sb, D).then_inc(v_ps, 1)
                if b is not None:
                    pe.wait_ge(xn2T_ready, b + 1)
                    by_feature(6, xn2T, xwq_sb).then_inc(q_ps, 1)
                if f is not None:
                    pe.wait_ge(z_ready, f + 1)
                    turn_tiles(4, y).then_inc(zT_ps, 1)
                if b is not None:
                    pe.wait_ge(kT_ready, b + 1)
                    pe.wait_ge(qT_ready, b + 1)
                    for t in range(TS):
                        for c in range(DC):
                            last = mm(ps[:, 7, t * S:(t + 1) * S], qT[:, c, t * P:(t + 1) * P], kT[:, c, :],
                                      c == 0, c == DC - 1)
                    last.then_inc(score_ps, 1)
                if f is not None:
                    if first(f):
                        pe.wait_ge(ffn_loaded, 16 * 4)
                    pe.wait_ge(hT_ready, f + 1)
                    for ff in range(FC):
                        for c in range(DC):
                            last = mm(ps[:, ff // 2, ff % 2 * S:(ff % 2 + 1) * S], w1_sb[:, c, ff * P:(ff + 1) * P],
                                      hT[:, c, :], c == 0, c == DC - 1)
                        if ff % 2:
                            last.then_inc(w1_ps, 1)

                def project(g, w):
                    if f is not None:
                        if g % 2 == 0:
                            pe.wait_ge(relu_act_ready, f * 2 + (g // 2 + 1))
                        else:
                            pe.wait_ge(relu_dve_ready, f * 2 + (g // 2 + 1))
                    t = g % TS
                    for c in range(DC):
                        last = mm(ps[:, g, :], xnT[:, c, t * P:(t + 1) * P], w[:, c, :], c == 0, c == DC - 1)
                    last.then_inc(proj_ps, 1)

                if a is not None:
                    project(0, wq_sb)
                    project(1, wq_sb)
                if b is not None:
                    by_token(6, ctx, xwv_sb, D).then_inc(v2_ps, 1)
                if a is not None:
                    project(2, wk_sb)
                    project(3, wk_sb)
                if b is not None:
                    pe.wait_ge(pr_ready, b + 1)
                    turn_tiles(7, pr).then_inc(prT_ps, 1)

                def ffn_out(t):
                    for ff in range(FC):
                        last = mm(ps[:, 4, t * D:(t + 1) * D], fT[:, ff, t * P:(t + 1) * P], w2_sb[:, ff, :],
                                  ff == 0, ff == FC - 1)
                    return last

                if f is not None:
                    pe.wait_ge(relu_act_ready, f * 2 + 2)
                    pe.wait_ge(relu_dve_ready, f * 2 + 2)
                    ffn_out(0)

                def turn_phi(g0, done):
                    pe.wait_ge(phi_ready, a * 4 + (g0 + 2))
                    for h in range(H):
                        for t in range(TS):
                            last = pe.transpose(ps[:, g0 + h // 2, h % 2 * S + t * P:h % 2 * S + (t + 1) * P],
                                                phi[:, g0 + t, h, :], ident[:, :])
                        if h % 2:
                            last.then_inc(done, 1)

                if a is not None:
                    turn_phi(0, qpT_ps)
                    turn_phi(2, kpT_ps)
                    pe.wait_ge(qpT_ready, a + 1)
                    pe.wait_ge(kpT_ready, a + 1)
                    for h in range(H):
                        mm(ps[:, h, 0:S], kpT[:, h, 0:P], qpT[:, h, :])
                        mm(ps[:, h, S:ATW], kpT[:, h, P:S], qpT[:, h, P:S]).then_inc(aT_ps, 1)
                if b is not None:
                    pe.wait_ge(prT_ready, b + 1)
                    pe.wait_ge(v2_ready, b + 1)
                    by_token(6, prT, v2, D).then_inc(av_ps, 1)
                if a is not None:
                    pe.wait_ge(v1_ready, a + 1)
                    for h in range(H):
                        pe.wait_ge(aT_ready, a * 4 + (h + 1 if h > 1 else 2))
                        col = slice(h * V1W, (h + 1) * V1W)
                        mm(ps[:, 0, col], aT[:, h, 0:P], v1[:, 0, h, :])
                        mm(ps[:, 1, col], aT[:, h, P:S], v1[:, 0, h, :], True, False)
                        last = mm(ps[:, 1, col], aT[:, h, S:ATW], v1[:, 1, h, :], False, True)
                    last.then_inc(num_ps, 1)
                if f is not None:
                    ffn_out(1).then_inc(w2_ps, 1)
                if b is not None:
                    pe.wait_ge(xn3_ready, b + 1)
                    turn_tiles(7, xn3).then_inc(xn3T_ps, 1)
                if a is not None:
                    pe.wait_ge(attn_ready, a + 1)
                    turn_tiles(2, attn).then_inc(attnT_ps, 1)
                if b is not None:
                    pe.wait_ge(xn3T_ready, b + 1)
                    by_token(6, xn3T, wg_sb, NE).then_inc(logit_ps, 1)
                if a is not None:
                    pe.wait_ge(attnT_ready, a + 1)
                    by_token(3, attnT, wo_sb, D).then_inc(wo_ps, 1)

            in_turns(pe, turn)

            pe.wait_ge(oh_ready, 1)
            oh_all = oh.rearrange("p t e -> p (t e)")
            mm(ps[:, 0, :], before[:, :], oh_all)
            mm(ps[:, 1, :], ones[:, :], oh_all).then_inc(rank_ps, 1)
            def place_assignments(g, begin, end):
                for k in range(HB):
                    pe.wait_ge(hot_ready, g * HB + (k + 1))
                    pe.matmul(ps[:, 2, 0:SLOT_TILES], hot_slot[:, k, :], hot_tile[:, k, :], start=begin and k == 0,
                              stop=end and k == HB - 1).then_inc(table_ps, 1)

            HG = NT * TOPK // HB
            place_assignments(0, True, False)
            with pe.Fori(1, HG - 1) as g:
                place_assignments(g, False, False)
            place_assignments(HG - 1, False, True)

            pe.wait_ge(em_loaded, 16 * 4)
            pe.wait_ge(e2_loaded, 16 * 2)
            pe.wait_ge(plan_ready, 1)

            def expert_of(s):
                return pe.value_load(expert_i[0:1, bass.ds(s, 1)], min_val=0, max_val=NE - 1)

            def turn_rows(s, u):
                pe.wait_ge(gathered[u], (s - u) * PER + 16)
                for c in range(DC):
                    last = pe.transpose(ps[:, u % 2, c * P:(c + 1) * P], xg[:, u, c * P:(c + 1) * P], ident[:, :])
                last.then_inc(xgT_ps, 1)

            def up(s, u):
                e = expert_of(s)
                pe.wait_ge(xgT_ready, s + 1)
                for c in range(DC):
                    last = mm(ps[:, 2 + u % 2, 0:2 * INTER], xgT[:, u % 2, c, :],
                              e13_sb[:, c, bass.ds(e, 1), :].rearrange("p e i -> p (e i)"), c == 0, c == DC - 1)
                last.then_inc(e13_ps, 1)

            def turn_hidden(s, u):
                pe.wait_ge(hid_ready, s + 1)
                pe.transpose(ps[:, 4 + u % 2, 0:P], hid[:, u % 2, 0:P], ident[:, :])
                pe.transpose(ps[0:IR, 4 + u % 2, P:2 * P], hid[:, u % 2, P:INTER], ident[:, :]).then_inc(hidT_ps, 1)

            def down(s, u):
                e = expert_of(s)
                if not (isinstance(s, int) and s < 2):
                    pe.wait_ge(yg_ready, s - 1)
                pe.wait_ge(hidT_ready, s + 1)
                mm(ps[:, 6 + u % 2, 0:D], hidT[:, u % 2, 0, :], e2a_sb[:, bass.ds(e, 1), :]
                   .rearrange("p e d -> p (e d)"), True, False)
                mm(ps[:, 6 + u % 2, 0:D], hidT[0:IR, u % 2, 1, :], e2b_sb[0:IR, bass.ds(e, 1), :]
                   .rearrange("p e d -> p (e d)"), False, True).then_inc(e2_ps, 1)

            turn_rows(0, 0)
            turn_rows(1, 1)
            up(0, 0)

            def slot_tiles(s, u, last):
                if not (last and u + 2 >= GB):
                    turn_rows(s + 2, (u + 2) % GB)
                if not (last and u + 1 >= GB):
                    up(s + 1, (u + 1) % GB)
                if not first(s):
                    down(s - 1, (u - 1) % GB)
                turn_hidden(s, u)

            in_groups(slot_tiles, pe)
            down(SLOT_TILES - 1, GB - 1)

        @block.scalar
        def _(act):
            def copy(out_, in_):
                return act.activation(out_, in_, ACT.Copy)

            def bank(n):
                return ps[:, n, :].rearrange("p (a b) -> p a b", a=2)

            act.wait_ge(const_ready, N_CONST)
            for n, w in enumerate((wq_sb, wk_sb)):
                for c in range(DC):
                    act.wait_ge(fused_ps, 2 * n + c + 1)
                    act.mul(w[:, c, :], ps[:, 2 * n + c, :], float(DH) ** -0.25).then_inc(fused_ready, 1)

            def turn(i, a, f, b, nxt):
                if a is not None:
                    act.wait_ge(xnT_ps, a + 1)
                    copy(xnT, bank(5)).then_inc(xnT_ready, 1)
                if b is not None:
                    act.wait_ge(xn2T_ps, b + 1)
                    copy(xn2T, bank(6)).then_inc(xn2T_ready, 1)
                if a is not None:
                    act.wait_ge(v_ps, a + 1)
                    copy(v1[:, :, :, 0:DH], ps[:, 5, :].rearrange("p (t h d) -> p t h d", t=TS, h=H))\
                        .then_inc(v1_ready, 1)
                if f is not None:
                    if first(f):
                        act.wait_ge(attn_loaded, 16 * 4)
                        act.wait_ge(ffn_loaded, 16 * 4)
                    act.wait_ge(zT_ps, f + 1)
                    for c in range(DC):
                        last = act.activation(hT[:, c, :], bank(4)[:, c, :], ACT.Identity, bias=bet_sb[:, c:c + 1],
                                              scale=gam_sb[:, c:c + 1])
                    last.then_inc(hT_ready, 1)
                if b is not None:
                    act.wait_ge(snmax_ready, b + 1)
                    for t in range(TS):
                        last = act.activation(pr[:, t, :], bank(7)[:, t, :], ACT.Exp, bias=snmax[:, t:t + 1],
                                              accum_out=ssum[:, t:t + 1])
                    last.then_inc(pr_ready, 1)
                if f is not None:
                    for g in (0, 2):
                        act.wait_ge(w1_ps, f * 4 + (g + 1))
                        for n in range(2):
                            last = act.activation(fT[:, 2 * g + n, :], bank(g)[:, n, :], ACT.Relu,
                                                  bias=b1_sb[:, 2 * g + n:2 * g + n + 1])
                        last.then_inc(relu_act_ready, 1)

                def features(g):
                    act.wait_ge(nmax_ready, a * 4 + (g + 1))
                    for h in range(H):
                        last = act.activation(phi[:, g, h, :], ps[:, g, h * M:(h + 1) * M], ACT.Exp,
                                              bias=nmax[:, g, h:h + 1])
                    last.then_inc(phi_ready, 1)

                if a is not None:
                    features(0)
                    features(1)
                if b is not None:
                    act.wait_ge(v2_ps, b + 1)
                    copy(v2, bank(6)).then_inc(v2_ready, 1)
                if a is not None:
                    features(2)
                    features(3)
                    for n in range(2):
                        act.wait_ge(qpT_ps, a * 2 + (n + 1))
                        last = act.activation(qpT[:, 2 * n:2 * n + 2, :], bank(n), ACT.Identity,
                                              bias=feat_eps[:, 0:1], scale=PHI_SCALE)
                    last.then_inc(qpT_ready, 1)
                if b is not None:
                    act.wait_ge(xn3T_ps, b + 1)
                    copy(xn3T, bank(7)).then_inc(xn3T_ready, 1)
                if a is not None:
                    act.wait_ge(attnT_ps, a + 1)
                    copy(attnT, bank(2)).then_inc(attnT_ready, 1)

            in_turns(act, turn)

            act.wait_ge(gap_ready, 1)
            act.activation(egap[:, :], gap[:, :], ACT.Exp).then_inc(egap_ready, 1)
            act.wait_ge(plan_ready, 1)

            def gate_half(s, u):
                if not (isinstance(s, int) and s < 2):
                    act.wait_ge(hid_ready, s - 1)
                act.wait_ge(e13_ps, s + 1)
                act.activation(silu[:, u % 2, :], ps[:, 2 + u % 2, 0:INTER], ACT.Silu).then_inc(silu_ready, 1)

            def rows_out(s, u):
                if not (isinstance(s, int) and s < GB):
                    act.wait_ge(scattered[u], (s - u) * PER)
                act.wait_ge(e2_ps, s + 1)
                copy(yg[:, u, :], ps[:, 6 + u % 2, 0:D]).then_inc(yg_ready, 1)

            gate_half(0, 0)

            def slot_tiles(s, u, last):
                if not (last and u + 1 >= GB):
                    gate_half(s + 1, (u + 1) % GB)
                if not first(s):
                    rows_out(s - 1, (u - 1) % GB)

            in_groups(slot_tiles, act)
            rows_out(SLOT_TILES - 1, GB - 1)

            with act.Fori(0, NSEQ) as n:
                act.wait_ge(sum_ready, n + 1)
                act.dma_start(out_v[:, tiles_of(n), :], X[:, tiles_of(n), :]).then_inc(out_stored, 16)
            act.wait_ge(out_stored, 16 * NSEQ)

        @block.vector
        def _(dve):
            def bank(n):
                return ps[:, n, :].rearrange("p (a b) -> p a b", a=2)

            def x_tile(seq, t):
                return X[:, bass.ds(seq * TS + t, 1), :].rearrange("p t d -> p (t d)")

            def ln_stats(n, seq, src):
                for t in range(TS):
                    last = dve.bn_stats(stat[:, n, t, :], src(t))
                last.then_inc(stat_ready[n], 1)
                hold(dve, stat_ready[n], seq + 1)
                for t in range(TS):
                    last = dve.bn_aggr(mv[:, n, t, :], stat[:, n, t, :])
                last.then_inc(mv_ready[n], 1)

            def ln_apply(n, seq, src, dst, done):
                dve.wait_ge(mv_ready[n], seq + 1)
                dve.wait_ge(rstd_ready[n], seq + 1)
                for t in range(TS):
                    last = dve.tensor_scalar(dst[:, t, :], src(t), mv[:, n, t, 0:1], rstd[:, n, t:t + 1],
                                             ALU.subtract, ALU.mult)
                last.then_inc(done, 1)

            dve.wait_ge(const_ready, N_CONST)
            hold(dve, x_loaded, 16)
            ln_stats(0, 0, lambda t: x_tile(0, t))
            ln_apply(0, 0, lambda t: x_tile(0, t), xn_next, xn_ready)

            def turn(i, a, f, b, nxt):
                if b is not None:
                    if first(b):
                        dve.wait_ge(cross_loaded, 16 * 7)
                    dve.wait_ge(k_ps, b + 1)
                    for c in range(DC):
                        last = dve.tensor_scalar(kT[:, c, :], bank(7)[:, c, :], bk_sb[:, c:c + 1], None, ALU.add)
                    last.then_inc(kT_ready, 1)
                    dve.wait_ge(q_ps, b + 1)
                    for c in range(DC):
                        last = dve.tensor_scalar(qT[:, c, :], bank(6)[:, c, :], bq_sb[:, c:c + 1], SCORE_SCALE,
                                                 ALU.add, ALU.mult)
                    last.then_inc(qT_ready, 1)
                    dve.wait_ge(score_ps, b + 1)
                    dve.tensor_reduce(snmax[:, :], bank(7), AX_X, ALU.max, negate=True).then_inc(snmax_ready, 1)
                if f is not None:
                    if first(f):
                        dve.wait_ge(ffn_loaded, 16 * 4)
                    for g in (1, 3):
                        dve.wait_ge(w1_ps, f * 4 + (g + 1))
                        for n in range(2):
                            last = dve.tensor_scalar(fT[:, 2 * g + n, :], bank(g)[:, n, :],
                                                     b1_sb[:, 2 * g + n:2 * g + n + 1], 0.0, ALU.add, ALU.max)
                        last.then_inc(relu_dve_ready, 1)

                def row_max(g):
                    dve.wait_ge(proj_ps, a * 4 + (g + 1))
                    dve.tensor_reduce(nmax[:, g, :], ps[:, g, :].rearrange("p (h m) -> p h m", h=H), AX_X, ALU.max,
                                      negate=True).then_inc(nmax_ready, 1)

                if a is not None:
                    for g in range(4):
                        row_max(g)
                if b is not None:
                    dve.wait_ge(prT_ps, b + 1)
                    dve.tensor_copy(prT, bank(7)).then_inc(prT_ready, 1)
                    dve.wait_ge(pr_ready, b + 1)
                    dve.reciprocal(rsum[:, :], ssum[:, :]).then_inc(rsum_ready, 1)
                if nxt is not None:
                    hold(dve, x_loaded, (nxt + 1) * 16)
                    ln_stats(0, nxt, lambda t: x_tile(nxt, t))
                if a is not None:
                    for n in range(2):
                        dve.wait_ge(kpT_ps, a * 2 + (n + 1))
                        last = dve.tensor_scalar(kpT[:, 2 * n:2 * n + 2, :], bank(2 + n), PHI_SCALE, FEAT_EPS,
                                                 ALU.mult, ALU.add)
                    last.then_inc(kpT_ready, 1)
                if nxt is not None:
                    dve.wait_ge(xn_kept, nxt)
                    ln_apply(0, nxt, lambda t: x_tile(nxt, t), xn_next, xn_ready)
                if a is not None:
                    for h in range(H):
                        dve.wait_ge(aT_ps, a * 4 + (h + 1))
                        dve.tensor_tensor(aT[:, h, :], ps[:, h, 0:ATW], mask[:, :], ALU.mult).then_inc(aT_ready, 1)
                if b is not None:
                    dve.wait_ge(av_ps, b + 1)
                    dve.wait_ge(xbv_ready, b + 1)
                    dve.wait_ge(rsum_ready, b + 1)
                    for t in range(TS):
                        last = dve.scalar_tensor_tensor(x_tile(b, t), bank(6)[:, t, :], rsum[:, t:t + 1], x_tile(b, t),
                                                        ALU.mult, ALU.add)
                    last.then_inc(x2_ready, 1)
                    hold(dve, x2_ready, b + 1)
                    ln_stats(3, b, lambda t: x_tile(b, t))
                if a is not None:
                    num = ps[:, 0:TS, 0:H * V1W].rearrange("p t (h d) -> p t h d", h=H)
                    dve.wait_ge(num_ps, a + 1)
                    dve.tensor_scalar(den[:, :, :], num[:, :, :, DH], FEAT_EPS, None, ALU.add).then_inc(den_ready, 1)
                    dve.wait_ge(den_ready, a + 1)
                    dve.reciprocal(rden[:, :, :], den[:, :, :]).then_inc(rden_ready, 1)
                    dve.wait_ge(rden_ready, a + 1)
                    dve.tensor_tensor(attn.rearrange("p t (h d) -> p t h d", h=H), num[:, :, :, 0:DH],
                                      rden[:, :, :].unsqueeze(3).broadcast_to([P, TS, H, DH]), ALU.mult)\
                        .then_inc(attn_ready, 1)
                if b is not None:
                    if not first(b):
                        dve.wait_ge(xn3_stored, b * 16)
                    ln_apply(3, b, lambda t: x_tile(b, t), xn3, xn3_ready)
                if f is not None:
                    dve.wait_ge(w2_ps, f + 1)
                    dve.wait_ge(xb2_ready, f + 1)
                    xs = X[:, tiles_of(f), :]
                    dve.tensor_tensor(xs, bank(4), xs, ALU.add).then_inc(x1_ready, 1)
                    hold(dve, x1_ready, f + 1)
                    ln_stats(2, f, lambda t: x_tile(f, t))
                if b is not None:
                    hold(dve, logit_ps, b + 1)
                    dve.tensor_copy(logits[:, tiles_of(b), :],
                                    ps[:, 6, 0:TS * NE].rearrange("p (t e) -> p t e", e=NE)).then_inc(logit_ready, 1)
                if f is not None:
                    ln_apply(2, f, lambda t: x_tile(f, t), xn2, xn2_ready)
                if a is not None:
                    dve.wait_ge(wo_ps, a + 1)
                    dve.wait_ge(xn_kept, a + 1)
                    dve.tensor_tensor(y, bank(3), xn, ALU.add).then_inc(y_ready, 1)
                    hold(dve, y_ready, a + 1)
                    ln_stats(1, a, lambda t: y[:, t, :])
                    ln_apply(1, a, lambda t: y[:, t, :], y, z_ready)

            in_turns(dve, turn)

            steps = [0]

            def then(ins):
                steps[0] += 1
                ins.then_inc(routed, 1)
                dve.wait_ge(routed, steps[0])

            def over_e(row):
                return row.unsqueeze(2).broadcast_to([P, NT, NE])

            def over_t(row):
                return row.unsqueeze(1).broadcast_to([P, NT, NE])

            dve.wait_ge(logit_ready, NSEQ)
            dve.wait_ge(xn3_stored, 16 * NSEQ)
            back = over_t(iota_back[:, :])

            def choose(scores, best, pick, hot):
                then(dve.tensor_reduce(best[:, :], scores, AX_X, ALU.max))
                then(dve.tensor_tensor(tmp_a, scores, over_e(best[:, :]), ALU.is_equal))
                then(dve.tensor_tensor(tmp_b, tmp_a, back, ALU.mult))
                then(dve.tensor_reduce(pick[:, :], tmp_b, AX_X, ALU.max))
                then(dve.tensor_tensor(hot, back, over_e(pick[:, :]), ALU.is_equal))

            choose(logits[:, :, :], best1, pick1, oh1)
            then(dve.scalar_tensor_tensor(masked, oh1, -3e38, logits[:, :, :], ALU.mult, ALU.add))
            choose(masked, best2, pick2, oh2)
            dve.tensor_tensor(gap[:, :], best2[:, :], best1[:, :], ALU.subtract).then_inc(gap_ready, 1)
            dve.tensor_tensor(oh, oh1, oh2, ALU.add).then_inc(oh_ready, 1)
            dve.wait_ge(egap_ready, 1)
            then(dve.tensor_scalar(gden[:, :], egap[:, :], 1.0, None, ALU.add))
            then(dve.reciprocal(gate1[:, :], gden[:, :]))
            then(dve.tensor_tensor(gate2[:, :], gate1[:, :], egap[:, :], ALU.mult))
            dve.wait_ge(rank_ps, 1)
            per_tile = ps[:, 1, :].rearrange("p (t e) -> p t e", e=NE)
            then(dve.tensor_copy(tot, per_tile))
            src, bufs, n = tot, (tmp_a, tmp_b), 1
            while n < NT:
                dst = bufs[0]
                bufs = bufs[::-1]
                dve.tensor_copy(dst[:, 0:n, :], src[:, 0:n, :])
                then(dve.tensor_tensor(dst[:, n:, :], src[:, n:, :], src[:, 0:NT - n, :], ALU.add))
                src, n = dst, 2 * n
            upto, spare = src, bufs[0]
            then(dve.tensor_scalar(need_i[:, :], upto[:, NT - 1, :], float(P - 1), None, ALU.add))
            then(dve.tensor_scalar(need_s[:, :], need_i[:, :], 7, None, ALU.logical_shift_right))
            then(dve.tensor_copy(need[:, :], need_s[:, :]))
            csrc, cbufs, n = need, (cum_a, cum_b), 1
            while n < NE:
                dst = cbufs[0]
                cbufs = cbufs[::-1]
                dve.tensor_copy(dst[:, 0:n], csrc[:, 0:n])
                then(dve.tensor_tensor(dst[:, n:], csrc[:, n:], csrc[:, 0:NE - n], ALU.add))
                csrc, n = dst, 2 * n
            cum = csrc
            then(dve.tensor_tensor(base[:, :], cum[:, :], need[:, :], ALU.subtract))
            then(dve.tensor_tensor(spare, upto, tot, ALU.subtract))
            then(dve.scalar_tensor_tensor(masked, over_t(base[:, :]), float(P), spare, ALU.mult, ALU.add))
            then(dve.tensor_tensor(spare, masked, ps[:, 0, :].rearrange("p (t e) -> p t e", e=NE), ALU.add))
            for j, hot in enumerate((oh1, oh2)):
                then(dve.tensor_tensor(masked, hot, spare, ALU.mult))
                then(dve.tensor_reduce(slot[:, :, j], masked, AX_X, ALU.add))
            then(dve.tensor_copy(slot_i[:, :, :], slot[:, :, :]))
            then(dve.tensor_scalar(slot_hi_i[:, :, :], slot_i[:, :, :], 7, None, ALU.logical_shift_right))
            then(dve.tensor_scalar(slot_lo_i[:, :, :], slot_i[:, :, :], P - 1, None, ALU.bitwise_and))
            then(dve.tensor_copy(slot_hi[:, :, :], slot_hi_i[:, :, :]))
            then(dve.tensor_copy(slot_lo[:, :, :], slot_lo_i[:, :, :]))
            then(dve.tensor_tensor(early[0:1], cum[0:1, :].unsqueeze(1).broadcast_to([1, SLOT_TILES, NE]),
                                   iota_tile[0:1, :].unsqueeze(2).broadcast_to([1, SLOT_TILES, NE]), ALU.is_le))
            then(dve.tensor_reduce(expert_f[0:1, :], early[0:1], AX_X, ALU.add))
            then(dve.tensor_scalar(expert_i[:, :], expert_f[0:1, :], float(NE - 1), None, ALU.min))
            def hots(g, again):
                for k in range(HB):
                    t, j = g * (HB // TOPK) + k // TOPK, k % TOPK
                    if again:
                        dve.wait_ge(table_ps, g * HB + (k + 1 - HB))
                    dve.tensor_scalar(hot_slot[:, k, :], iota_slot[:, :], slot_lo[:, bass.ds(t, 1), j], None,
                                      ALU.is_equal)
                    dve.tensor_scalar(hot_tile[:, k, :], iota_tile[:, :], slot_hi[:, bass.ds(t, 1), j],
                                      assign_no[:, bass.ds(t, 1), j], ALU.is_equal, ALU.mult).then_inc(hot_ready, 1)

            hots(0, False)
            with dve.Fori(1, NT * TOPK // HB) as g:
                hots(g, True)
            dve.wait_ge(table_ps, NT * TOPK)
            then(dve.tensor_copy(table[:, :], ps[:, 2, 0:SLOT_TILES]))
            then(dve.tensor_scalar(empty[:, :], table[:, :], 0.0, None, ALU.is_equal))
            then(dve.tensor_tensor(gath_f[:, :], empty[:, :], dump_no[:, :], ALU.mult))
            then(dve.tensor_tensor(scat_f[:, :], table[:, :], gath_f[:, :], ALU.add))
            then(dve.tensor_scalar(scat_i[:, :], scat_f[:, :], -1.0, None, ALU.add))
            then(dve.tensor_scalar(gath_j[:, :], table[:, :], -1.0, 0.0, ALU.add, ALU.max))
            dve.tensor_scalar(gath_i[:, :], gath_j[:, :], 1, None, ALU.logical_shift_right).then_inc(plan_ready, 1)

            dve.wait_ge(plan_ready, 1)

            def rows_in(s, u):
                dve.wait_ge(xgT_ps, s + 1)
                dve.tensor_copy(xgT[:, u % 2], ps[:, u % 2, 0:D].rearrange("p (c s) -> p c s", c=DC))\
                    .then_inc(xgT_ready, 1)

            def product(s, u):
                dve.wait_ge(silu_ready, s + 1)
                dve.tensor_tensor(hid[:, u % 2, :], ps[:, 2 + u % 2, INTER:2 * INTER], silu[:, u % 2, :], ALU.mult)\
                    .then_inc(hid_ready, 1)

            def hidden_in(s, u):
                if not (isinstance(s, int) and s < 2):
                    dve.wait_ge(e2_ps, s - 1)
                dve.wait_ge(hidT_ps, s + 1)
                dve.tensor_copy(hidT[:, u % 2, 0, :], ps[:, 4 + u % 2, 0:P])
                dve.tensor_copy(hidT[0:IR, u % 2, 1, :], ps[0:IR, 4 + u % 2, P:2 * P]).then_inc(hidT_ready, 1)

            rows_in(0, 0)
            rows_in(1, 1)
            product(0, 0)

            def slot_tiles(s, u, last):
                if not (last and u + 2 >= GB):
                    rows_in(s + 2, (u + 2) % GB)
                if not (last and u + 1 >= GB):
                    product(s + 1, (u + 1) % GB)
                hidden_in(s, u)

            in_groups(slot_tiles, dve)

            with dve.Fori(0, NSEQ // YB) as g:
                for u in range(YB):
                    n = g * YB + u
                    dve.wait_ge(y_loaded[u], g * 16 + 16)
                    for j, gate, done in ((0, gate1, part_ready), (1, gate2, sum_ready)):
                        for t in range(TS):
                            last = dve.scalar_tensor_tensor(x_tile(n, t), yl[:, u, t, j, :],
                                                            gate[:, bass.ds(n * TS + t, 1)], x_tile(n, t),
                                                            ALU.mult, ALU.add)
                        last.then_inc(done, 1)
                        if j == 0:
                            dve.wait_ge(part_ready, n + 1)




def kernel(**inputs):
    import numpy as np
    import concourse.bacc as bacc
    from concourse.bass_utils import run_bass_kernel_spmd

    def flat(name):
        return np.ascontiguousarray(inputs[name])

    def turned(name, axes=None):
        return np.ascontiguousarray(np.transpose(inputs[name], axes))

    def by_partition(name):
        return np.ascontiguousarray(inputs[name].reshape(-1, P).T)

    arrays = {
        "x": flat("x"),
        "ctxT": turned("ctx_1024", (0, 2, 1)),
        "WqT": turned("L0_attn_Wq"),
        "WkT": turned("L0_attn_Wk"),
        "Wv": flat("L0_attn_Wv"),
        "Wo": flat("L0_attn_Wo"),
        "omegaT": turned("L0_attn_omega"),
        "W1": flat("L0_attn_W1"),
        "b1": by_partition("L0_attn_b1"),
        "W2": flat("L0_attn_W2"),
        "b2": flat("L0_attn_b2"),
        "gamma": by_partition("L0_attn_gamma"),
        "beta": by_partition("L0_attn_beta"),
        "xWqT": turned("L0_xattn_Wq"),
        "xbq": by_partition("L0_xattn_bq"),
        "xWkT": turned("L0_xattn_Wk"),
        "xbk": by_partition("L0_xattn_bk"),
        "xWvT": turned("L0_xattn_Wv"),
        "xbv": flat("L0_xattn_bv"),
        "WgT": turned("L0_ffn_Wg"),
        "E1": flat("L0_ffn_W1"),
        "E3": flat("L0_ffn_W3"),
        "E2": flat("L0_ffn_W2"),
    }
    nc = bacc.Bacc("TRN2", target_bir_lowering=False, num_devices=1)
    aps = {n: nc.dram_tensor(f"in_{n}", a.shape, mybir.dt.from_np(a.dtype), kind="ExternalInput").ap()
           for n, a in arrays.items()}
    out = nc.dram_tensor("out", inputs["x"].shape, F32, kind="ExternalOutput").ap()
    decoder(nc, **aps, out=out)
    r = run_bass_kernel_spmd(nc, [{f"in_{n}": a for n, a in arrays.items()}], core_ids=[0])
    return r.results[0]["out"]
```

```python
from contextlib import ExitStack

import concourse.bass as bass
from concourse import mybir

F32 = mybir.dt.float32
F32R = mybir.dt.float32r
I32 = mybir.dt.int32
ALU = mybir.AluOpType
ACT = mybir.ActivationFunctionType
AX_X = mybir.AxisListType.X

P = 128
LN_EPS = 1e-5
ATTN_LN_EPS = 1e6
FEAT_EPS = 1e-6


def decoder(nc, x, ctxT, WqT, WkT, Wv, Wo, omegaT, W1, b1, W2, b2, gamma, beta,
            xWqT, xbq, xWkT, xbk, xWvT, xbv, WgT, E1, E3, E2, out):
    NSEQ, S, D = x.shape
    DC = D // P
    TS = S // P
    NT = NSEQ * TS
    DH, M = omegaT.shape
    H = D // DH
    FF = W1.shape[1]
    FC = FF // P
    NE = WgT.shape[1]
    INTER = E1.shape[2]
    IR = INTER - P
    TOPK = 2
    SLOT_TILES = NT * TOPK + NE
    NASSIGN = NT * P * TOPK
    SCORE_SCALE = float(D) ** -0.5
    PHI_SCALE = float(M) ** -0.5
    PROJ_SCALE = float(DH) ** -0.25
    V1W = DH + 1
    ATW = S + P
    assert DC == 2 and TS == 2 and H * P == 512 and M == P and FC == 8

    xn3_dram = nc.dram_tensor("xn3_rows", (NT * P, D), F32, kind="Internal").ap()
    y_dram = nc.dram_tensor("expert_rows", (NASSIGN + SLOT_TILES * P, D), F32, kind="Internal").ap()

    x_v = x.rearrange("b (t p) d -> p (b t) d", p=P)
    out_v = out.rearrange("b (t p) d -> p (b t) d", p=P)
    ctx_v = ctxT.rearrange("b (c p) s -> p b c s", p=P)
    xn3_v = xn3_dram.rearrange("(t p) d -> p t d", p=P)
    y_v = y_dram[0:NASSIGN, :].rearrange("(t p j) d -> p t (j d)", p=P, j=TOPK)

    with ExitStack() as stack:
        def sb(name, shape, dt=F32):
            return stack.enter_context(nc.sbuf_tensor(name, shape, dt))

        def sem(name):
            return stack.enter_context(nc.semaphore(name))

        X = sb("X", [P, NT, D])
        wg_sb = sb("wg_sb", [P, DC, NE])
        b1_sb = sb("b1_sb", [P, FC])
        gam_sb = sb("gam_sb", [P, DC])
        bet_sb = sb("bet_sb", [P, DC])
        bq_sb = sb("bq_sb", [P, DC])
        bk_sb = sb("bk_sb", [P, DC])
        b2_sb = sb("b2_sb", [P, D])
        bv_sb = sb("bv_sb", [P, D])
        ident = sb("ident", [P, P])
        mask = sb("mask", [P, ATW])
        before = sb("before", [P, P])
        ones = sb("ones", [P, P])
        halfneg = sb("halfneg", [P, TS])
        eps_ln = sb("eps_ln", [P, TS])
        eps_attn = sb("eps_attn", [P, TS])
        feat_eps = sb("feat_eps", [P, 1])
        iota_slot = sb("iota_slot", [P, P])
        iota_tile = sb("iota_tile", [P, SLOT_TILES])
        iota_back = sb("iota_back", [P, NE])
        assign_no = sb("assign_no", [P, NT, TOPK])
        dump_no = sb("dump_no", [P, SLOT_TILES])

        logits = sb("logits", [P, NT, NE])
        stat = sb("stat", [P, 4, TS, 6])
        mv = sb("mv", [P, 4, TS, 2])
        veps = sb("veps", [P, 4, TS])
        rstd = sb("rstd", [P, 4, TS])
        nmax = sb("nmax", [P, 4, H])
        den = sb("den", [P, TS, H])
        rden = sb("rden", [P, TS, H])
        snmax = sb("snmax", [P, TS])
        ssum = sb("ssum", [P, TS])
        rsum = sb("rsum", [P, TS])
        best1, best2, pick1, pick2, gap, egap, gden, gate1, gate2 = (sb(n, [P, NT]) for n in (
            "best1", "best2", "pick1", "pick2", "gap", "egap", "gden", "gate1", "gate2"))
        need_i, need_s = sb("need_i", [P, NE], I32), sb("need_s", [P, NE], I32)
        need, cum_a, cum_b, base = (sb(n, [P, NE]) for n in ("need", "cum_a", "cum_b", "base"))
        slot = sb("slot", [P, NT, TOPK])
        slot_i, slot_hi_i, slot_lo_i = (sb(n, [P, NT, TOPK], I32) for n in ("slot_i", "slot_hi_i", "slot_lo_i"))
        slot_hi, slot_lo = sb("slot_hi", [P, NT, TOPK]), sb("slot_lo", [P, NT, TOPK])
        table, empty, scat_f, gath_f = (sb(n, [P, SLOT_TILES]) for n in ("table", "empty", "scat_f", "gath_f"))
        scat_i, gath_i, gath_j = (sb(n, [P, SLOT_TILES], I32) for n in ("scat_i", "gath_i", "gath_j"))
        expert_f = sb("expert_f", [P, SLOT_TILES])
        expert_i = sb("expert_i", [1, SLOT_TILES], I32)

        early_scope = ExitStack()

        def sb1(name, shape, dt=F32, scope=early_scope):
            return scope.enter_context(nc.sbuf_tensor(name, shape, dt))

        def pair(name, n):
            return tuple(sb1(f"{name}_{part}", [P, n], F32R)[:, :] for part in ("hi", "lo"))

        def cut(tiles, pattern, **sizes):
            return tuple(t.rearrange(pattern, **sizes) for t in tiles)

        wq, wk = (cut(pair(n, DC * H * M), "p (c n) -> p c n", c=DC) for n in ("wq", "wk"))
        wv, wo = (cut(pair(n, DC * D), "p (c n) -> p c n", c=DC) for n in ("wv", "wo"))
        w1 = cut(pair("w1", DC * FF), "p (c n) -> p c n", c=DC)
        w2 = cut(pair("w2", FC * D), "p (c n) -> p c n", c=FC)
        phi = sb1("phi", [P, 4, H, M])
        qpT = sb1("qpT", [P, H, S])
        kpT = sb1("kpT", [P, H, S])
        freed_cols = 2 * (2 * DC * H * M + 2 * DC * D + DC * FF + FC * D) + 4 * H * M + 2 * H * S
        with ExitStack() as raw_scope:
            raw_wT = sb1("raw_wT", [DH, 2 * H * D + M], F32, raw_scope)
            raw_v, raw_o = (sb1(f"raw_{n}", [P, DC, D], F32, raw_scope) for n in "vo")
            raw_w1 = sb1("raw_w1", [P, DC, FF], F32, raw_scope)
            raw_w2 = sb1("raw_w2", [P, FC, D], F32, raw_scope)
            raw_xq, raw_xk, raw_xv = (sb1(f"raw_x{n}", [P, DC, D], F32, raw_scope) for n in "qkv")
        fT = cut(pair("fT", FC * S), "p (f s) -> p f s", f=FC)
        freed_cols += 2 * FC * S
        xn2T, kT, qT, v2, prT, ctx = (cut(pair(n, DC * S), "p (c s) -> p c s", c=DC) for n in (
            "xn2T", "kT", "qT", "v2", "prT", "ctx"))
        xwq, xwk, xwv = (cut(pair(n, DC * D), "p (c n) -> p c n", c=DC) for n in ("xwq", "xwk", "xwv"))
        xnT, hT, attnT = (cut(pair(n, DC * S), "p (c s) -> p c s", c=DC) for n in ("xnT", "hT", "attnT"))
        xn_next, xn, attn, y, xn2, pr, xn3, xn3T, ctx_raw = (sb1(n, [P, TS, D])[:, :, :] for n in (
            "xn_next", "xn", "attn", "y", "xn2", "pr", "xn3", "xn3T", "ctx_raw"))
        relu = sb1("relu", [P, 2, 2, S])
        v1 = sb1("v1", [P, TS, H, V1W])
        aT = phi[:, :, :, :].rearrange("p g h m -> p (g h m)")[:, 0:H * ATW].rearrange("p (h s) -> p h s", h=H)
        early_scope.close()

        e13_sb = sb("e13_sb", [P, DC, NE, 2 * INTER])
        e2a_sb = sb("e2a_sb", [P, NE, D])[:, :, :]
        e2b_sb = sb("e2b_sb", [P, NE, D])[:, :, :]
        fill = freed_cols - DC * NE * 2 * INTER - 2 * NE * D
        assert fill > 0
        sb("fill", [P, fill])
        narrow = sb("narrow", [P, 17 * 512])
        place = [0]

        def carve(n):
            place[0] += n
            return narrow[:, place[0] - n:place[0]]

        oh1, oh2, oh, masked, tmp_a, tmp_b, tot = (carve(NT * NE).rearrange("p (t e) -> p t e", e=NE) for _ in range(7))
        HB = 4
        hot_slot = carve(HB * P).rearrange("p (u s) -> p u s", u=HB)
        hot_tile = carve(HB * SLOT_TILES).rearrange("p (u s) -> p u s", u=HB)
        early = carve(SLOT_TILES * NE).rearrange("p (s e) -> p s e", e=NE)
        place[0] = 0
        GB = 8
        PER = 16 // GB
        LAG = 2
        xg = carve(GB * D).rearrange("p (u d) -> p u d", u=GB)
        yg = carve(GB * D).rearrange("p (u d) -> p u d", u=GB)
        xgT = carve(2 * D).rearrange("p (u c s) -> p u c s", u=2, c=DC)
        silu = carve(2 * INTER).rearrange("p (u i) -> p u i", u=2)
        hid = carve(2 * INTER).rearrange("p (u i) -> p u i", u=2)
        hidT = carve(2 * 2 * P).rearrange("p (u c s) -> p u c s", u=2, c=2)
        gidx = sb("gidx", [P, GB], I32)
        sidx = sb("sidx", [P, GB], I32)
        place[0] = 0
        YB = 4
        yl = carve(YB * TS * TOPK * D).rearrange("p (u t j d) -> p u t j d", u=YB, t=TS, j=TOPK)

        ps = stack.enter_context(nc.psum_tensor("ps", [P, 8, 512], F32))

        fuse_loaded, attn_loaded, ffn_loaded, cross_loaded = (sem(n) for n in (
            "fuse_loaded", "attn_loaded", "ffn_loaded", "cross_loaded"))
        em_loaded, e2_loaded = sem("em_loaded"), sem("e2_loaded")
        x_loaded, ctx_loaded, xn3_stored = sem("x_loaded"), sem("ctx_loaded"), sem("xn3_stored")
        blank, const_ready = sem("blank"), sem("const_ready")
        fused_ps = sem("fused_ps")
        split_hi, split_lo, b1_ps, b1_ready = sem("split_hi"), sem("split_lo"), sem("b1_ps"), sem("b1_ready")
        xnT_hi, attnT_hi, hT_hi, xn2T_hi, kT_hi, qT_hi, v2_hi, prT_hi, ctx_hi = (sem(f"{n}_hi_ready") for n in (
            "xnT", "attnT", "hT", "xn2T", "kT", "qT", "v2", "prT", "ctx"))
        ctx_ready = sem("ctx_ready")
        stat_ready = [sem(f"stat{n}_ready") for n in range(4)]
        mv_ready = [sem(f"mv{n}_ready") for n in range(4)]
        veps_ready = [sem(f"veps{n}_ready") for n in range(4)]
        rstd_ready = [sem(f"rstd{n}_ready") for n in range(4)]
        xn_kept = sem("xn_kept")
        xn_ready, z_ready, xn2_ready, xn3_ready = sem("xn_ready"), sem("z_ready"), sem("xn2_ready"), sem("xn3_ready")
        xnT_ps, xnT_ready = sem("xnT_ps"), sem("xnT_ready")
        proj_ps, nmax_ready, phi_ready = sem("proj_ps"), sem("nmax_ready"), sem("phi_ready")
        v_ps, v1_ready = sem("v_ps"), sem("v1_ready")
        qpT_ps, qpT_ready, kpT_ps, kpT_ready = sem("qpT_ps"), sem("qpT_ready"), sem("kpT_ps"), sem("kpT_ready")
        aT_ps, aT_ready = sem("aT_ps"), sem("aT_ready")
        num_ps, den_ready, rden_ready, attn_ready = sem("num_ps"), sem("den_ready"), sem("rden_ready"), sem("attn_ready")
        attnT_ps, attnT_ready = sem("attnT_ps"), sem("attnT_ready")
        wo_ps, y_ready = sem("wo_ps"), sem("y_ready")
        zT_ps, hT_ready = sem("zT_ps"), sem("hT_ready")
        w1_ps, relu_ready, fT_ready = sem("w1_ps"), sem("relu_ready"), sem("fT_ready")
        w2_ps, xb2_ready, x1_ready = sem("w2_ps"), sem("xb2_ready"), sem("x1_ready")
        xn2T_ps, xn2T_ready = sem("xn2T_ps"), sem("xn2T_ready")
        k_ps, kT_ready, q_ps, qT_ready = sem("k_ps"), sem("kT_ready"), sem("q_ps"), sem("qT_ready")
        score_ps, snmax_ready, pr_ready, rsum_ready = sem("score_ps"), sem("snmax_ready"), sem("pr_ready"), sem("rsum_ready")
        v2_ps, v2_ready, prT_ps, prT_ready = sem("v2_ps"), sem("v2_ready"), sem("prT_ps"), sem("prT_ready")
        av_ps, xbv_ready, x2_ready = sem("av_ps"), sem("xbv_ready"), sem("x2_ready")
        xn3T_ps, xn3T_ready = sem("xn3T_ps"), sem("xn3T_ready")
        logit_ps, logit_ready = sem("logit_ps"), sem("logit_ready")
        routed = sem("routed")
        gap_ready, egap_ready, oh_ready, rank_ps, hot_ready, table_ps, plan_ready = (sem(n) for n in (
            "gap_ready", "egap_ready", "oh_ready", "rank_ps", "hot_ready", "table_ps", "plan_ready"))
        gidx_ready, sidx_ready = sem("gidx_ready"), sem("sidx_ready")
        gathered = [sem(f"gathered{u}") for u in range(GB)]
        scattered = [sem(f"scattered{u}") for u in range(GB)]
        xgT_ps, xgT_ready, e13_ps, silu_ready, hid_ready, hidT_ps, hidT_ready, e2_ps, yg_ready = (sem(n) for n in (
            "xgT_ps", "xgT_ready", "e13_ps", "silu_ready", "hid_ready", "hidT_ps", "hidT_ready", "e2_ps", "yg_ready"))
        y_loaded = [sem(f"y_loaded{u}") for u in range(YB)]
        part_ready, sum_ready, out_stored = sem("part_ready"), sem("sum_ready"), sem("out_stored")
        held = sem("held")

        N_CONST = 14
        N_SPLIT = 14

        def hold(eng, s, value):
            eng.wait_ge(s, value)
            eng.sem_inc(held)

        def in_turns(eng, turn):
            for i in range(3):
                turn(i, i, i - 1 if i >= 1 else None, i - 2 if i >= 2 else None, i + 1)
            with eng.Fori(3, NSEQ - 1) as i:
                turn(i, i, i - 1, i - 2, i + 1)
            turn(NSEQ - 1, NSEQ - 1, NSEQ - 2, NSEQ - 3, None)
            turn(NSEQ, None, NSEQ - 1, NSEQ - 2, None)
            turn(NSEQ + 1, None, None, NSEQ - 1, None)

        def in_groups(step, eng):
            for u in range(GB):
                step(u, u, False)
            with eng.Fori(1, SLOT_TILES // GB - 1) as g:
                for u in range(GB):
                    step(g * GB + u, u, False)
            for u in range(GB):
                step(SLOT_TILES - GB + u, u, True)

        def first(n):
            return isinstance(n, int) and n == 0

        def tiles_of(seq):
            return bass.ds(seq * TS, TS)

        block = stack.enter_context(nc.Block())

        @block.sync
        def _(sp):
            def load(dst, src, s):
                sp.dma_start(dst, src).then_inc(s, 16)

            def load_x(n):
                if not first(n):
                    sp.wait_ge(x_loaded, n * 16)
                sp.dma_start(X[:, tiles_of(n), :], x_v[:, tiles_of(n), :]).then_inc(x_loaded, 16)

            load_x(0)
            load(raw_wT[:, 0:H * D].rearrange("p (h d) -> p h d", h=H), WqT.rearrange("(h e) d -> e h d", h=H), fuse_loaded)
            load(raw_wT[:, H * D:2 * H * D].rearrange("p (h d) -> p h d", h=H), WkT.rearrange("(h e) d -> e h d", h=H),
                 fuse_loaded)
            load(raw_wT[:, 2 * H * D:], omegaT, fuse_loaded)
            load(raw_v[:, :, :], Wv.rearrange("(c p) n -> p c n", p=P), attn_loaded)
            load(raw_o[:, :, :], Wo.rearrange("(c p) n -> p c n", p=P), attn_loaded)
            load(raw_w1[:, :, :], W1.rearrange("(c p) n -> p c n", p=P), ffn_loaded)
            load(b1_sb[:, :], b1, ffn_loaded)
            load(gam_sb[:, :], gamma, ffn_loaded)
            load(bet_sb[:, :], beta, ffn_loaded)
            load(raw_w2[:, :, :], W2.rearrange("(c p) n -> p c n", p=P), ffn_loaded)
            load(b2_sb[:, :], b2.partition_broadcast(P), ffn_loaded)
            load(raw_xq[:, :, :], xWqT.rearrange("(c p) n -> p c n", p=P), cross_loaded)
            load(raw_xk[:, :, :], xWkT.rearrange("(c p) n -> p c n", p=P), cross_loaded)
            load(raw_xv[:, :, :], xWvT.rearrange("(c p) n -> p c n", p=P), cross_loaded)
            load(bq_sb[:, :], xbq, cross_loaded)
            load(bk_sb[:, :], xbk, cross_loaded)
            load(bv_sb[:, :], xbv.partition_broadcast(P), cross_loaded)
            load(wg_sb[:, :, :], WgT.rearrange("(c p) n -> p c n", p=P), cross_loaded)
            load(ctx_raw, ctx_v[:, 0, :, :], ctx_loaded)

            def load_experts():
                sp.wait_ge(w2_ps, NSEQ)
                for c in range(DC):
                    for n, w in enumerate((E1, E3)):
                        load(e13_sb[:, c, :, n * INTER:(n + 1) * INTER],
                             w[:, c * P:(c + 1) * P, :].rearrange("e p i -> p e i"), em_loaded)
                load(e2a_sb, E2[:, 0:P, :].rearrange("e p d -> p e d"), e2_loaded)
                load(e2b_sb[0:IR], E2[:, P:INTER, :].rearrange("e p d -> p e d"), e2_loaded)

            def turn(i, a, f, b, nxt):
                if nxt is not None:
                    load_x(nxt)
                if b is not None:
                    if not (isinstance(b, int) and b == NSEQ - 1):
                        sp.wait_ge(ctx_ready, b + 1)
                        sp.dma_start(ctx_raw, ctx_v[:, bass.ds(b + 1, 1), :, :]
                                     .rearrange("p b c s -> p (b c) s")).then_inc(ctx_loaded, 16)
                    sp.wait_ge(xn3_ready, b + 1)
                    sp.dma_start(xn3_v[:, tiles_of(b), :], xn3).then_inc(xn3_stored, 16)
                if isinstance(i, int) and i == NSEQ:
                    load_experts()

            in_turns(sp, turn)
            for u in range(GB):
                sp.wait_ge(scattered[u], 16 * (SLOT_TILES // GB))
            sp.wait_ge(yg_ready, SLOT_TILES)

            def fetch(n, u):
                if not (isinstance(n, int) and n < YB):
                    sp.wait_ge(sum_ready, n - YB + 1)
                sp.dma_start(yl[:, u].rearrange("p t j d -> p t (j d)"), y_v[:, tiles_of(n), :])\
                    .then_inc(y_loaded[u], 16)

            for u in range(YB):
                fetch(u, u)
            with sp.Fori(1, NSEQ // YB) as g:
                for u in range(YB):
                    fetch(g * YB + u, u)

        @block.gpsimd
        def _(pool):
            pool.memset(ones[:, :], 1.0).then_inc(blank, 1)
            pool.memset(halfneg[:, :], -0.5).then_inc(const_ready, 1)
            pool.memset(eps_ln[:, :], LN_EPS).then_inc(const_ready, 1)
            pool.memset(eps_attn[:, :], ATTN_LN_EPS).then_inc(const_ready, 1)
            pool.memset(feat_eps[:, :], FEAT_EPS).then_inc(const_ready, 1)
            pool.memset(v1[:, :, :, DH:V1W], 1.0).then_inc(const_ready, 1)
            pool.memset(mask[:, :], 1.0).then_inc(blank, 1)
            pool.wait_ge(blank, 2)
            pool.affine_select(out=ident[:, :], in_=ones[:, :], compare_op=ALU.is_equal, fill=0.0, base=0,
                               pattern=[[-1, P]], channel_multiplier=1).then_inc(const_ready, 1)
            pool.affine_select(out=before[:, :], in_=ones[:, :], compare_op=ALU.is_gt, fill=0.0, base=0,
                               pattern=[[1, P]], channel_multiplier=-1).then_inc(const_ready, 1)
            for lo in (0, S):
                pool.affine_select(out=mask[:, lo:lo + P], in_=mask[:, lo:lo + P], compare_op=ALU.is_ge, fill=0.0,
                                   base=0, pattern=[[1, P]], channel_multiplier=-1).then_inc(const_ready, 1)
            fl = {"allow_small_or_imprecise_dtypes": True}
            pool.iota(iota_slot[:, :], pattern=[[1, P]], base=0, channel_multiplier=0, **fl).then_inc(const_ready, 1)
            pool.iota(iota_tile[:, :], pattern=[[1, SLOT_TILES]], base=0, channel_multiplier=0, **fl)\
                .then_inc(const_ready, 1)
            pool.iota(iota_back[:, :], pattern=[[-1, NE]], base=NE, channel_multiplier=0, **fl)\
                .then_inc(const_ready, 1)
            pool.iota(assign_no[:, :, :], pattern=[[P * TOPK, NT], [1, TOPK]], base=1, channel_multiplier=TOPK, **fl)\
                .then_inc(const_ready, 1)
            pool.iota(dump_no[:, :], pattern=[[P, SLOT_TILES]], base=NASSIGN + 1, channel_multiplier=1, **fl)\
                .then_inc(const_ready, 1)
            pool.wait_ge(const_ready, N_CONST)
            pool.wait_ge(ffn_loaded, 16 * 6)
            pool.wait_ge(cross_loaded, 16 * 7)

            def root(n, seq, eps):
                pool.wait_ge(mv_ready[n], seq + 1)
                pool.tensor_tensor(veps[:, n, :], mv[:, n, :, 1], eps[:, :], ALU.add).then_inc(veps_ready[n], 1)
                pool.wait_ge(veps_ready[n], seq + 1)
                pool.tensor_tensor(rstd[:, n, :], veps[:, n, :], halfneg[:, :], ALU.pow).then_inc(rstd_ready[n], 1)

            def add_bias(seq, row, after, done):
                hold(pool, after, seq + 1)
                xs = X[:, tiles_of(seq), :]
                pool.tensor_tensor(xs, xs, row[:, :].unsqueeze(1).broadcast_to([P, TS, D]), ALU.add).then_inc(done, 1)

            def split_ctx(seq):
                hold(pool, ctx_loaded, (seq + 1) * 16)
                pool.tensor_copy(ctx[0], ctx_raw).then_inc(ctx_hi, 1)
                hold(pool, ctx_hi, seq + 1)
                pool.tensor_tensor(ctx[1], ctx_raw, ctx[0].bitcast(F32), ALU.subtract).then_inc(ctx_ready, 1)

            def turn(i, a, f, b, nxt):
                if a is not None:
                    hold(pool, xn_ready, a + 1)
                    if not first(a):
                        hold(pool, y_ready, a)
                    pool.tensor_copy(xn, xn_next).then_inc(xn_kept, 1)
                    add_bias(a, b2_sb, xn_ready, xb2_ready)
                if isinstance(i, int) and i == 1:
                    pool.wait_ge(split_lo, N_SPLIT)
                    split_ctx(0)
                if b is not None:
                    add_bias(b, bv_sb, xn2_ready, xbv_ready)
                    if not (isinstance(b, int) and b == NSEQ - 1):
                        hold(pool, v2_ps, b + 1)
                        split_ctx(b + 1)
                if nxt is not None:
                    root(0, nxt, eps_ln)
                if b is not None:
                    root(3, b, eps_ln)
                if f is not None:
                    root(2, f, eps_ln)
                if a is not None:
                    root(1, a, eps_attn)

            root(0, 0, eps_ln)
            in_turns(pool, turn)

            pool.wait_ge(plan_ready, 1)
            pool.wait_ge(xn3_stored, 16 * NSEQ)

            def gather(s, u):
                if not (isinstance(s, int) and s < GB):
                    hold(pool, xgT_ps, s - GB + 1)
                pool.tensor_copy(gidx[:, u:u + 1], gath_i[:, bass.ds(s, 1)]).then_inc(gidx_ready, 1)
                hold(pool, gidx_ready, s + 1)
                pool.indirect_dma_start(xg[:, u, :], None, xn3_dram, bass.IndirectOffsetOnAxis(gidx[:, u:u + 1], 0))\
                    .then_inc(gathered[u], 16)

            def scatter(s, u):
                if not (isinstance(s, int) and s < GB):
                    hold(pool, scattered[u], (s - u) * PER)
                pool.tensor_copy(sidx[:, u:u + 1], scat_i[:, bass.ds(s, 1)]).then_inc(sidx_ready, 1)
                hold(pool, sidx_ready, s + 1)
                hold(pool, yg_ready, s + 1)
                pool.indirect_dma_start(y_dram, bass.IndirectOffsetOnAxis(sidx[:, u:u + 1], 0), yg[:, u, :], None)\
                    .then_inc(scattered[u], 16)

            for s in range(GB):
                gather(s, s)

            def slot_tiles(s, u, last):
                if not last:
                    gather(s + GB, u)
                if not (isinstance(s, int) and s < LAG):
                    scatter(s - LAG, (u - LAG) % GB)

            in_groups(slot_tiles, pool)
            for u in range(GB - LAG, GB):
                scatter(SLOT_TILES - GB + u, u)
            for u in range(GB):
                pool.wait_ge(scattered[u], 16 * (SLOT_TILES // GB))

        @block.tensor
        def _(pe):
            def mm(out_, lhsT, rhs, start=True, stop=True):
                return pe.matmul(out_, lhsT, rhs, start=start, stop=stop)

            def turn_tiles(bank, src):
                for c in range(DC):
                    for t in range(TS):
                        lo = c * S + t * P
                        last = pe.transpose(ps[:, bank, lo:lo + P], src[:, t, c * P:(c + 1) * P], ident[:, :])
                return last

            def mm3(out_, lhsT, rhs, at_l, at_r, start, stop):
                mm(out_, lhsT[0][at_l], rhs[0][at_r], start, False)
                mm(out_, lhsT[0][at_l], rhs[1][at_r], False, False)
                return mm(out_, lhsT[1][at_l], rhs[0][at_r], False, stop)

            def cols(c, lo, n):
                return (slice(None), c, slice(lo, lo + n))

            def by_token(bank, srcT, w):
                for t in range(TS):
                    for c in range(DC):
                        last = mm3(ps[:, bank, t * D:(t + 1) * D], srcT, w, cols(c, t * P, P), cols(c, 0, D),
                                   c == 0, c == DC - 1)
                return last

            def by_feature(bank, srcT, w):
                for e in range(DC):
                    for c in range(DC):
                        last = mm3(ps[:, bank, e * S:(e + 1) * S], w, srcT, cols(c, e * P, P), cols(c, 0, S),
                                   c == 0, c == DC - 1)
                return last

            pe.wait_ge(fuse_loaded, 16 * 3)
            pe.wait_ge(const_ready, N_CONST)
            for n in range(2):
                for c in range(DC):
                    for h in range(H):
                        lo = n * H * D + h * D + c * P
                        last = mm(ps[:, 2 * n + c, h * M:(h + 1) * M], raw_wT[:, lo:lo + P], raw_wT[:, 2 * H * D:])
                    last.then_inc(fused_ps, 1)

            def turn_next(a):
                pe.wait_ge(xn_ready, a + 1)
                turn_tiles(5, xn_next).then_inc(xnT_ps, 1)

            def turn(i, a, f, b, nxt):
                if first(i):
                    turn_next(0)
                    pe.wait_ge(split_lo, 6)

                def project(g, w):
                    t = g % TS
                    for c in range(DC):
                        last = mm3(ps[:, g, :], xnT, w, cols(c, t * P, P), cols(c, 0, H * M), c == 0, c == DC - 1)
                    last.then_inc(proj_ps, 1)

                def ffn_in(g, bank):
                    for n in range(2):
                        for c in range(DC):
                            last = mm3(ps[:, bank, n * S:(n + 1) * S], w1, hT, cols(c, (2 * g + n) * P, P),
                                       cols(c, 0, S), c == 0, c == DC - 1)
                    last.then_inc(w1_ps, 1)

                if a is not None:
                    pe.wait_ge(xnT_ready, a + 1)
                    by_token(5, xnT, wv).then_inc(v_ps, 1)
                    project(0, wq)
                if b is not None:
                    pe.wait_ge(ctx_ready, b + 1)
                    by_feature(7, ctx, xwk).then_inc(k_ps, 1)
                    if not first(b):
                        pe.wait_ge(logit_ready, b)
                    pe.wait_ge(xn2_ready, b + 1)
                    turn_tiles(6, xn2).then_inc(xn2T_ps, 1)
                if a is not None:
                    project(1, wq)
                if f is not None:
                    pe.wait_ge(z_ready, f + 1)
                    turn_tiles(4, y).then_inc(zT_ps, 1)
                if b is not None:
                    pe.wait_ge(xn2T_ready, b + 1)
                    by_feature(6, xn2T, xwq).then_inc(q_ps, 1)
                if f is not None:
                    pe.wait_ge(hT_ready, f + 1)
                    ffn_in(0, 2)
                if b is not None:
                    pe.wait_ge(kT_ready, b + 1)
                    pe.wait_ge(qT_ready, b + 1)
                    for t in range(TS):
                        for c in range(DC):
                            last = mm3(ps[:, 7, t * S:(t + 1) * S], qT, kT, cols(c, t * P, P), cols(c, 0, S),
                                       c == 0, c == DC - 1)
                    last.then_inc(score_ps, 1)
                if f is not None:
                    ffn_in(1, 3)
                if b is not None:
                    by_token(6, ctx, xwv).then_inc(v2_ps, 1)
                if f is not None:
                    if a is not None:
                        pe.wait_ge(phi_ready, a * 4 + 2)
                    ffn_in(2, 0)
                    ffn_in(3, 1)
                if a is not None:
                    if f is not None:
                        pe.wait_ge(relu_ready, f * 4 + 2)
                    project(2, wk)
                    project(3, wk)
                if b is not None:
                    pe.wait_ge(pr_ready, b + 1)
                    turn_tiles(7, pr).then_inc(prT_ps, 1)

                def ffn_out(t, lo, hi):
                    for ff in range(lo, hi):
                        last = mm3(ps[:, 4, t * D:(t + 1) * D], fT, w2, cols(ff, t * P, P), cols(ff, 0, D),
                                   ff == 0, ff == FC - 1)
                    return last

                if f is not None:
                    pe.wait_ge(fT_ready, f * 4 + 4)
                    ffn_out(0, 0, FC)

                def turn_phi(g0, done):
                    pe.wait_ge(phi_ready, a * 4 + (g0 + 2))
                    for h in range(H):
                        for t in range(TS):
                            last = pe.transpose(ps[:, g0 + h // 2, h % 2 * S + t * P:h % 2 * S + (t + 1) * P],
                                                phi[:, g0 + t, h, :], ident[:, :])
                        if h % 2:
                            last.then_inc(done, 1)

                if a is not None:
                    turn_phi(0, qpT_ps)
                    turn_phi(2, kpT_ps)
                if b is not None:
                    pe.wait_ge(prT_ready, b + 1)
                    pe.wait_ge(v2_ready, b + 1)
                    by_token(6, prT, v2).then_inc(av_ps, 1)
                if a is not None:
                    pe.wait_ge(qpT_ready, a + 1)
                    pe.wait_ge(kpT_ready, a + 1)
                    for h in range(H):
                        mm(ps[:, h, 0:S], kpT[:, h, 0:P], qpT[:, h, :])
                        mm(ps[:, h, S:ATW], kpT[:, h, P:S], qpT[:, h, P:S]).then_inc(aT_ps, 1)
                if f is not None:
                    ffn_out(1, 0, FC // 2)
                if a is not None:
                    pe.wait_ge(v1_ready, a + 1)
                    for h in range(H):
                        pe.wait_ge(aT_ready, a * 4 + (h + 1 if h > 1 else 2))
                        col = slice(h * V1W, (h + 1) * V1W)
                        mm(ps[:, 0, col], aT[:, h, 0:P], v1[:, 0, h, :])
                        mm(ps[:, 1, col], aT[:, h, P:S], v1[:, 0, h, :], True, False)
                        last = mm(ps[:, 1, col], aT[:, h, S:ATW], v1[:, 1, h, :], False, True)
                    last.then_inc(num_ps, 1)
                if f is not None:
                    ffn_out(1, FC // 2, FC).then_inc(w2_ps, 1)
                if b is not None:
                    pe.wait_ge(xn3_ready, b + 1)
                    turn_tiles(7, xn3).then_inc(xn3T_ps, 1)
                if a is not None:
                    pe.wait_ge(attn_ready, a + 1)
                    turn_tiles(2, attn).then_inc(attnT_ps, 1)
                if nxt is not None:
                    turn_next(nxt)
                if b is not None:
                    pe.wait_ge(xn3T_ready, b + 1)
                    for t in range(TS):
                        for c in range(DC):
                            last = mm(ps[:, 6, t * NE:(t + 1) * NE], xn3T[:, c, t * P:(t + 1) * P], wg_sb[:, c, :],
                                      c == 0, c == DC - 1)
                    last.then_inc(logit_ps, 1)
                if a is not None:
                    pe.wait_ge(attnT_ready, a + 1)
                    by_token(3, attnT, wo).then_inc(wo_ps, 1)
                if first(i):
                    pe.wait_ge(ffn_loaded, 16 * 6)
                    for ff in range(FC):
                        for c in range(DC):
                            last = mm(ps[:, 4, ff:ff + 1], raw_w1[:, c, ff * P:(ff + 1) * P], bet_sb[:, c:c + 1],
                                      c == 0, c == DC - 1)
                    last.then_inc(b1_ps, 1)
                    pe.wait_ge(split_lo, N_SPLIT)

            in_turns(pe, turn)

            pe.wait_ge(oh_ready, 1)
            oh_all = oh.rearrange("p t e -> p (t e)")
            mm(ps[:, 0, :], before[:, :], oh_all)
            mm(ps[:, 1, :], ones[:, :], oh_all).then_inc(rank_ps, 1)
            def place_assignments(g, begin, end):
                for k in range(HB):
                    pe.wait_ge(hot_ready, g * HB + (k + 1))
                    pe.matmul(ps[:, 2, 0:SLOT_TILES], hot_slot[:, k, :], hot_tile[:, k, :], start=begin and k == 0,
                              stop=end and k == HB - 1).then_inc(table_ps, 1)

            HG = NT * TOPK // HB
            place_assignments(0, True, False)
            with pe.Fori(1, HG - 1) as g:
                place_assignments(g, False, False)
            place_assignments(HG - 1, False, True)

            pe.wait_ge(em_loaded, 16 * 4)
            pe.wait_ge(e2_loaded, 16 * 2)
            pe.wait_ge(plan_ready, 1)

            def expert_of(s):
                return pe.value_load(expert_i[0:1, bass.ds(s, 1)], min_val=0, max_val=NE - 1)

            def turn_rows(s, u):
                pe.wait_ge(gathered[u], (s - u) * PER + 16)
                for c in range(DC):
                    last = pe.transpose(ps[:, u % 2, c * P:(c + 1) * P], xg[:, u, c * P:(c + 1) * P], ident[:, :])
                last.then_inc(xgT_ps, 1)

            def up(s, u):
                e = expert_of(s)
                pe.wait_ge(xgT_ready, s + 1)
                for c in range(DC):
                    last = mm(ps[:, 2 + u % 2, 0:2 * INTER], xgT[:, u % 2, c, :],
                              e13_sb[:, c, bass.ds(e, 1), :].rearrange("p e i -> p (e i)"), c == 0, c == DC - 1)
                last.then_inc(e13_ps, 1)

            def turn_hidden(s, u):
                pe.wait_ge(hid_ready, s + 1)
                pe.transpose(ps[:, 4 + u % 2, 0:P], hid[:, u % 2, 0:P], ident[:, :])
                pe.transpose(ps[0:IR, 4 + u % 2, P:2 * P], hid[:, u % 2, P:INTER], ident[:, :]).then_inc(hidT_ps, 1)

            def down(s, u):
                e = expert_of(s)
                if not (isinstance(s, int) and s < 2):
                    pe.wait_ge(yg_ready, s - 1)
                pe.wait_ge(hidT_ready, s + 1)
                mm(ps[:, 6 + u % 2, 0:D], hidT[:, u % 2, 0, :], e2a_sb[:, bass.ds(e, 1), :]
                   .rearrange("p e d -> p (e d)"), True, False)
                mm(ps[:, 6 + u % 2, 0:D], hidT[0:IR, u % 2, 1, :], e2b_sb[0:IR, bass.ds(e, 1), :]
                   .rearrange("p e d -> p (e d)"), False, True).then_inc(e2_ps, 1)

            turn_rows(0, 0)
            turn_rows(1, 1)
            up(0, 0)

            def slot_tiles(s, u, last):
                if not (last and u + 2 >= GB):
                    turn_rows(s + 2, (u + 2) % GB)
                if not (last and u + 1 >= GB):
                    up(s + 1, (u + 1) % GB)
                if not first(s):
                    down(s - 1, (u - 1) % GB)
                turn_hidden(s, u)

            in_groups(slot_tiles, pe)
            down(SLOT_TILES - 1, GB - 1)

        @block.scalar
        def _(act):
            def copy(out_, in_):
                return act.activation(out_, in_, ACT.Copy)

            def bank(n):
                return ps[:, n, :].rearrange("p (a b) -> p a b", a=2)

            act.wait_ge(const_ready, N_CONST)
            for n, w in enumerate((wq, wk)):
                for c in range(DC):
                    act.wait_ge(fused_ps, 2 * n + c + 1)
                    act.mul(w[0][:, c, :], ps[:, 2 * n + c, :], PROJ_SCALE).then_inc(split_hi, 1)
            def copy_next(a):
                act.wait_ge(xnT_ps, a + 1)
                copy(xnT[0], bank(5)).then_inc(xnT_hi, 1)

            act.wait_ge(attn_loaded, 16 * 2)
            for w, raw in ((wv, raw_v), (wo, raw_o)):
                copy(w[0], raw[:, :, :]).then_inc(split_hi, 1)
            copy_next(0)

            def turn(i, a, f, b, nxt):
                if a is not None:
                    act.wait_ge(v_ps, a + 1)
                    copy(v1[:, :, :, 0:DH], ps[:, 5, :].rearrange("p (t h d) -> p t h d", t=TS, h=H))\
                        .then_inc(v1_ready, 1)
                def features(g):
                    act.wait_ge(nmax_ready, a * 4 + (g + 1))
                    for h in range(H):
                        last = act.activation(phi[:, g, h, :], ps[:, g, h * M:(h + 1) * M], ACT.Exp,
                                              bias=nmax[:, g, h:h + 1])
                    last.then_inc(phi_ready, 1)

                def hidden(g, bank_no):
                    act.wait_ge(w1_ps, f * 4 + (g + 1))
                    if g >= 2:
                        act.wait_ge(fT_ready, f * 4 + (g - 1))
                    elif not first(f):
                        act.wait_ge(fT_ready, f * 4 + (g - 1))
                    for n in range(2):
                        bias = b1_sb[:, 2 * g + n:2 * g + n + 1]
                        act.activation(fT[0][:, 2 * g + n, :], bank(bank_no)[:, n, :], ACT.Relu, bias=bias)
                        last = act.activation(relu[:, g % 2, n, :], bank(bank_no)[:, n, :], ACT.Relu, bias=bias)
                    last.then_inc(relu_ready, 1)

                if b is not None:
                    act.wait_ge(k_ps, b + 1)
                    for c in range(DC):
                        last = act.activation(kT[0][:, c, :], bank(7)[:, c, :], ACT.Identity, bias=bk_sb[:, c:c + 1])
                    last.then_inc(kT_hi, 1)
                if b is not None:
                    act.wait_ge(xn2T_ps, b + 1)
                    copy(xn2T[0], bank(6)).then_inc(xn2T_hi, 1)
                if a is not None:
                    features(0)
                if f is not None:
                    act.wait_ge(zT_ps, f + 1)
                    copy(hT[0], bank(4)).then_inc(hT_hi, 1)
                if b is not None:
                    act.wait_ge(q_ps, b + 1)
                    for c in range(DC):
                        last = act.activation(qT[0][:, c, :], bank(6)[:, c, :], ACT.Identity, bias=bq_sb[:, c:c + 1])
                    last.then_inc(qT_hi, 1)
                if a is not None:
                    features(1)
                if f is not None:
                    if first(f):
                        act.wait_ge(b1_ready, 1)
                    hidden(0, 2)
                if b is not None:
                    act.wait_ge(snmax_ready, b + 1)
                    for t in range(TS):
                        last = act.activation(pr[:, t, :], bank(7)[:, t, :], ACT.Exp, bias=snmax[:, t:t + 1],
                                              accum_out=ssum[:, t:t + 1])
                    last.then_inc(pr_ready, 1)
                if f is not None:
                    hidden(1, 3)
                if b is not None:
                    act.wait_ge(v2_ps, b + 1)
                    copy(v2[0], bank(6)).then_inc(v2_hi, 1)
                if f is not None:
                    hidden(2, 0)
                    hidden(3, 1)
                if a is not None:
                    features(2)
                    features(3)
                if b is not None:
                    act.wait_ge(prT_ps, b + 1)
                    copy(prT[0], bank(7)).then_inc(prT_hi, 1)
                if a is not None:
                    for n in range(2):
                        act.wait_ge(qpT_ps, a * 2 + (n + 1))
                        last = act.activation(qpT[:, 2 * n:2 * n + 2, :], bank(n), ACT.Identity,
                                              bias=feat_eps[:, 0:1], scale=PHI_SCALE)
                    last.then_inc(qpT_ready, 1)
                if b is not None:
                    act.wait_ge(xn3T_ps, b + 1)
                    copy(xn3T, bank(7)).then_inc(xn3T_ready, 1)
                if a is not None:
                    act.wait_ge(attnT_ps, a + 1)
                    copy(attnT[0], bank(2)).then_inc(attnT_hi, 1)
                if nxt is not None:
                    copy_next(nxt)
                if first(i):
                    act.wait_ge(ffn_loaded, 16 * 6)
                    for c in range(DC):
                        act.activation(w1[0][:, c, :], raw_w1[:, c, :], ACT.Copy, scale=gam_sb[:, c:c + 1])\
                            .then_inc(split_hi, 1)
                    for c in range(2):
                        half = slice(c * FC // 2, (c + 1) * FC // 2)
                        copy(w2[0][:, half, :], raw_w2[:, half, :]).then_inc(split_hi, 1)
                    act.wait_ge(cross_loaded, 16 * 7)
                    act.mul(xwq[0], raw_xq[:, :, :], SCORE_SCALE).then_inc(split_hi, 1)
                    copy(xwk[0], raw_xk[:, :, :]).then_inc(split_hi, 1)
                    copy(xwv[0], raw_xv[:, :, :]).then_inc(split_hi, 1)
                    act.wait_ge(split_lo, N_SPLIT)

            in_turns(act, turn)

            act.wait_ge(gap_ready, 1)
            act.activation(egap[:, :], gap[:, :], ACT.Exp).then_inc(egap_ready, 1)
            act.wait_ge(plan_ready, 1)

            def gate_half(s, u):
                if not (isinstance(s, int) and s < 2):
                    act.wait_ge(hid_ready, s - 1)
                act.wait_ge(e13_ps, s + 1)
                act.activation(silu[:, u % 2, :], ps[:, 2 + u % 2, 0:INTER], ACT.Silu).then_inc(silu_ready, 1)

            def rows_out(s, u):
                if not (isinstance(s, int) and s < GB):
                    act.wait_ge(scattered[u], (s - u) * PER)
                act.wait_ge(e2_ps, s + 1)
                copy(yg[:, u, :], ps[:, 6 + u % 2, 0:D]).then_inc(yg_ready, 1)

            gate_half(0, 0)

            def slot_tiles(s, u, last):
                if not (last and u + 1 >= GB):
                    gate_half(s + 1, (u + 1) % GB)
                if not first(s):
                    rows_out(s - 1, (u - 1) % GB)

            in_groups(slot_tiles, act)
            rows_out(SLOT_TILES - 1, GB - 1)

            with act.Fori(0, NSEQ) as n:
                act.wait_ge(sum_ready, n + 1)
                act.dma_start(out_v[:, tiles_of(n), :], X[:, tiles_of(n), :]).then_inc(out_stored, 16)
            act.wait_ge(out_stored, 16 * NSEQ)

        @block.vector
        def _(dve):
            def bank(n):
                return ps[:, n, :].rearrange("p (a b) -> p a b", a=2)

            def x_tile(seq, t):
                return X[:, bass.ds(seq * TS + t, 1), :].rearrange("p t d -> p (t d)")

            def ln_stats(n, seq, src):
                for t in range(TS):
                    last = dve.bn_stats(stat[:, n, t, :], src(t))
                last.then_inc(stat_ready[n], 1)
                hold(dve, stat_ready[n], seq + 1)
                for t in range(TS):
                    last = dve.bn_aggr(mv[:, n, t, :], stat[:, n, t, :])
                last.then_inc(mv_ready[n], 1)

            def ln_apply(n, seq, src, dst, done):
                dve.wait_ge(mv_ready[n], seq + 1)
                dve.wait_ge(rstd_ready[n], seq + 1)
                for t in range(TS):
                    last = dve.tensor_scalar(dst[:, t, :], src(t), mv[:, n, t, 0:1], rstd[:, n, t:t + 1],
                                             ALU.subtract, ALU.mult)
                last.then_inc(done, 1)

            def rest(dst, whole, hi, waits, value, done):
                dve.wait_ge(waits, value)
                dve.tensor_tensor(dst, whole, hi.bitcast(F32), ALU.subtract).then_inc(done, 1)

            def rest_biased(dst, whole, bias, hi, waits, value, done):
                dve.wait_ge(waits, value)
                for c in range(DC):
                    last = dve.scalar_tensor_tensor(dst[:, c, :], whole[:, c, :], bias[:, c:c + 1],
                                                    hi[:, c, :].bitcast(F32), ALU.add, ALU.subtract)
                last.then_inc(done, 1)

            dve.wait_ge(const_ready, N_CONST)
            hold(dve, x_loaded, 16)
            ln_stats(0, 0, lambda t: x_tile(0, t))
            ln_apply(0, 0, lambda t: x_tile(0, t), xn_next, xn_ready)
            for n, w in enumerate((wq, wk)):
                for c in range(DC):
                    dve.wait_ge(split_hi, 2 * n + c + 1)
                    dve.scalar_tensor_tensor(w[1][:, c, :], ps[:, 2 * n + c, :], PROJ_SCALE,
                                             w[0][:, c, :].bitcast(F32), ALU.mult, ALU.subtract).then_inc(split_lo, 1)
            for n, (w, raw) in enumerate(((wv, raw_v), (wo, raw_o))):
                rest(w[1], raw[:, :, :], w[0], split_hi, 5 + n, split_lo)

            def rest_next(a):
                rest(xnT[1], bank(5), xnT[0], xnT_hi, a + 1, xnT_ready)

            rest_next(0)

            def turn(i, a, f, b, nxt):
                def row_max(g):
                    dve.wait_ge(proj_ps, a * 4 + (g + 1))
                    dve.tensor_reduce(nmax[:, g, :], ps[:, g, :].rearrange("p (h m) -> p h m", h=H), AX_X, ALU.max,
                                      negate=True).then_inc(nmax_ready, 1)

                def hidden(g):
                    rest(fT[1][:, 2 * g:2 * g + 2, :], relu[:, g % 2], fT[0][:, 2 * g:2 * g + 2, :],
                         relu_ready, f * 4 + (g + 1), fT_ready)

                if a is not None:
                    row_max(0)
                if f is not None:
                    ln_apply(1, f, lambda t: y[:, t, :], y, z_ready)
                if b is not None:
                    rest_biased(kT[1], bank(7), bk_sb, kT[0], kT_hi, b + 1, kT_ready)
                if b is not None:
                    rest(xn2T[1], bank(6), xn2T[0], xn2T_hi, b + 1, xn2T_ready)
                if a is not None:
                    row_max(1)
                if f is not None:
                    rest(hT[1], bank(4), hT[0], hT_hi, f + 1, hT_ready)
                if b is not None:
                    rest_biased(qT[1], bank(6), bq_sb, qT[0], qT_hi, b + 1, qT_ready)
                if b is not None:
                    dve.wait_ge(score_ps, b + 1)
                    dve.tensor_reduce(snmax[:, :], bank(7), AX_X, ALU.max, negate=True).then_inc(snmax_ready, 1)
                if f is not None:
                    hidden(0)
                    hidden(1)
                if b is not None:
                    rest(v2[1], bank(6), v2[0], v2_hi, b + 1, v2_ready)
                if f is not None:
                    hidden(2)
                    hidden(3)
                if a is not None:
                    row_max(2)
                    row_max(3)
                if b is not None:
                    rest(prT[1], bank(7), prT[0], prT_hi, b + 1, prT_ready)
                    dve.wait_ge(pr_ready, b + 1)
                    dve.reciprocal(rsum[:, :], ssum[:, :]).then_inc(rsum_ready, 1)
                if nxt is not None:
                    hold(dve, x_loaded, (nxt + 1) * 16)
                    ln_stats(0, nxt, lambda t: x_tile(nxt, t))
                if a is not None:
                    for n in range(2):
                        dve.wait_ge(kpT_ps, a * 2 + (n + 1))
                        last = dve.tensor_scalar(kpT[:, 2 * n:2 * n + 2, :], bank(2 + n), PHI_SCALE, FEAT_EPS,
                                                 ALU.mult, ALU.add)
                    last.then_inc(kpT_ready, 1)
                if b is not None:
                    dve.wait_ge(av_ps, b + 1)
                    dve.wait_ge(xbv_ready, b + 1)
                    dve.wait_ge(rsum_ready, b + 1)
                    for t in range(TS):
                        last = dve.scalar_tensor_tensor(x_tile(b, t), bank(6)[:, t, :], rsum[:, t:t + 1], x_tile(b, t),
                                                        ALU.mult, ALU.add)
                    last.then_inc(x2_ready, 1)
                if a is not None:
                    for h in range(H):
                        dve.wait_ge(aT_ps, a * 4 + (h + 1))
                        dve.tensor_tensor(aT[:, h, :], ps[:, h, 0:ATW], mask[:, :], ALU.mult).then_inc(aT_ready, 1)
                if b is not None:
                    hold(dve, x2_ready, b + 1)
                    ln_stats(3, b, lambda t: x_tile(b, t))
                if nxt is not None:
                    dve.wait_ge(xn_kept, nxt)
                    ln_apply(0, nxt, lambda t: x_tile(nxt, t), xn_next, xn_ready)
                if b is not None:
                    if not first(b):
                        dve.wait_ge(xn3_stored, b * 16)
                    ln_apply(3, b, lambda t: x_tile(b, t), xn3, xn3_ready)
                if a is not None:
                    num = ps[:, 0:TS, 0:H * V1W].rearrange("p t (h d) -> p t h d", h=H)
                    dve.wait_ge(num_ps, a + 1)
                    dve.tensor_scalar(den[:, :, :], num[:, :, :, DH], FEAT_EPS, None, ALU.add).then_inc(den_ready, 1)
                    dve.wait_ge(den_ready, a + 1)
                    dve.reciprocal(rden[:, :, :], den[:, :, :]).then_inc(rden_ready, 1)
                    dve.wait_ge(rden_ready, a + 1)
                    dve.tensor_tensor(attn.rearrange("p t (h d) -> p t h d", h=H), num[:, :, :, 0:DH],
                                      rden[:, :, :].unsqueeze(3).broadcast_to([P, TS, H, DH]), ALU.mult)\
                        .then_inc(attn_ready, 1)
                    rest(attnT[1], bank(2), attnT[0], attnT_hi, a + 1, attnT_ready)
                if nxt is not None:
                    rest_next(nxt)
                if f is not None:
                    dve.wait_ge(w2_ps, f + 1)
                    dve.wait_ge(xb2_ready, f + 1)
                    xs = X[:, tiles_of(f), :]
                    dve.tensor_tensor(xs, bank(4), xs, ALU.add).then_inc(x1_ready, 1)
                    hold(dve, x1_ready, f + 1)
                    ln_stats(2, f, lambda t: x_tile(f, t))
                if b is not None:
                    hold(dve, logit_ps, b + 1)
                    dve.tensor_copy(logits[:, tiles_of(b), :],
                                    ps[:, 6, 0:TS * NE].rearrange("p (t e) -> p t e", e=NE)).then_inc(logit_ready, 1)
                if a is not None:
                    dve.wait_ge(wo_ps, a + 1)
                    dve.wait_ge(xn_kept, a + 1)
                    dve.tensor_tensor(y, bank(3), xn, ALU.add).then_inc(y_ready, 1)
                    hold(dve, y_ready, a + 1)
                    ln_stats(1, a, lambda t: y[:, t, :])
                if f is not None:
                    ln_apply(2, f, lambda t: x_tile(f, t), xn2, xn2_ready)
                if first(i):
                    for c in range(DC):
                        dve.wait_ge(split_hi, 7 + c)
                        dve.scalar_tensor_tensor(w1[1][:, c, :], raw_w1[:, c, :], gam_sb[:, c:c + 1],
                                                 w1[0][:, c, :].bitcast(F32), ALU.mult, ALU.subtract)\
                            .then_inc(split_lo, 1)
                    for c in range(2):
                        half = slice(c * FC // 2, (c + 1) * FC // 2)
                        rest(w2[1][:, half, :], raw_w2[:, half, :], w2[0][:, half, :], split_hi, 9 + c, split_lo)
                    dve.wait_ge(split_hi, 11)
                    dve.scalar_tensor_tensor(xwq[1], raw_xq[:, :, :], SCORE_SCALE, xwq[0].bitcast(F32),
                                             ALU.mult, ALU.subtract).then_inc(split_lo, 1)
                    rest(xwk[1], raw_xk[:, :, :], xwk[0], split_hi, 12, split_lo)
                    rest(xwv[1], raw_xv[:, :, :], xwv[0], split_hi, 13, split_lo)
                    dve.tensor_scalar(bq_sb[:, :], bq_sb[:, :], SCORE_SCALE, None, ALU.mult).then_inc(split_lo, 1)
                    dve.wait_ge(b1_ps, 1)
                    dve.tensor_tensor(b1_sb[:, :], ps[:, 4, 0:FC], b1_sb[:, :], ALU.add).then_inc(b1_ready, 1)

            in_turns(dve, turn)

            steps = [0]

            def then(ins):
                steps[0] += 1
                ins.then_inc(routed, 1)
                dve.wait_ge(routed, steps[0])

            def over_e(row):
                return row.unsqueeze(2).broadcast_to([P, NT, NE])

            def over_t(row):
                return row.unsqueeze(1).broadcast_to([P, NT, NE])

            dve.wait_ge(logit_ready, NSEQ)
            dve.wait_ge(xn3_stored, 16 * NSEQ)
            back = over_t(iota_back[:, :])

            def choose(scores, best, pick, hot):
                then(dve.tensor_reduce(best[:, :], scores, AX_X, ALU.max))
                then(dve.tensor_tensor(tmp_a, scores, over_e(best[:, :]), ALU.is_equal))
                then(dve.tensor_tensor(tmp_b, tmp_a, back, ALU.mult))
                then(dve.tensor_reduce(pick[:, :], tmp_b, AX_X, ALU.max))
                then(dve.tensor_tensor(hot, back, over_e(pick[:, :]), ALU.is_equal))

            choose(logits[:, :, :], best1, pick1, oh1)
            then(dve.scalar_tensor_tensor(masked, oh1, -3e38, logits[:, :, :], ALU.mult, ALU.add))
            choose(masked, best2, pick2, oh2)
            dve.tensor_tensor(gap[:, :], best2[:, :], best1[:, :], ALU.subtract).then_inc(gap_ready, 1)
            dve.tensor_tensor(oh, oh1, oh2, ALU.add).then_inc(oh_ready, 1)
            dve.wait_ge(egap_ready, 1)
            then(dve.tensor_scalar(gden[:, :], egap[:, :], 1.0, None, ALU.add))
            then(dve.reciprocal(gate1[:, :], gden[:, :]))
            then(dve.tensor_tensor(gate2[:, :], gate1[:, :], egap[:, :], ALU.mult))
            dve.wait_ge(rank_ps, 1)
            per_tile = ps[:, 1, :].rearrange("p (t e) -> p t e", e=NE)
            then(dve.tensor_copy(tot, per_tile))
            src, bufs, n = tot, (tmp_a, tmp_b), 1
            while n < NT:
                dst = bufs[0]
                bufs = bufs[::-1]
                dve.tensor_copy(dst[:, 0:n, :], src[:, 0:n, :])
                then(dve.tensor_tensor(dst[:, n:, :], src[:, n:, :], src[:, 0:NT - n, :], ALU.add))
                src, n = dst, 2 * n
            upto, spare = src, bufs[0]
            then(dve.tensor_scalar(need_i[:, :], upto[:, NT - 1, :], float(P - 1), None, ALU.add))
            then(dve.tensor_scalar(need_s[:, :], need_i[:, :], 7, None, ALU.logical_shift_right))
            then(dve.tensor_copy(need[:, :], need_s[:, :]))
            csrc, cbufs, n = need, (cum_a, cum_b), 1
            while n < NE:
                dst = cbufs[0]
                cbufs = cbufs[::-1]
                dve.tensor_copy(dst[:, 0:n], csrc[:, 0:n])
                then(dve.tensor_tensor(dst[:, n:], csrc[:, n:], csrc[:, 0:NE - n], ALU.add))
                csrc, n = dst, 2 * n
            cum = csrc
            then(dve.tensor_tensor(base[:, :], cum[:, :], need[:, :], ALU.subtract))
            then(dve.tensor_tensor(spare, upto, tot, ALU.subtract))
            then(dve.scalar_tensor_tensor(masked, over_t(base[:, :]), float(P), spare, ALU.mult, ALU.add))
            then(dve.tensor_tensor(spare, masked, ps[:, 0, :].rearrange("p (t e) -> p t e", e=NE), ALU.add))
            for j, hot in enumerate((oh1, oh2)):
                then(dve.tensor_tensor(masked, hot, spare, ALU.mult))
                then(dve.tensor_reduce(slot[:, :, j], masked, AX_X, ALU.add))
            then(dve.tensor_copy(slot_i[:, :, :], slot[:, :, :]))
            then(dve.tensor_scalar(slot_hi_i[:, :, :], slot_i[:, :, :], 7, None, ALU.logical_shift_right))
            then(dve.tensor_scalar(slot_lo_i[:, :, :], slot_i[:, :, :], P - 1, None, ALU.bitwise_and))
            then(dve.tensor_copy(slot_hi[:, :, :], slot_hi_i[:, :, :]))
            then(dve.tensor_copy(slot_lo[:, :, :], slot_lo_i[:, :, :]))
            then(dve.tensor_tensor(early[0:1], cum[0:1, :].unsqueeze(1).broadcast_to([1, SLOT_TILES, NE]),
                                   iota_tile[0:1, :].unsqueeze(2).broadcast_to([1, SLOT_TILES, NE]), ALU.is_le))
            then(dve.tensor_reduce(expert_f[0:1, :], early[0:1], AX_X, ALU.add))
            then(dve.tensor_scalar(expert_i[:, :], expert_f[0:1, :], float(NE - 1), None, ALU.min))
            def hots(g, again):
                for k in range(HB):
                    t, j = g * (HB // TOPK) + k // TOPK, k % TOPK
                    if again:
                        dve.wait_ge(table_ps, g * HB + (k + 1 - HB))
                    dve.tensor_scalar(hot_slot[:, k, :], iota_slot[:, :], slot_lo[:, bass.ds(t, 1), j], None,
                                      ALU.is_equal)
                    dve.tensor_scalar(hot_tile[:, k, :], iota_tile[:, :], slot_hi[:, bass.ds(t, 1), j],
                                      assign_no[:, bass.ds(t, 1), j], ALU.is_equal, ALU.mult).then_inc(hot_ready, 1)

            hots(0, False)
            with dve.Fori(1, NT * TOPK // HB) as g:
                hots(g, True)
            dve.wait_ge(table_ps, NT * TOPK)
            then(dve.tensor_copy(table[:, :], ps[:, 2, 0:SLOT_TILES]))
            then(dve.tensor_scalar(empty[:, :], table[:, :], 0.0, None, ALU.is_equal))
            then(dve.tensor_tensor(gath_f[:, :], empty[:, :], dump_no[:, :], ALU.mult))
            then(dve.tensor_tensor(scat_f[:, :], table[:, :], gath_f[:, :], ALU.add))
            then(dve.tensor_scalar(scat_i[:, :], scat_f[:, :], -1.0, None, ALU.add))
            then(dve.tensor_scalar(gath_j[:, :], table[:, :], -1.0, 0.0, ALU.add, ALU.max))
            dve.tensor_scalar(gath_i[:, :], gath_j[:, :], 1, None, ALU.logical_shift_right).then_inc(plan_ready, 1)

            dve.wait_ge(plan_ready, 1)

            def rows_in(s, u):
                dve.wait_ge(xgT_ps, s + 1)
                dve.tensor_copy(xgT[:, u % 2], ps[:, u % 2, 0:D].rearrange("p (c s) -> p c s", c=DC))\
                    .then_inc(xgT_ready, 1)

            def product(s, u):
                dve.wait_ge(silu_ready, s + 1)
                dve.tensor_tensor(hid[:, u % 2, :], ps[:, 2 + u % 2, INTER:2 * INTER], silu[:, u % 2, :], ALU.mult)\
                    .then_inc(hid_ready, 1)

            def hidden_in(s, u):
                if not (isinstance(s, int) and s < 2):
                    dve.wait_ge(e2_ps, s - 1)
                dve.wait_ge(hidT_ps, s + 1)
                dve.tensor_copy(hidT[:, u % 2, 0, :], ps[:, 4 + u % 2, 0:P])
                dve.tensor_copy(hidT[0:IR, u % 2, 1, :], ps[0:IR, 4 + u % 2, P:2 * P]).then_inc(hidT_ready, 1)

            rows_in(0, 0)
            rows_in(1, 1)
            product(0, 0)

            def slot_tiles(s, u, last):
                if not (last and u + 2 >= GB):
                    rows_in(s + 2, (u + 2) % GB)
                if not (last and u + 1 >= GB):
                    product(s + 1, (u + 1) % GB)
                hidden_in(s, u)

            in_groups(slot_tiles, dve)

            with dve.Fori(0, NSEQ // YB) as g:
                for u in range(YB):
                    n = g * YB + u
                    dve.wait_ge(y_loaded[u], g * 16 + 16)
                    for j, gate, done in ((0, gate1, part_ready), (1, gate2, sum_ready)):
                        for t in range(TS):
                            last = dve.scalar_tensor_tensor(x_tile(n, t), yl[:, u, t, j, :],
                                                            gate[:, bass.ds(n * TS + t, 1)], x_tile(n, t),
                                                            ALU.mult, ALU.add)
                        last.then_inc(done, 1)
                        if j == 0:
                            dve.wait_ge(part_ready, n + 1)




def kernel(**inputs):
    import numpy as np
    import concourse.bacc as bacc
    from concourse.bass_utils import run_bass_kernel_spmd

    def flat(name):
        return np.ascontiguousarray(inputs[name])

    def turned(name, axes=None):
        return np.ascontiguousarray(np.transpose(inputs[name], axes))

    def by_partition(name):
        return np.ascontiguousarray(inputs[name].reshape(-1, P).T)

    arrays = {
        "x": flat("x"),
        "ctxT": turned("ctx_1024", (0, 2, 1)),
        "WqT": turned("L0_attn_Wq"),
        "WkT": turned("L0_attn_Wk"),
        "Wv": flat("L0_attn_Wv"),
        "Wo": flat("L0_attn_Wo"),
        "omegaT": turned("L0_attn_omega"),
        "W1": flat("L0_attn_W1"),
        "b1": by_partition("L0_attn_b1"),
        "W2": flat("L0_attn_W2"),
        "b2": flat("L0_attn_b2"),
        "gamma": by_partition("L0_attn_gamma"),
        "beta": by_partition("L0_attn_beta"),
        "xWqT": turned("L0_xattn_Wq"),
        "xbq": by_partition("L0_xattn_bq"),
        "xWkT": turned("L0_xattn_Wk"),
        "xbk": by_partition("L0_xattn_bk"),
        "xWvT": turned("L0_xattn_Wv"),
        "xbv": flat("L0_xattn_bv"),
        "WgT": turned("L0_ffn_Wg"),
        "E1": flat("L0_ffn_W1"),
        "E3": flat("L0_ffn_W3"),
        "E2": flat("L0_ffn_W2"),
    }
    nc = bacc.Bacc("TRN2", target_bir_lowering=False, num_devices=1)
    aps = {n: nc.dram_tensor(f"in_{n}", a.shape, mybir.dt.from_np(a.dtype), kind="ExternalInput").ap()
           for n, a in arrays.items()}
    out = nc.dram_tensor("out", inputs["x"].shape, F32, kind="ExternalOutput").ap()
    decoder(nc, **aps, out=out)
    r = run_bass_kernel_spmd(nc, [{f"in_{n}": a for n, a in arrays.items()}], core_ids=[0])
    return r.results[0]["out"]
```

```python
from contextlib import ExitStack

import concourse.bass as bass
from concourse import mybir

F32 = mybir.dt.float32
F32R = mybir.dt.float32r
I32 = mybir.dt.int32
ALU = mybir.AluOpType
ACT = mybir.ActivationFunctionType
AX_X = mybir.AxisListType.X

P = 128
LN_EPS = 1e-5
ATTN_LN_EPS = 1e6
FEAT_EPS = 1e-6


def decoder(nc, x, ctxT, WqT, WkT, Wv, Wo, omegaT, W1, b1, W2, b2, gamma, beta,
            xWqT, xbq, xWkT, xbk, xWvT, xbv, WgT, E1, E3, E2, out):
    NSEQ, S, D = x.shape
    DC = D // P
    TS = S // P
    NT = NSEQ * TS
    DH, M = omegaT.shape
    H = D // DH
    FF = W1.shape[1]
    FC = FF // P
    NE = WgT.shape[1]
    INTER = E1.shape[2]
    IR = INTER - P
    LO = 64
    TOPK = 2
    SLOT_TILES = NT * TOPK + NE
    NASSIGN = NT * P * TOPK
    SCORE_SCALE = float(D) ** -0.5
    PHI_SCALE = float(M) ** -0.5
    PROJ_SCALE = float(DH) ** -0.25
    V1W = DH + 1
    ATW = S + P
    assert DC == 2 and TS == 2 and H * P == 512 and M == P and FC == 8
    assert SLOT_TILES <= P and SLOT_TILES % 16 == 0 and IR <= LO and LO + IR <= P

    xn3_dram = nc.dram_tensor("xn3_rows", (NT * P, D), F32, kind="Internal").ap()
    y_dram = nc.dram_tensor("expert_rows", (NASSIGN + SLOT_TILES * P, D), F32, kind="Internal").ap()

    x_v = x.rearrange("b (t p) d -> p (b t) d", p=P)
    out_v = out.rearrange("b (t p) d -> p (b t) d", p=P)
    ctx_v = ctxT.rearrange("b (c p) s -> p b c s", p=P)
    TABLE_ROWS = NE * NT + 1
    table_dram = nc.dram_tensor("assignments", (TABLE_ROWS, P), F32, kind="Internal").ap()
    table_flat = table_dram.rearrange("r (c o) -> (r c) o", o=1)

    xn3_v = xn3_dram.rearrange("(t p) d -> p t d", p=P)
    y_v = y_dram[0:NASSIGN, :].rearrange("(t p j) d -> p t (j d)", p=P, j=TOPK)

    with ExitStack() as stack:
        def sb(name, shape, dt=F32):
            return stack.enter_context(nc.sbuf_tensor(name, shape, dt))

        def sem(name):
            return stack.enter_context(nc.semaphore(name))

        X = sb("X", [P, NT, D])
        wg_sb = sb("wg_sb", [P, DC, NE])
        b1_sb = sb("b1_sb", [P, FC])
        gam_sb = sb("gam_sb", [P, DC])
        bet_sb = sb("bet_sb", [P, DC])
        bq_sb = sb("bq_sb", [P, DC])
        bk_sb = sb("bk_sb", [P, DC])
        b2_sb = sb("b2_sb", [P, D])
        bv_sb = sb("bv_sb", [P, D])
        ident = sb("ident", [P, P])
        mask = sb("mask", [P, ATW])
        before = sb("before", [P, P])
        ones = sb("ones", [P, P])
        halfneg = sb("halfneg", [P, TS])
        eps_ln = sb("eps_ln", [P, TS])
        eps_attn = sb("eps_attn", [P, TS])
        feat_eps = sb("feat_eps", [P, 1])
        back = sb("back", [P, TS, NE])
        part_no = sb("part_no", [P, 1])
        place0 = sb("place0", [P, NE])
        assign_no = sb("assign_no", [P, NT, TOPK])
        dump_no = sb("dump_no", [P, SLOT_TILES])

        logits, eq, masked, oh, upto = (sb(n, [P, TS, NE]) for n in ("logits", "eq", "masked", "oh", "upto"))
        hot = sb("hot", [P, TOPK, TS, NE])
        best, pick = sb("best", [P, TOPK, TS]), sb("pick", [P, TOPK, TS])
        counts = sb("counts", [P, 2 * TS, NE])
        carry = sb("carry", [P, TS, NE])
        sums = sb("sums", [P, TOPK, TS, NE])
        place_i = sb("place_i", [P, TOPK, TS], I32)
        assign = sb("assign", [P, TS * TOPK])
        stat = sb("stat", [P, 4, TS, 6])
        mv = sb("mv", [P, 4, TS, 2])
        veps = sb("veps", [P, 4, TS])
        rstd = sb("rstd", [P, 4, TS])
        nmax = sb("nmax", [P, 4, H])
        den = sb("den", [P, TS, H])
        rden = sb("rden", [P, TS, H])
        snmax = sb("snmax", [P, TS])
        ssum = sb("ssum", [P, TS])
        rsum = sb("rsum", [P, TS])
        gap, egap, gden, gate1, gate2 = (sb(n, [P, NT]) for n in ("gap", "egap", "gden", "gate1", "gate2"))
        need_i, need_s = sb("need_i", [P, NE], I32), sb("need_s", [P, NE], I32)
        total, need, cum_a, cum_b, ended, ended_need = (sb(n, [P, NE]) for n in (
            "total", "need", "cum_a", "cum_b", "ended", "ended_need"))
        expert_of_tile, first_tile, row_f, row_g = (sb(n, [P, 1]) for n in (
            "expert_of_tile", "first_tile", "row_f", "row_g"))
        silu_first = sb("silu_first", [P, 1])
        row_i = sb("row_i", [P, 1], I32)
        by_tile = sb("by_tile", [P, P])
        table, empty, scat_f, gath_f = (sb(n, [P, SLOT_TILES]) for n in ("table", "empty", "scat_f", "gath_f"))
        scat_i, gath_i, gath_j = (sb(n, [P, SLOT_TILES], I32) for n in ("scat_i", "gath_i", "gath_j"))
        expert_i = sb("expert_i", [1, SLOT_TILES], I32)

        early_scope = ExitStack()

        def sb1(name, shape, dt=F32, scope=early_scope):
            return scope.enter_context(nc.sbuf_tensor(name, shape, dt))

        def pair(name, n):
            return tuple(sb1(f"{name}_{part}", [P, n], F32R)[:, :] for part in ("hi", "lo"))

        def cut(tiles, pattern, **sizes):
            return tuple(t.rearrange(pattern, **sizes) for t in tiles)

        wq, wk = (cut(pair(n, DC * H * M), "p (c n) -> p c n", c=DC) for n in ("wq", "wk"))
        wv, wo = (cut(pair(n, DC * D), "p (c n) -> p c n", c=DC) for n in ("wv", "wo"))
        phi = sb1("phi", [P, 4, H, M])
        qpT = sb1("qpT", [P, H, S])
        kpT = sb1("kpT", [P, H, S])
        xnT, attnT = (cut(pair(n, DC * S), "p (c s) -> p c s", c=DC) for n in ("xnT", "attnT"))
        attn_cols = 2 * (2 * DC * H * M + 2 * DC * D) + 4 * H * M + 2 * H * S + 4 * DC * S
        assert DC * NE * 2 * INTER <= attn_cols
        w1 = cut(pair("w1", DC * FF), "p (c n) -> p c n", c=DC)
        w2 = cut(pair("w2", FC * D), "p (c n) -> p c n", c=FC)
        hT = cut(pair("hT", DC * S), "p (c s) -> p c s", c=DC)
        freed_cols = attn_cols + 2 * (DC * FF + FC * D) + 2 * DC * S
        with ExitStack() as raw_scope:
            raw_wT = sb1("raw_wT", [DH, 2 * H * D + M], F32, raw_scope)
            raw_v, raw_o = (sb1(f"raw_{n}", [P, DC, D], F32, raw_scope) for n in "vo")
            raw_w1 = sb1("raw_w1", [P, DC, FF], F32, raw_scope)
            raw_w2 = sb1("raw_w2", [P, FC, D], F32, raw_scope)
            raw_xq, raw_xk, raw_xv = (sb1(f"raw_x{n}", [P, DC, D], F32, raw_scope) for n in "qkv")
        fT = cut(pair("fT", FC * S), "p (f s) -> p f s", f=FC)
        freed_cols += 2 * FC * S
        xn2T, kT, qT, v2, prT, ctx = (cut(pair(n, DC * S), "p (c s) -> p c s", c=DC) for n in (
            "xn2T", "kT", "qT", "v2", "prT", "ctx"))
        xwq, xwk, xwv = (cut(pair(n, DC * D), "p (c n) -> p c n", c=DC) for n in ("xwq", "xwk", "xwv"))
        xn_next, xn, attn, y, xn2, pr, xn3, xn3T, ctx_raw = (sb1(n, [P, TS, D])[:, :, :] for n in (
            "xn_next", "xn", "attn", "y", "xn2", "pr", "xn3", "xn3T", "ctx_raw"))
        relu = sb1("relu", [P, 2, 2, S])
        v1 = sb1("v1", [P, TS, H, V1W])
        zero_rows = relu[:, :, :, :].rearrange("p a b s -> p (a b s)")[:, 0:TABLE_ROWS]
        aT = phi[:, :, :, :].rearrange("p g h m -> p (g h m)")[:, 0:H * ATW].rearrange("p (h s) -> p h s", h=H)
        early_scope.close()

        QE = NE // 4
        e13_sb = sb("e13_sb", [P, DC, NE, 2 * INTER])
        assert attn_cols == DC * NE * 2 * INTER + QE * D
        e2_tmp_a = sb("e2_tmp_a", [P, QE, D], F32R)
        e2a = tuple(sb(f"e2a_{part}", [P, NE, D], F32R)[:, :, :] for part in ("hi", "lo"))
        e2b = sb("e2b", [P, NE, D], F32R)[:, :, :]
        e2_tmp = (e2_tmp_a, sb("e2_tmp_b", [P, QE, D], F32R))
        assert freed_cols == attn_cols + 3 * NE * D + QE * D
        narrow = sb("narrow", [P, 17 * 512])
        place = [0]

        def carve(n):
            place[0] += n
            return narrow[:, place[0] - n:place[0]]

        GB = 8
        PER = 16 // GB
        LAG = 2
        xg = carve(GB * D).rearrange("p (u d) -> p u d", u=GB)
        yg = carve(GB * D).rearrange("p (u d) -> p u d", u=GB)
        xgT = carve(2 * D).rearrange("p (u c s) -> p u c s", u=2, c=DC)
        silu = carve(2 * INTER).rearrange("p (u i) -> p u i", u=2)
        hid = carve(2 * 2 * P).rearrange("p (u i) -> p u i", u=2)
        hidT = tuple(sb(f"hidT_{part}", [P, 2, 2, P], F32R)[:, :, :, :] for part in ("hi", "lo"))
        gidx = sb("gidx", [P, GB], I32)
        sidx = sb("sidx", [P, GB], I32)
        place[0] = 0
        YB = 4
        yl = carve(YB * TS * TOPK * D).rearrange("p (u t j d) -> p u t j d", u=YB, t=TS, j=TOPK)

        ps = stack.enter_context(nc.psum_tensor("ps", [P, 8, 512], F32))

        fuse_loaded, attn_loaded, ffn_loaded, cross_loaded = (sem(n) for n in (
            "fuse_loaded", "attn_loaded", "ffn_loaded", "cross_loaded"))
        em_loaded, e2_loaded = sem("em_loaded"), sem("e2_loaded")
        hid_zero, e2b_zero, e2_hi, e2_ready = (sem(n) for n in ("hid_zero", "e2b_zero", "e2_hi", "e2_ready"))
        x_loaded, ctx_loaded, xn3_stored = sem("x_loaded"), sem("ctx_loaded"), sem("xn3_stored")
        blank, const_ready = sem("blank"), sem("const_ready")
        fused_ps = sem("fused_ps")
        split_hi, split_lo, pool_split_lo, b1_ps, b1_ready = (sem(n) for n in (
            "split_hi", "split_lo", "pool_split_lo", "b1_ps", "b1_ready"))
        xnT_hi, attnT_hi, hT_hi, xn2T_hi, kT_hi, qT_hi, v2_hi, prT_hi, ctx_hi = (sem(f"{n}_hi_ready") for n in (
            "xnT", "attnT", "hT", "xn2T", "kT", "qT", "v2", "prT", "ctx"))
        ctx_ready = sem("ctx_ready")
        stat_ready = [sem(f"stat{n}_ready") for n in range(4)]
        mv_ready = [sem(f"mv{n}_ready") for n in range(4)]
        veps_ready = [sem(f"veps{n}_ready") for n in range(4)]
        rstd_ready = [sem(f"rstd{n}_ready") for n in range(4)]
        xn_kept = sem("xn_kept")
        xn_ready, z_ready, xn2_ready, xn3_ready = sem("xn_ready"), sem("z_ready"), sem("xn2_ready"), sem("xn3_ready")
        xnT_ps, xnT_ready = sem("xnT_ps"), sem("xnT_ready")
        proj_ps, nmax_ready, phi_ready = sem("proj_ps"), sem("nmax_ready"), sem("phi_ready")
        v_ps, v1_ready = sem("v_ps"), sem("v1_ready")
        qpT_ps, qpT_ready, kpT_ps, kpT_ready = sem("qpT_ps"), sem("qpT_ready"), sem("kpT_ps"), sem("kpT_ready")
        aT_ps, aT_ready = sem("aT_ps"), sem("aT_ready")
        num_ps, den_ready, rden_ready, attn_ready = (sem(n) for n in (
            "num_ps", "den_ready", "rden_ready", "attn_ready"))
        attnT_ps, attnT_ready = sem("attnT_ps"), sem("attnT_ready")
        wo_ps, y_ready = sem("wo_ps"), sem("y_ready")
        zT_ps, hT_ready = sem("zT_ps"), sem("hT_ready")
        w1_ps, relu_ready, fT_ready = sem("w1_ps"), sem("relu_ready"), sem("fT_ready")
        w2_ps, xb2_ready, x1_ready = sem("w2_ps"), sem("xb2_ready"), sem("x1_ready")
        xn2T_ps, xn2T_ready = sem("xn2T_ps"), sem("xn2T_ready")
        k_ps, kT_ready, q_ps, qT_ready = sem("k_ps"), sem("kT_ready"), sem("q_ps"), sem("qT_ready")
        score_ps, snmax_ready, pr_ready, rsum_ready = (sem(n) for n in (
            "score_ps", "snmax_ready", "pr_ready", "rsum_ready"))
        v2_ps, v2_ready, prT_ps, prT_ready = sem("v2_ps"), sem("v2_ready"), sem("prT_ps"), sem("prT_ready")
        av_ps, xbv_ready, x2_ready = sem("av_ps"), sem("xbv_ready"), sem("x2_ready")
        xn3T_ps, xn3T_ready = sem("xn3T_ps"), sem("xn3T_ready")
        logit_ps, logit_ready = sem("logit_ps"), sem("logit_ready")
        chosen = sem("chosen")
        ranked = sem("ranked")
        routed = sem("routed")
        (table_zero, table_cleared, oh_ready, rank_ps, counts_ready, hot_used, assign_ready, place_ready, placed,
         gap_ready, egap_ready, row_ready, expert_ps, table_loaded, table_ps, plan_ready) = (sem(n) for n in (
             "table_zero", "table_cleared", "oh_ready", "rank_ps", "counts_ready", "hot_used", "assign_ready",
             "place_ready", "placed", "gap_ready", "egap_ready", "row_ready", "expert_ps", "table_loaded",
             "table_ps", "plan_ready"))
        gidx_ready, sidx_ready = sem("gidx_ready"), sem("sidx_ready")
        gathered = [sem(f"gathered{u}") for u in range(GB)]
        scattered = [sem(f"scattered{u}") for u in range(GB)]
        xgT_ps, xgT_ready, e13_ps, silu_ready, hid_ready = (sem(n) for n in (
            "xgT_ps", "xgT_ready", "e13_ps", "silu_ready", "hid_ready"))
        hidT_ps, hidT_hi, hidT_ready, e2_ps, yg_ready = (sem(n) for n in (
            "hidT_ps", "hidT_hi_ready", "hidT_ready", "e2_ps", "yg_ready"))
        y_loaded = [sem(f"y_loaded{u}") for u in range(YB)]
        part_ready, sum_ready, out_stored = sem("part_ready"), sem("sum_ready"), sem("out_stored")
        held = sem("held")

        N_CONST = 15
        N_ATTN_SPLIT = 6
        N_DVE_SPLIT = N_ATTN_SPLIT + 4
        N_POOL_SPLIT = 4

        def hold(eng, s, value):
            eng.wait_ge(s, value)
            eng.sem_inc(held)

        def in_turns(eng, turn):
            for i in range(3):
                turn(i, i, i - 1 if i >= 1 else None, i - 2 if i >= 2 else None, None, i + 1)
            with eng.Fori(3, NSEQ - 1) as i:
                turn(i, i, i - 1, i - 2, i - 3, i + 1)
            turn(NSEQ - 1, NSEQ - 1, NSEQ - 2, NSEQ - 3, NSEQ - 4, None)
            turn(NSEQ, None, NSEQ - 1, NSEQ - 2, NSEQ - 3, None)
            turn(NSEQ + 1, None, None, NSEQ - 1, NSEQ - 2, None)
            turn(NSEQ + 2, None, None, None, NSEQ - 1, None)


        def in_groups(step, eng):
            for u in range(GB):
                step(u, u, False)
            with eng.Fori(0, (SLOT_TILES // GB - 2) // 2) as g:
                for u in range(2 * GB):
                    step(g * 2 * GB + (GB + u), u % GB, False)
            for u in range(GB):
                step(SLOT_TILES - GB + u, u, True)

        def first(n):
            return isinstance(n, int) and n == 0

        def tiles_of(seq):
            return bass.ds(seq * TS, TS)

        block = stack.enter_context(nc.Block())

        @block.sync
        def _(sp):
            def load(dst, src, s):
                sp.dma_start(dst, src).then_inc(s, 16)

            def load_x(n):
                if not first(n):
                    sp.wait_ge(x_loaded, n * 16)
                sp.dma_start(X[:, tiles_of(n), :], x_v[:, tiles_of(n), :]).then_inc(x_loaded, 16)

            load_x(0)
            for n, w in enumerate((WqT, WkT)):
                load(raw_wT[:, n * H * D:(n + 1) * H * D].rearrange("p (h d) -> p h d", h=H),
                     w.rearrange("(h e) d -> e h d", h=H), fuse_loaded)
            load(raw_wT[:, 2 * H * D:], omegaT, fuse_loaded)
            load(raw_v[:, :, :], Wv.rearrange("(c p) n -> p c n", p=P), attn_loaded)
            load(raw_o[:, :, :], Wo.rearrange("(c p) n -> p c n", p=P), attn_loaded)
            load(raw_w1[:, :, :], W1.rearrange("(c p) n -> p c n", p=P), ffn_loaded)
            load(b1_sb[:, :], b1, ffn_loaded)
            load(gam_sb[:, :], gamma, ffn_loaded)
            load(bet_sb[:, :], beta, ffn_loaded)
            load(raw_w2[:, :, :], W2.rearrange("(c p) n -> p c n", p=P), ffn_loaded)
            load(b2_sb[:, :], b2.partition_broadcast(P), ffn_loaded)
            load(raw_xq[:, :, :], xWqT.rearrange("(c p) n -> p c n", p=P), cross_loaded)
            load(raw_xk[:, :, :], xWkT.rearrange("(c p) n -> p c n", p=P), cross_loaded)
            load(raw_xv[:, :, :], xWvT.rearrange("(c p) n -> p c n", p=P), cross_loaded)
            load(bq_sb[:, :], xbq, cross_loaded)
            load(bk_sb[:, :], xbk, cross_loaded)
            load(bv_sb[:, :], xbv.partition_broadcast(P), cross_loaded)
            load(wg_sb[:, :, :], WgT.rearrange("(c p) n -> p c n", p=P), cross_loaded)
            load(ctx_raw, ctx_v[:, 0, :, :], ctx_loaded)
            sp.wait_ge(table_zero, 1)
            sp.dma_start(table_dram.rearrange("r c -> (r c)").rearrange("(p k) -> p k", p=P), zero_rows)\
                .then_inc(table_cleared, 16)

            def load_experts_up():
                sp.wait_ge(wo_ps, NSEQ)
                for c in range(DC):
                    for n, w in enumerate((E1, E3)):
                        load(e13_sb[:, c, :, n * INTER:(n + 1) * INTER],
                             w[:, c * P:(c + 1) * P, :].rearrange("e p i -> p e i"), em_loaded)

            def load_experts_down():
                sp.wait_ge(w2_ps, NSEQ)
                load(e2a[1].bitcast(F32), E2[:, 0:P, :].rearrange("e p d -> p e d"), e2_loaded)
                sp.wait_ge(e2b_zero, 1)
                for lo in (0, LO):
                    load(e2b[lo:lo + IR].bitcast(F32), E2[:, P:INTER, :].rearrange("e p d -> p e d"), e2_loaded)

            def turn(i, a, f, b, r, nxt):
                last_ffn = isinstance(i, int) and i == NSEQ
                if last_ffn:
                    load_experts_up()
                if nxt is not None:
                    load_x(nxt)
                if b is not None:
                    if not (isinstance(b, int) and b == NSEQ - 1):
                        sp.wait_ge(ctx_ready, b + 1)
                        sp.dma_start(ctx_raw, ctx_v[:, bass.ds(b + 1, 1), :, :]
                                     .rearrange("p b c s -> p (b c) s")).then_inc(ctx_loaded, 16)
                    if last_ffn:
                        load_experts_down()
                    sp.wait_ge(xn3_ready, b + 1)
                    sp.dma_start(xn3_v[:, tiles_of(b), :], xn3).then_inc(xn3_stored, 16)

            in_turns(sp, turn)
            for u in range(GB):
                sp.wait_ge(scattered[u], 16 * (SLOT_TILES // GB))
            sp.wait_ge(yg_ready, SLOT_TILES)

            def fetch(n, u):
                if not (isinstance(n, int) and n < YB):
                    sp.wait_ge(sum_ready, n - YB + 1)
                sp.dma_start(yl[:, u].rearrange("p t j d -> p t (j d)"), y_v[:, tiles_of(n), :])\
                    .then_inc(y_loaded[u], 16)

            for u in range(YB):
                fetch(u, u)
            with sp.Fori(1, NSEQ // YB) as g:
                for u in range(YB):
                    fetch(g * YB + u, u)

        @block.gpsimd
        def _(pool):
            pool.memset(ones[:, :], 1.0).then_inc(blank, 1)
            pool.memset(halfneg[:, :], -0.5).then_inc(const_ready, 1)
            pool.memset(eps_ln[:, :], LN_EPS).then_inc(const_ready, 1)
            pool.memset(eps_attn[:, :], ATTN_LN_EPS).then_inc(const_ready, 1)
            pool.memset(feat_eps[:, :], FEAT_EPS).then_inc(const_ready, 1)
            pool.memset(v1[:, :, :, DH:V1W], 1.0).then_inc(const_ready, 1)
            pool.memset(mask[:, :], 1.0).then_inc(blank, 1)
            pool.wait_ge(blank, 2)
            pool.affine_select(out=ident[:, :], in_=ones[:, :], compare_op=ALU.is_equal, fill=0.0, base=0,
                               pattern=[[-1, P]], channel_multiplier=1).then_inc(const_ready, 1)
            pool.affine_select(out=before[:, :], in_=ones[:, :], compare_op=ALU.is_gt, fill=0.0, base=0,
                               pattern=[[1, P]], channel_multiplier=-1).then_inc(const_ready, 1)
            for lo in (0, S):
                pool.affine_select(out=mask[:, lo:lo + P], in_=mask[:, lo:lo + P], compare_op=ALU.is_ge, fill=0.0,
                                   base=0, pattern=[[1, P]], channel_multiplier=-1).then_inc(const_ready, 1)
            fl = {"allow_small_or_imprecise_dtypes": True}
            pool.iota(back[:, :, :], pattern=[[0, TS], [-1, NE]], base=NE, channel_multiplier=0, **fl)\
                .then_inc(const_ready, 1)
            pool.iota(part_no[:, :], pattern=[[1, 1]], base=0, channel_multiplier=1, **fl).then_inc(const_ready, 1)
            for c in (place0[:, :], carry[:, 0, :]):
                pool.iota(c, pattern=[[NT * P, NE]], base=0, channel_multiplier=0, **fl).then_inc(const_ready, 1)
            pool.iota(assign_no[:, :, :], pattern=[[P * TOPK, NT], [1, TOPK]], base=1, channel_multiplier=TOPK, **fl)\
                .then_inc(const_ready, 1)
            pool.iota(dump_no[:, :], pattern=[[P, SLOT_TILES]], base=NASSIGN + 1, channel_multiplier=1, **fl)\
                .then_inc(const_ready, 1)
            pool.memset(zero_rows, 0.0).then_inc(table_zero, 1)
            pool.wait_ge(const_ready, N_CONST)

            def root(n, seq, eps):
                pool.wait_ge(mv_ready[n], seq + 1)
                pool.tensor_tensor(veps[:, n, :], mv[:, n, :, 1], eps[:, :], ALU.add).then_inc(veps_ready[n], 1)
                pool.wait_ge(veps_ready[n], seq + 1)
                pool.tensor_tensor(rstd[:, n, :], veps[:, n, :], halfneg[:, :], ALU.pow).then_inc(rstd_ready[n], 1)

            def add_bias(seq, row, after, done):
                hold(pool, after, seq + 1)
                xs = X[:, tiles_of(seq), :]
                pool.tensor_tensor(xs, xs, row[:, :].unsqueeze(1).broadcast_to([P, TS, D]), ALU.add).then_inc(done, 1)

            def split_ctx(seq):
                hold(pool, ctx_loaded, (seq + 1) * 16)
                pool.tensor_copy(ctx[0], ctx_raw).then_inc(ctx_hi, 1)
                hold(pool, ctx_hi, seq + 1)
                pool.tensor_tensor(ctx[1], ctx_raw, ctx[0].bitcast(F32), ALU.subtract).then_inc(ctx_ready, 1)

            RANK_STEPS = 3 + 4

            def place_assignments(r):
                step = [0]

                def then(ins):
                    step[0] += 1
                    ins.then_inc(ranked, 1)
                    pool.wait_ge(ranked, r * RANK_STEPS + step[0])

                if first(r):
                    pool.wait_ge(table_cleared, 16)
                else:
                    hold(pool, placed, r * 16 * TOPK * TS)
                pool.tensor_copy(assign[:, :], assign_no[:, tiles_of(r), :].rearrange("p t j -> p (t j)"))\
                    .then_inc(assign_ready, 1)
                pool.wait_ge(counts_ready, r + 1)
                then(pool.tensor_tensor(carry[:, 1, :], carry[:, 0, :], counts[:, TS, :], ALU.add))
                then(pool.tensor_tensor(upto[:, :, :], carry[:, :, :], counts[:, 0:TS, :], ALU.add))
                then(pool.tensor_tensor(carry[:, 0, :], carry[:, 1, :], counts[:, TS + 1, :], ALU.add))
                for j in range(TOPK):
                    last = pool.tensor_tensor(sums[:, j, :, :], hot[:, j, :, :], upto[:, :, :], ALU.mult)
                last.then_inc(hot_used, 1)
                pool.wait_ge(hot_used, r + 1)
                n = NE
                while n > 1:
                    n //= 2
                    then(pool.tensor_tensor(sums[:, :, :, 0:n], sums[:, :, :, 0:n], sums[:, :, :, n:2 * n], ALU.add))
                pool.sem_inc(held)
                pool.tensor_copy(place_i[:, :, :], sums[:, :, :, 0]).then_inc(place_ready, 1)
                hold(pool, place_ready, r + 1)
                hold(pool, assign_ready, r + 1)
                for j in range(TOPK):
                    for t in range(TS):
                        n = t * TOPK + j
                        pool.indirect_dma_start(table_flat, bass.IndirectOffsetOnAxis(place_i[:, j, t:t + 1], 0),
                                                assign[:, n:n + 1], None).then_inc(placed, 16)

            def turn(i, a, f, b, r, nxt):
                if a is not None:
                    hold(pool, xn_ready, a + 1)
                    if not first(a):
                        hold(pool, y_ready, a)
                    pool.tensor_copy(xn, xn_next).then_inc(xn_kept, 1)
                    add_bias(a, b2_sb, xn_ready, xb2_ready)
                if first(i):
                    for c in range(2):
                        half = slice(c * FC // 2, (c + 1) * FC // 2)
                        pool.wait_ge(split_hi, N_ATTN_SPLIT + 2 + (c + 1))
                        pool.tensor_tensor(w2[1][:, half, :], raw_w2[:, half, :], w2[0][:, half, :].bitcast(F32),
                                           ALU.subtract).then_inc(pool_split_lo, 1)
                    for n, (w, raw) in enumerate(((xwk, raw_xk), (xwv, raw_xv))):
                        pool.wait_ge(split_hi, N_ATTN_SPLIT + 5 + (n + 1))
                        pool.tensor_tensor(w[1], raw[:, :, :], w[0].bitcast(F32), ALU.subtract)\
                            .then_inc(pool_split_lo, 1)
                if isinstance(i, int) and i == 1:
                    pool.wait_ge(pool_split_lo, N_POOL_SPLIT)
                    pool.wait_ge(split_lo, N_DVE_SPLIT)
                    pool.wait_ge(b1_ps, 1)
                    split_ctx(0)
                if b is not None:
                    add_bias(b, bv_sb, xn2_ready, xbv_ready)
                    if not (isinstance(b, int) and b == NSEQ - 1):
                        hold(pool, v2_ps, b + 1)
                        split_ctx(b + 1)
                last_ffn = isinstance(i, int) and i == NSEQ
                last_cross = isinstance(i, int) and i == NSEQ + 1
                if r is not None and not last_ffn and not last_cross:
                    place_assignments(r)
                if nxt is not None:
                    root(0, nxt, eps_ln)
                if b is not None and not last_ffn:
                    root(3, b, eps_ln)
                if last_cross:
                    place_assignments(r)
                if f is not None:
                    root(2, f, eps_ln)
                if last_ffn:
                    root(3, b, eps_ln)
                if a is not None:
                    root(1, a, eps_attn)
                if last_ffn:
                    pool.wait_ge(w2_ps, NSEQ)
                    pool.wait_ge(rstd_ready[3], b + 1)
                    pool.memset(e2b[P // 4:LO].bitcast(F32), 0.0).then_inc(e2b_zero, 1)
                    pool.wait_ge(e2b_zero, 1)
                    place_assignments(r)

            root(0, 0, eps_ln)
            pool.wait_ge(ffn_loaded, 16 * 6)
            pool.wait_ge(cross_loaded, 16 * 7)
            in_turns(pool, turn)

            pool.wait_ge(placed, NSEQ * 16 * TOPK * TS)
            pool.wait_ge(row_ready, 1)
            pool.indirect_dma_start(by_tile[:, :], None, table_dram, bass.IndirectOffsetOnAxis(row_i[:, :], 0))\
                .then_inc(table_loaded, 16)

            pool.wait_ge(xn3_stored, 16 * NSEQ)
            pool.memset(hid, 0.0).then_inc(hid_zero, 1)
            pool.wait_ge(hid_zero, 1)

            pool.wait_ge(plan_ready, 1)

            def gather(s, u):
                hold(pool, gidx_ready, s + 1)
                pool.indirect_dma_start(xg[:, u, :], None, xn3_dram, bass.IndirectOffsetOnAxis(gidx[:, u:u + 1], 0))\
                    .then_inc(gathered[u], 16)

            def scatter(s, u):
                hold(pool, sidx_ready, s + 1)
                hold(pool, yg_ready, s + 1)
                pool.indirect_dma_start(y_dram, bass.IndirectOffsetOnAxis(sidx[:, u:u + 1], 0), yg[:, u, :], None)\
                    .then_inc(scattered[u], 16)

            for s in range(GB):
                gather(s, s)

            def slot_tiles(s, u, last):
                if not last:
                    gather(s + GB, u)
                if not (isinstance(s, int) and s < LAG):
                    scatter(s - LAG, (u - LAG) % GB)

            in_groups(slot_tiles, pool)
            for u in range(GB - LAG, GB):
                scatter(SLOT_TILES - GB + u, u)
            for u in range(GB):
                pool.wait_ge(scattered[u], 16 * (SLOT_TILES // GB))

        @block.tensor
        def _(pe):
            def mm(out_, lhsT, rhs, start=True, stop=True):
                return pe.matmul(out_, lhsT, rhs, start=start, stop=stop)

            def turn_tiles(bank, src):
                for c in range(DC):
                    for t in range(TS):
                        lo = c * S + t * P
                        last = pe.transpose(ps[:, bank, lo:lo + P], src[:, t, c * P:(c + 1) * P], ident[:, :])
                return last

            def mm3(out_, lhsT, rhs, at_l, at_r, start, stop):
                mm(out_, lhsT[0][at_l], rhs[0][at_r], start, False)
                mm(out_, lhsT[0][at_l], rhs[1][at_r], False, False)
                return mm(out_, lhsT[1][at_l], rhs[0][at_r], False, stop)

            def cols(c, lo, n):
                return (slice(None), c, slice(lo, lo + n))

            def by_token(bank, srcT, w):
                for t in range(TS):
                    for c in range(DC):
                        last = mm3(ps[:, bank, t * D:(t + 1) * D], srcT, w, cols(c, t * P, P), cols(c, 0, D),
                                   c == 0, c == DC - 1)
                return last

            def by_feature(bank, srcT, w):
                for e in range(DC):
                    for c in range(DC):
                        last = mm3(ps[:, bank, e * S:(e + 1) * S], w, srcT, cols(c, e * P, P), cols(c, 0, S),
                                   c == 0, c == DC - 1)
                return last

            def fuse(n):
                for c in range(DC):
                    for h in range(H):
                        lo = n * H * D + h * D + c * P
                        last = mm(ps[:, 2 * n + c, h * M:(h + 1) * M], raw_wT[:, lo:lo + P], raw_wT[:, 2 * H * D:])
                    last.then_inc(fused_ps, 1)

            def beta_w1(lo, hi):
                for ff in range(lo, hi):
                    for c in range(DC):
                        last = mm(ps[:, 4, ff:ff + 1], raw_w1[:, c, ff * P:(ff + 1) * P], bet_sb[:, c:c + 1],
                                  c == 0, c == DC - 1)
                return last

            def turn_next(a):
                pe.wait_ge(xn_ready, a + 1)
                turn_tiles(5, xn_next).then_inc(xnT_ps, 1)

            def turn_router_rows(b, bank):
                pe.wait_ge(xn3_ready, b + 1)
                turn_tiles(bank, xn3).then_inc(xn3T_ps, 1)

            def router(b, bank):
                pe.wait_ge(xn3T_ready, b + 1)
                for t in range(TS):
                    for c in range(DC):
                        last = mm(ps[:, bank, t * NE:(t + 1) * NE], xn3T[:, c, t * P:(t + 1) * P], wg_sb[:, c, :],
                                  c == 0, c == DC - 1)
                last.then_inc(logit_ps, 1)

            def turn(i, a, f, b, r, nxt):
                last_ffn = isinstance(i, int) and i == NSEQ
                last_cross = isinstance(i, int) and i == NSEQ + 1
                def project(g, w):
                    t = g % TS
                    for c in range(DC):
                        last = mm3(ps[:, g, :], xnT, w, cols(c, t * P, P), cols(c, 0, H * M), c == 0, c == DC - 1)
                    last.then_inc(proj_ps, 1)

                def ffn_in(g, bank):
                    for n in range(2):
                        for c in range(DC):
                            last = mm3(ps[:, bank, n * S:(n + 1) * S], w1, hT, cols(c, (2 * g + n) * P, P),
                                       cols(c, 0, S), c == 0, c == DC - 1)
                    last.then_inc(w1_ps, 1)

                if a is not None:
                    if first(a):
                        pe.wait_ge(split_lo, 4)
                    pe.wait_ge(xnT_ready, a + 1)
                    by_token(5, xnT, wv).then_inc(v_ps, 1)
                    project(0, wq)
                if b is not None:
                    pe.wait_ge(ctx_ready, b + 1)
                    by_feature(7, ctx, xwk).then_inc(k_ps, 1)
                    if last_cross:
                        pe.wait_ge(x2_ready, b)
                    elif not first(b):
                        pe.wait_ge(logit_ready, b)
                    pe.wait_ge(xn2_ready, b + 1)
                    turn_tiles(6, xn2).then_inc(xn2T_ps, 1)
                if a is not None:
                    project(1, wq)
                if f is not None:
                    pe.wait_ge(z_ready, f + 1)
                    turn_tiles(4, y).then_inc(zT_ps, 1)
                if b is not None:
                    pe.wait_ge(xn2T_ready, b + 1)
                    by_feature(6, xn2T, xwq).then_inc(q_ps, 1)
                if last_cross:
                    turn_router_rows(b - 1, 0)
                if f is not None:
                    if first(f):
                        pe.wait_ge(split_lo, N_DVE_SPLIT)
                        pe.wait_ge(pool_split_lo, N_POOL_SPLIT)
                    pe.wait_ge(hT_ready, f + 1)
                    ffn_in(0, 2)
                    ffn_in(1, 3)
                if b is not None:
                    pe.wait_ge(kT_ready, b + 1)
                    pe.wait_ge(qT_ready, b + 1)
                    for t in range(TS):
                        for c in range(DC):
                            last = mm3(ps[:, 7, t * S:(t + 1) * S], qT, kT, cols(c, t * P, P), cols(c, 0, S),
                                       c == 0, c == DC - 1)
                    last.then_inc(score_ps, 1)
                if last_cross:
                    router(b - 1, 1)
                def count_choices():
                    if a is not None:
                        pe.wait_ge(v1_ready, a + 1)
                    pe.wait_ge(oh_ready, r + 1)
                    oh_rows = oh[:, :, :].rearrange("p t e -> p (t e)")
                    mm(ps[:, 5, 0:TS * NE], before[:, :], oh_rows)
                    mm(ps[:, 5, TS * NE:2 * TS * NE], ones[:, :], oh_rows).then_inc(rank_ps, 1)

                if b is not None and not last_ffn:
                    by_token(6, ctx, xwv).then_inc(v2_ps, 1)
                if f is not None:
                    if a is not None:
                        pe.wait_ge(phi_ready, a * 4 + 2)
                    ffn_in(2, 0)
                if f is not None:
                    ffn_in(3, 1)
                if r is not None and not last_ffn and not last_cross:
                    count_choices()
                if a is not None:
                    if f is not None:
                        pe.wait_ge(relu_ready, f * 4 + 2)
                    if first(a):
                        pe.wait_ge(split_lo, N_ATTN_SPLIT)
                    project(2, wk)
                    project(3, wk)
                if last_ffn:
                    by_token(6, ctx, xwv).then_inc(v2_ps, 1)
                if b is not None:
                    pe.wait_ge(pr_ready, b + 1)
                    turn_tiles(7, pr).then_inc(prT_ps, 1)

                def ffn_out(t, lo, hi):
                    for ff in range(lo, hi):
                        last = mm3(ps[:, 4, t * D:(t + 1) * D], fT, w2, cols(ff, t * P, P), cols(ff, 0, D),
                                   ff == 0, ff == FC - 1)
                    return last

                if f is not None:
                    pe.wait_ge(fT_ready, f * 4 + 4)
                    ffn_out(0, 0, FC)
                if last_ffn:
                    ffn_out(1, 0, FC).then_inc(w2_ps, 1)
                    count_choices()

                def turn_phi(g0, done):
                    pe.wait_ge(phi_ready, a * 4 + (g0 + 2))
                    for h in range(H):
                        for t in range(TS):
                            last = pe.transpose(ps[:, g0 + h // 2, h % 2 * S + t * P:h % 2 * S + (t + 1) * P],
                                                phi[:, g0 + t, h, :], ident[:, :])
                        if h % 2:
                            last.then_inc(done, 1)

                if a is not None:
                    turn_phi(0, qpT_ps)
                    turn_phi(2, kpT_ps)
                if b is not None:
                    pe.wait_ge(prT_ready, b + 1)
                    pe.wait_ge(v2_ready, b + 1)
                    by_token(6, prT, v2).then_inc(av_ps, 1)
                if a is not None:
                    pe.wait_ge(qpT_ready, a + 1)
                    pe.wait_ge(kpT_ready, a + 1)
                    for h in range(H):
                        mm(ps[:, h, 0:S], kpT[:, h, 0:P], qpT[:, h, :])
                        mm(ps[:, h, S:ATW], kpT[:, h, P:S], qpT[:, h, P:S]).then_inc(aT_ps, 1)
                if f is not None and not last_ffn:
                    ffn_out(1, 0, FC // 2)
                if a is not None:
                    pe.wait_ge(v1_ready, a + 1)
                    for h in range(H):
                        pe.wait_ge(aT_ready, a * 4 + (h + 1 if h > 1 else 2))
                        col = slice(h * V1W, (h + 1) * V1W)
                        mm(ps[:, 0, col], aT[:, h, 0:P], v1[:, 0, h, :])
                        mm(ps[:, 1, col], aT[:, h, P:S], v1[:, 0, h, :], True, False)
                        last = mm(ps[:, 1, col], aT[:, h, S:ATW], v1[:, 1, h, :], False, True)
                    last.then_inc(num_ps, 1)
                if first(i):
                    pe.wait_ge(ffn_loaded, 16 * 6)
                    beta_w1(0, 4)
                if last_cross:
                    count_choices()
                if f is not None and not last_ffn:
                    ffn_out(1, FC // 2, FC - 2)
                if b is not None and not last_ffn:
                    turn_router_rows(b, 7)
                if first(i):
                    beta_w1(4, FC).then_inc(b1_ps, 1)
                if nxt is not None:
                    if r is not None:
                        pe.wait_ge(counts_ready, r + 1)
                    turn_next(nxt)
                if a is not None:
                    pe.wait_ge(attn_ready, a + 1)
                    turn_tiles(2, attn).then_inc(attnT_ps, 1)
                if f is not None and not last_ffn:
                    ffn_out(1, FC - 2, FC).then_inc(w2_ps, 1)
                if b is not None and not last_ffn:
                    router(b, 6)
                if a is not None:
                    pe.wait_ge(attnT_ready, a + 1)
                    by_token(3, attnT, wo).then_inc(wo_ps, 1)

            pe.wait_ge(fuse_loaded, 16 * 3)
            pe.wait_ge(const_ready, N_CONST)
            fuse(0)
            turn_next(0)
            fuse(1)
            in_turns(pe, turn)

            pe.wait_ge(row_ready, 1)
            mm(ps[0:1, 1, 0:P], expert_of_tile[:, :], ident[:, :]).then_inc(expert_ps, 1)
            pe.wait_ge(table_loaded, 16)
            pe.transpose(ps[:, 2, 0:P], by_tile[:, :], ident[:, :]).then_inc(table_ps, 1)

            pe.wait_ge(em_loaded, 16 * 4)
            pe.wait_ge(e2_ready, 8)
            pe.wait_ge(plan_ready, 1)

            def expert_of(s):
                return pe.value_load(expert_i[0:1, bass.ds(s, 1)], min_val=0, max_val=NE - 1)

            def turn_rows(s, u):
                pe.wait_ge(gathered[u], (s - u) * PER + 16)
                for c in range(DC):
                    last = pe.transpose(ps[:, u % 2, c * P:(c + 1) * P], xg[:, u, c * P:(c + 1) * P], ident[:, :])
                last.then_inc(xgT_ps, 1)

            def up(s, u):
                e = expert_of(s)
                pe.wait_ge(xgT_ready, s + 1)
                for c in range(DC):
                    last = mm(ps[:, 2 + u % 2, 0:2 * INTER], xgT[:, u % 2, c, :],
                              e13_sb[:, c, bass.ds(e, 1), :].rearrange("p e i -> p (e i)"), c == 0, c == DC - 1)
                last.then_inc(e13_ps, 1)

            def turn_hidden(s, u):
                pe.wait_ge(hid_ready, s + 1)
                for c in range(2):
                    last = pe.transpose(ps[:, 4 + u % 2, c * P:(c + 1) * P], hid[:, u % 2, c * P:(c + 1) * P],
                                        ident[:, :])
                last.then_inc(hidT_ps, 1)

            def down(s, u):
                e = expert_of(s)
                if not (isinstance(s, int) and s < 2):
                    pe.wait_ge(yg_ready, s - 1)
                pe.wait_ge(hidT_ready, s + 1)

                def part(hid_part, c, w, rows, start, stop):
                    return mm(ps[:, 6 + u % 2, 0:D], hidT[hid_part][0:rows, u % 2, c, :],
                              w[0:rows, bass.ds(e, 1), :].rearrange("p e d -> p (e d)"), start, stop)

                part(0, 0, e2a[0], P, True, False)
                part(0, 0, e2a[1], P, False, False)
                part(1, 0, e2a[0], P, False, False)
                part(0, 1, e2b, LO + IR, False, False)
                part(1, 1, e2b, IR, False, True).then_inc(e2_ps, 1)

            turn_rows(0, 0)
            turn_rows(1, 1)
            up(0, 0)

            def slot_tiles(s, u, last):
                if not (last and u + 2 >= GB):
                    turn_rows(s + 2, (u + 2) % GB)
                if not (last and u + 1 >= GB):
                    up(s + 1, (u + 1) % GB)
                if not first(s):
                    down(s - 1, (u - 1) % GB)
                turn_hidden(s, u)

            in_groups(slot_tiles, pe)
            down(SLOT_TILES - 1, GB - 1)

        @block.scalar
        def _(act):
            def copy(out_, in_):
                return act.activation(out_, in_, ACT.Copy)

            def bank(n):
                return ps[:, n, :].rearrange("p (a b) -> p a b", a=2)

            def e2a_first(q):
                part = slice(q * QE, (q + 1) * QE)
                copy(e2a[0][:, part, :], e2a[1][:, part, :].bitcast(F32)).then_inc(e2_hi, 1)

            def e2_rounded(q):
                copy(e2_tmp[q % 2][LO:LO + IR, :, :], e2b[LO:LO + IR, q * QE:(q + 1) * QE, :].bitcast(F32))\
                    .then_inc(e2_hi, 1)

            def copy_next(a):
                act.wait_ge(xnT_ps, a + 1)
                copy(xnT[0], bank(5)).then_inc(xnT_hi, 1)

            def split_fused(n, w):
                for c in range(DC):
                    act.wait_ge(fused_ps, 2 * n + c + 1)
                    act.mul(w[0][:, c, :], ps[:, 2 * n + c, :], PROJ_SCALE).then_inc(split_hi, 1)

            act.wait_ge(const_ready, N_CONST)
            act.wait_ge(attn_loaded, 16 * 2)
            for w, raw in ((wv, raw_v), (wo, raw_o)):
                copy(w[0], raw[:, :, :]).then_inc(split_hi, 1)
            split_fused(0, wq)
            copy_next(0)
            split_fused(1, wk)
            act.wait_ge(ffn_loaded, 16 * 6)
            for c in range(DC):
                act.activation(w1[0][:, c, :], raw_w1[:, c, :], ACT.Copy, scale=gam_sb[:, c:c + 1])\
                    .then_inc(split_hi, 1)
            for c in range(2):
                half = slice(c * FC // 2, (c + 1) * FC // 2)
                copy(w2[0][:, half, :], raw_w2[:, half, :]).then_inc(split_hi, 1)

            def copy_router_rows(b, bank_no):
                act.wait_ge(xn3T_ps, b + 1)
                copy(xn3T, bank(bank_no)).then_inc(xn3T_ready, 1)

            def turn(i, a, f, b, r, nxt):
                last_ffn = isinstance(i, int) and i == NSEQ
                last_cross = isinstance(i, int) and i == NSEQ + 1
                if a is not None:
                    act.wait_ge(v_ps, a + 1)
                    copy(v1[:, :, :, 0:DH], ps[:, 5, :].rearrange("p (t h d) -> p t h d", t=TS, h=H))\
                        .then_inc(v1_ready, 1)
                def features(g):
                    act.wait_ge(nmax_ready, a * 4 + (g + 1))
                    for h in range(H):
                        last = act.activation(phi[:, g, h, :], ps[:, g, h * M:(h + 1) * M], ACT.Exp,
                                              bias=nmax[:, g, h:h + 1])
                    last.then_inc(phi_ready, 1)

                def hidden(g, bank_no):
                    act.wait_ge(w1_ps, f * 4 + (g + 1))
                    if g >= 2:
                        act.wait_ge(fT_ready, f * 4 + (g - 1))
                    elif not first(f):
                        act.wait_ge(fT_ready, f * 4 + (g - 1))
                    for n in range(2):
                        bias = b1_sb[:, 2 * g + n:2 * g + n + 1]
                        act.activation(fT[0][:, 2 * g + n, :], bank(bank_no)[:, n, :], ACT.Relu, bias=bias)
                        last = act.activation(relu[:, g % 2, n, :], bank(bank_no)[:, n, :], ACT.Relu, bias=bias)
                    last.then_inc(relu_ready, 1)

                if b is not None:
                    act.wait_ge(xn2T_ps, b + 1)
                    copy(xn2T[0], bank(6)).then_inc(xn2T_hi, 1)
                if b is not None:
                    act.wait_ge(k_ps, b + 1)
                    for c in range(DC):
                        last = act.activation(kT[0][:, c, :], bank(7)[:, c, :], ACT.Identity, bias=bk_sb[:, c:c + 1])
                    last.then_inc(kT_hi, 1)
                if f is not None:
                    act.wait_ge(zT_ps, f + 1)
                    copy(hT[0], bank(4)).then_inc(hT_hi, 1)
                if a is not None:
                    features(0)
                if b is not None:
                    act.wait_ge(q_ps, b + 1)
                    for c in range(DC):
                        last = act.activation(qT[0][:, c, :], bank(6)[:, c, :], ACT.Identity, bias=bq_sb[:, c:c + 1])
                    last.then_inc(qT_hi, 1)
                if last_cross:
                    copy_router_rows(b - 1, 0)
                    act.wait_ge(e2_loaded, 16 * 3)
                    for q in range(2):
                        e2a_first(q)
                if a is not None:
                    features(1)
                if first(i):
                    act.wait_ge(cross_loaded, 16 * 7)
                    act.mul(xwq[0], raw_xq[:, :, :], SCORE_SCALE).then_inc(split_hi, 1)
                    copy(xwk[0], raw_xk[:, :, :]).then_inc(split_hi, 1)
                    copy(xwv[0], raw_xv[:, :, :]).then_inc(split_hi, 1)
                if f is not None:
                    if first(f):
                        act.wait_ge(split_lo, N_DVE_SPLIT)
                        act.wait_ge(pool_split_lo, N_POOL_SPLIT)
                        act.wait_ge(b1_ready, 1)
                        act.wait_ge(table_cleared, 16)
                    hidden(0, 2)
                    hidden(1, 3)
                if b is not None:
                    act.wait_ge(snmax_ready, b + 1)
                    for t in range(TS):
                        last = act.activation(pr[:, t, :], bank(7)[:, t, :], ACT.Exp, bias=snmax[:, t:t + 1],
                                              accum_out=ssum[:, t:t + 1])
                    last.then_inc(pr_ready, 1)
                def values_and_counts(seq_b, seq_r):
                    if seq_b is not None:
                        act.wait_ge(v2_ps, seq_b + 1)
                        copy(v2[0], bank(6)).then_inc(v2_hi, 1)
                    if seq_r is not None:
                        if not first(seq_r):
                            act.wait_ge(hot_used, seq_r)
                        act.wait_ge(rank_ps, seq_r + 1)
                        copy(counts[:, :, :].rearrange("p n e -> p (n e)"), ps[:, 5, 0:2 * TS * NE])\
                            .then_inc(counts_ready, 1)

                if last_ffn:
                    hidden(2, 0)
                    hidden(3, 1)
                    values_and_counts(b, None)
                else:
                    values_and_counts(b, None)
                    if f is not None:
                        hidden(2, 0)
                    if not last_cross:
                        values_and_counts(None, r)
                    if f is not None:
                        hidden(3, 1)
                if a is not None:
                    features(2)
                    features(3)
                if b is not None:
                    act.wait_ge(prT_ps, b + 1)
                    copy(prT[0], bank(7)).then_inc(prT_hi, 1)
                if last_ffn or last_cross:
                    values_and_counts(None, r)
                if last_cross:
                    for q in range(2, 4):
                        e2a_first(q)
                if a is not None:
                    for n in range(2):
                        act.wait_ge(qpT_ps, a * 2 + (n + 1))
                        last = act.activation(qpT[:, 2 * n:2 * n + 2, :], bank(n), ACT.Identity,
                                              bias=feat_eps[:, 0:1], scale=PHI_SCALE)
                    last.then_inc(qpT_ready, 1)
                if b is not None and not last_ffn:
                    if last_cross:
                        act.wait_ge(logit_ps, b)
                    copy_router_rows(b, 7)
                if a is not None:
                    act.wait_ge(attnT_ps, a + 1)
                    copy(attnT[0], bank(2)).then_inc(attnT_hi, 1)
                if nxt is not None:
                    copy_next(nxt)
                if last_cross:
                    for q in range(2):
                        e2_rounded(q)
                    for q in range(4):
                        part = slice(q * QE, (q + 1) * QE)
                        last = copy(e2b[0:IR, part, :], e2b[0:IR, part, :].bitcast(F32))
                    last.then_inc(e2_hi, 1)

            in_turns(act, turn)

            act.wait_ge(gap_ready, NSEQ)
            act.activation(egap[:, :], gap[:, :], ACT.Exp).then_inc(egap_ready, 1)
            act.activation(silu_first[:, :], feat_eps[:, :], ACT.Silu)
            for q in range(2, 4):
                act.wait_ge(e2_ready, 4 + (q - 1))
                e2_rounded(q)
            act.wait_ge(plan_ready, 1)

            def gate_half(s, u):
                if not (isinstance(s, int) and s < 2):
                    act.wait_ge(hid_ready, s - 1)
                act.wait_ge(e13_ps, s + 1)
                act.activation(silu[:, u % 2, :], ps[:, 2 + u % 2, 0:INTER], ACT.Silu).then_inc(silu_ready, 1)

            def hidden_hi(s, u):
                if not (isinstance(s, int) and s < 2):
                    act.wait_ge(e2_ps, s - 1)
                act.wait_ge(hidT_ps, s + 1)
                copy(hidT[0][:, u % 2], ps[:, 4 + u % 2, 0:2 * P].rearrange("p (c s) -> p c s", c=2))\
                    .then_inc(hidT_hi, 1)

            def rows_out(s, u):
                if not (isinstance(s, int) and s < GB):
                    act.wait_ge(scattered[u], (s - u) * PER)
                act.wait_ge(e2_ps, s + 1)
                copy(yg[:, u, :], ps[:, 6 + u % 2, 0:D]).then_inc(yg_ready, 1)

            gate_half(0, 0)

            def slot_tiles(s, u, last):
                if not (last and u + 1 >= GB):
                    gate_half(s + 1, (u + 1) % GB)
                if not first(s):
                    rows_out(s - 1, (u - 1) % GB)
                hidden_hi(s, u)

            in_groups(slot_tiles, act)
            rows_out(SLOT_TILES - 1, GB - 1)

            with act.Fori(0, NSEQ) as n:
                act.wait_ge(sum_ready, n + 1)
                act.dma_start(out_v[:, tiles_of(n), :], X[:, tiles_of(n), :]).then_inc(out_stored, 16)
            act.wait_ge(out_stored, 16 * NSEQ)

        @block.vector
        def _(dve):
            def bank(n):
                return ps[:, n, :].rearrange("p (a b) -> p a b", a=2)

            def x_tile(seq, t):
                return X[:, bass.ds(seq * TS + t, 1), :].rearrange("p t d -> p (t d)")

            def ln_stats(n, seq, src):
                for t in range(TS):
                    last = dve.bn_stats(stat[:, n, t, :], src(t))
                last.then_inc(stat_ready[n], 1)
                hold(dve, stat_ready[n], seq + 1)
                for t in range(TS):
                    last = dve.bn_aggr(mv[:, n, t, :], stat[:, n, t, :])
                last.then_inc(mv_ready[n], 1)

            def ln_apply(n, seq, src, dst, done):
                dve.wait_ge(mv_ready[n], seq + 1)
                dve.wait_ge(rstd_ready[n], seq + 1)
                for t in range(TS):
                    last = dve.tensor_scalar(dst[:, t, :], src(t), mv[:, n, t, 0:1], rstd[:, n, t:t + 1],
                                             ALU.subtract, ALU.mult)
                last.then_inc(done, 1)

            def rest(dst, whole, hi, waits, value, done):
                dve.wait_ge(waits, value)
                dve.tensor_tensor(dst, whole, hi.bitcast(F32), ALU.subtract).then_inc(done, 1)

            def rest_biased(dst, whole, bias, hi, waits, value, done):
                dve.wait_ge(waits, value)
                for c in range(DC):
                    last = dve.scalar_tensor_tensor(dst[:, c, :], whole[:, c, :], bias[:, c:c + 1],
                                                    hi[:, c, :].bitcast(F32), ALU.add, ALU.subtract)
                last.then_inc(done, 1)

            dve.wait_ge(const_ready, N_CONST)
            hold(dve, x_loaded, 16)
            ln_stats(0, 0, lambda t: x_tile(0, t))
            ln_apply(0, 0, lambda t: x_tile(0, t), xn_next, xn_ready)
            def rest_next(a):
                rest(xnT[1], bank(5), xnT[0], xnT_hi, a + 1, xnT_ready)

            def rest_fused(n, w):
                for c in range(DC):
                    dve.wait_ge(split_hi, 2 + 2 * n + c + 1)
                    dve.scalar_tensor_tensor(w[1][:, c, :], ps[:, 2 * n + c, :], PROJ_SCALE,
                                             w[0][:, c, :].bitcast(F32), ALU.mult, ALU.subtract).then_inc(split_lo, 1)

            for n, (w, raw) in enumerate(((wv, raw_v), (wo, raw_o))):
                rest(w[1], raw[:, :, :], w[0], split_hi, n + 1, split_lo)
            rest_fused(0, wq)
            rest_next(0)
            rest_fused(1, wk)
            for c in range(DC):
                dve.wait_ge(split_hi, N_ATTN_SPLIT + (c + 1))
                dve.scalar_tensor_tensor(w1[1][:, c, :], raw_w1[:, c, :], gam_sb[:, c:c + 1],
                                         w1[0][:, c, :].bitcast(F32), ALU.mult, ALU.subtract).then_inc(split_lo, 1)

            def e2_rest(q):
                part = slice(q % 4 * QE, (q % 4 + 1) * QE)
                dve.wait_ge(e2_hi, q + 1 if q < 6 else q + 2)
                if q < 4:
                    whole, rounded = e2a[1][:, part, :], e2a[0][:, part, :]
                else:
                    whole, rounded = e2b[LO:LO + IR, part, :], e2_tmp[q % 2][LO:LO + IR, :, :]
                dve.tensor_tensor(whole, whole.bitcast(F32), rounded.bitcast(F32), ALU.subtract).then_inc(e2_ready, 1)

            CHOICE_STEPS = 4 + 1 + 4

            def choose(r, j, scores):
                step = [j * 5]

                def then(ins):
                    step[0] += 1
                    ins.then_inc(chosen, 1)
                    dve.wait_ge(chosen, r * CHOICE_STEPS + step[0])

                then(dve.tensor_reduce(best[:, j, :], scores[:, :, :], AX_X, ALU.max))
                for t in range(TS):
                    last = dve.scalar_tensor_tensor(eq[:, t, :], scores[:, t, :], best[:, j, t:t + 1], back[:, t, :],
                                                    ALU.is_equal, ALU.mult)
                then(last)
                then(dve.tensor_reduce(pick[:, j, :], eq[:, :, :], AX_X, ALU.max))
                then(dve.tensor_tensor(hot[:, j], back[:, :, :], pick[:, j, :].unsqueeze(2).broadcast_to([P, TS, NE]),
                                       ALU.is_equal))
                if j == 0:
                    then(dve.scalar_tensor_tensor(masked[:, :, :], hot[:, 0], -3e38, scores[:, :, :],
                                                  ALU.mult, ALU.add))

            def logits_in(b, bank_no):
                hold(dve, logit_ps, b + 1)
                dve.tensor_copy(logits[:, :, :], ps[:, bank_no, 0:TS * NE].rearrange("p (t e) -> p t e", e=NE))\
                    .then_inc(logit_ready, 1)

            def first_sum(f):
                dve.wait_ge(w2_ps, f + 1)
                dve.wait_ge(xb2_ready, f + 1)
                xs = X[:, tiles_of(f), :]
                dve.tensor_tensor(xs, bank(4), xs, ALU.add).then_inc(x1_ready, 1)
                hold(dve, x1_ready, f + 1)
                ln_stats(2, f, lambda t: x_tile(f, t))

            def turn(i, a, f, b, r, nxt):
                last_ffn = isinstance(i, int) and i == NSEQ
                last_cross = isinstance(i, int) and i == NSEQ + 1
                def row_max(g):
                    dve.wait_ge(proj_ps, a * 4 + (g + 1))
                    dve.tensor_reduce(nmax[:, g, :], ps[:, g, :].rearrange("p (h m) -> p h m", h=H), AX_X, ALU.max,
                                      negate=True).then_inc(nmax_ready, 1)

                def hidden(g):
                    rest(fT[1][:, 2 * g:2 * g + 2, :], relu[:, g % 2], fT[0][:, 2 * g:2 * g + 2, :],
                         relu_ready, f * 4 + (g + 1), fT_ready)

                if a is not None:
                    row_max(0)
                if f is not None:
                    ln_apply(1, f, lambda t: y[:, t, :], y, z_ready)
                if b is not None:
                    rest(xn2T[1], bank(6), xn2T[0], xn2T_hi, b + 1, xn2T_ready)
                if b is not None:
                    rest_biased(kT[1], bank(7), bk_sb, kT[0], kT_hi, b + 1, kT_ready)
                if f is not None:
                    rest(hT[1], bank(4), hT[0], hT_hi, f + 1, hT_ready)
                if a is not None:
                    row_max(1)
                if b is not None:
                    rest_biased(qT[1], bank(6), bq_sb, qT[0], qT_hi, b + 1, qT_ready)
                def first_choice():
                    if not first(r):
                        dve.wait_ge(hot_used, r)
                    dve.wait_ge(logit_ready, r + 1)
                    choose(r, 0, logits)

                if r is not None and not last_cross:
                    first_choice()
                if f is not None:
                    hidden(0)
                if b is not None:
                    dve.wait_ge(score_ps, b + 1)
                    dve.tensor_reduce(snmax[:, :], bank(7), AX_X, ALU.max, negate=True).then_inc(snmax_ready, 1)
                if last_cross:
                    logits_in(b - 1, 1)
                    first_choice()
                if f is not None:
                    hidden(1)
                if last_ffn:
                    hidden(2)
                    hidden(3)
                if r is not None:
                    choose(r, 1, masked)
                    dve.tensor_tensor(oh[:, :, :], hot[:, 0], hot[:, 1], ALU.add).then_inc(oh_ready, 1)
                    dve.tensor_tensor(gap[:, tiles_of(r)], best[:, 1, :], best[:, 0, :], ALU.subtract)\
                        .then_inc(gap_ready, 1)
                if b is not None:
                    rest(v2[1], bank(6), v2[0], v2_hi, b + 1, v2_ready)
                if f is not None and not last_ffn:
                    hidden(2)
                    hidden(3)
                if a is not None:
                    row_max(2)
                    row_max(3)
                if first(i):
                    dve.wait_ge(split_hi, N_ATTN_SPLIT + 5)
                    dve.scalar_tensor_tensor(xwq[1], raw_xq[:, :, :], SCORE_SCALE, xwq[0].bitcast(F32),
                                             ALU.mult, ALU.subtract).then_inc(split_lo, 1)
                    dve.wait_ge(cross_loaded, 16 * 7)
                    dve.tensor_scalar(bq_sb[:, :], bq_sb[:, :], SCORE_SCALE, None, ALU.mult).then_inc(split_lo, 1)
                if b is not None:
                    rest(prT[1], bank(7), prT[0], prT_hi, b + 1, prT_ready)
                    dve.wait_ge(pr_ready, b + 1)
                    dve.reciprocal(rsum[:, :], ssum[:, :]).then_inc(rsum_ready, 1)
                if a is not None:
                    for n in range(2):
                        dve.wait_ge(kpT_ps, a * 2 + (n + 1))
                        last = dve.tensor_scalar(kpT[:, 2 * n:2 * n + 2, :], bank(2 + n), PHI_SCALE, FEAT_EPS,
                                                 ALU.mult, ALU.add)
                    last.then_inc(kpT_ready, 1)
                if nxt is not None:
                    hold(dve, x_loaded, (nxt + 1) * 16)
                    ln_stats(0, nxt, lambda t: x_tile(nxt, t))
                if last_cross:
                    e2_rest(0)
                if last_ffn:
                    first_sum(f)
                if b is not None:
                    dve.wait_ge(av_ps, b + 1)
                    dve.wait_ge(xbv_ready, b + 1)
                    dve.wait_ge(rsum_ready, b + 1)
                    for t in range(TS):
                        last = dve.scalar_tensor_tensor(x_tile(b, t), bank(6)[:, t, :], rsum[:, t:t + 1], x_tile(b, t),
                                                        ALU.mult, ALU.add)
                    last.then_inc(x2_ready, 1)
                if a is not None:
                    for h in range(H):
                        dve.wait_ge(aT_ps, a * 4 + (h + 1))
                        dve.tensor_tensor(aT[:, h, :], ps[:, h, 0:ATW], mask[:, :], ALU.mult).then_inc(aT_ready, 1)
                if b is not None:
                    hold(dve, x2_ready, b + 1)
                    ln_stats(3, b, lambda t: x_tile(b, t))
                if nxt is not None:
                    dve.wait_ge(xn_kept, nxt)
                    ln_apply(0, nxt, lambda t: x_tile(nxt, t), xn_next, xn_ready)
                if last_ffn:
                    ln_apply(2, f, lambda t: x_tile(f, t), xn2, xn2_ready)
                if b is not None:
                    if not first(b):
                        dve.wait_ge(xn3_stored, b * 16)
                    ln_apply(3, b, lambda t: x_tile(b, t), xn3, xn3_ready)
                if a is not None:
                    num = ps[:, 0:TS, 0:H * V1W].rearrange("p t (h d) -> p t h d", h=H)
                    dve.wait_ge(num_ps, a + 1)
                    dve.tensor_scalar(den[:, :, :], num[:, :, :, DH], FEAT_EPS, None, ALU.add).then_inc(den_ready, 1)
                    dve.wait_ge(den_ready, a + 1)
                    dve.reciprocal(rden[:, :, :], den[:, :, :]).then_inc(rden_ready, 1)
                    dve.wait_ge(rden_ready, a + 1)
                    dve.tensor_tensor(attn.rearrange("p t (h d) -> p t h d", h=H), num[:, :, :, 0:DH],
                                      rden[:, :, :].unsqueeze(3).broadcast_to([P, TS, H, DH]), ALU.mult)\
                        .then_inc(attn_ready, 1)
                    rest(attnT[1], bank(2), attnT[0], attnT_hi, a + 1, attnT_ready)
                if nxt is not None:
                    rest_next(nxt)
                if last_cross:
                    e2_rest(1)
                    e2_rest(2)
                if f is not None and not last_ffn:
                    first_sum(f)
                if b is not None and not last_ffn:
                    logits_in(b, 6)
                if a is not None:
                    dve.wait_ge(wo_ps, a + 1)
                    dve.wait_ge(xn_kept, a + 1)
                    dve.tensor_tensor(y, bank(3), xn, ALU.add).then_inc(y_ready, 1)
                    hold(dve, y_ready, a + 1)
                    ln_stats(1, a, lambda t: y[:, t, :])
                if f is not None and not last_ffn:
                    ln_apply(2, f, lambda t: x_tile(f, t), xn2, xn2_ready)
                if first(i):
                    dve.wait_ge(b1_ps, 1)
                    dve.tensor_tensor(b1_sb[:, :], ps[:, 4, 0:FC], b1_sb[:, :], ALU.add).then_inc(b1_ready, 1)

            in_turns(dve, turn)

            steps = [0]

            def then(ins):
                steps[0] += 1
                ins.then_inc(routed, 1)
                dve.wait_ge(routed, steps[0])

            dve.wait_ge(egap_ready, 1)
            then(dve.tensor_scalar(gden[:, :], egap[:, :], 1.0, None, ALU.add))
            then(dve.reciprocal(gate1[:, :], gden[:, :]))
            then(dve.tensor_tensor(gate2[:, :], gate1[:, :], egap[:, :], ALU.mult))
            dve.wait_ge(hot_used, NSEQ)
            then(dve.tensor_tensor(total[:, :], carry[:, 0, :], place0[:, :], ALU.subtract))
            then(dve.tensor_scalar(need_i[:, :], total[:, :], float(P - 1), None, ALU.add))
            then(dve.tensor_scalar(need_s[:, :], need_i[:, :], 7, None, ALU.logical_shift_right))
            then(dve.tensor_copy(need[:, :], need_s[:, :]))
            cum, cbufs, n = need, (cum_a, cum_b), 1
            while n < NE:
                dst = cbufs[0]
                cbufs = cbufs[::-1]
                dve.tensor_copy(dst[:, 0:n], cum[:, 0:n])
                then(dve.tensor_tensor(dst[:, n:], cum[:, n:], cum[:, 0:NE - n], ALU.add))
                cum, n = dst, 2 * n
            then(dve.tensor_scalar(ended[:, :], cum[:, :], part_no[:, :], None, ALU.is_le))
            dve.tensor_tensor(ended_need[:, :], ended[:, :], need[:, :], ALU.mult)
            then(dve.tensor_reduce(expert_of_tile[:, :], ended[:, :], AX_X, ALU.add))
            then(dve.tensor_reduce(first_tile[:, :], ended_need[:, :], AX_X, ALU.add))
            then(dve.tensor_tensor(row_f[:, :], part_no[:, :], first_tile[:, :], ALU.subtract))
            then(dve.scalar_tensor_tensor(row_g[:, :], expert_of_tile[:, :], float(NT), row_f[:, :],
                                          ALU.mult, ALU.add))
            dve.tensor_scalar(row_i[:, :], row_g[:, :], float(TABLE_ROWS - 1), None, ALU.min).then_inc(row_ready, 1)
            for q in range(3, 8):
                e2_rest(q)
            dve.wait_ge(expert_ps, 1)
            dve.tensor_scalar(expert_i[:, :], ps[0:1, 1, 0:SLOT_TILES], float(NE - 1), None, ALU.min)
            dve.wait_ge(table_ps, 1)
            then(dve.tensor_copy(table[:, :], ps[:, 2, 0:SLOT_TILES]))
            then(dve.tensor_scalar(empty[:, :], table[:, :], 0.0, None, ALU.is_equal))
            then(dve.tensor_tensor(gath_f[:, :], empty[:, :], dump_no[:, :], ALU.mult))
            then(dve.tensor_tensor(scat_f[:, :], table[:, :], gath_f[:, :], ALU.add))
            then(dve.tensor_scalar(scat_i[:, :], scat_f[:, :], -1.0, None, ALU.add))
            then(dve.tensor_scalar(gath_j[:, :], table[:, :], -1.0, 0.0, ALU.add, ALU.max))
            dve.tensor_scalar(gath_i[:, :], gath_j[:, :], 1, None, ALU.logical_shift_right).then_inc(plan_ready, 1)

            dve.wait_ge(plan_ready, 1)

            def rows_in(s, u):
                dve.wait_ge(xgT_ps, s + 1)
                dve.tensor_copy(xgT[:, u % 2], ps[:, u % 2, 0:D].rearrange("p (c s) -> p c s", c=DC))\
                    .then_inc(xgT_ready, 1)

            def product(s, u):
                dve.wait_ge(silu_ready, s + 1)
                dve.tensor_tensor(hid[:, u % 2, 0:INTER], ps[:, 2 + u % 2, INTER:2 * INTER], silu[:, u % 2, :],
                                  ALU.mult)
                dve.tensor_tensor(hid[:, u % 2, P + LO:LO + INTER], ps[:, 2 + u % 2, INTER + P:2 * INTER],
                                  silu[:, u % 2, P:INTER], ALU.mult).then_inc(hid_ready, 1)

            def hidden_in(s, u):
                dve.wait_ge(hidT_hi, s + 1)
                dve.tensor_tensor(hidT[1][:, u % 2], ps[:, 4 + u % 2, 0:2 * P].rearrange("p (c s) -> p c s", c=2),
                                  hidT[0][:, u % 2].bitcast(F32), ALU.subtract).then_inc(hidT_ready, 1)

            def gather_index(s, u):
                dve.tensor_copy(gidx[:, u:u + 1], gath_i[:, bass.ds(s, 1)]).then_inc(gidx_ready, 1)

            def scatter_index(s, u):
                if not (isinstance(s, int) and s < GB):
                    hold(dve, scattered[u], (s - u) * PER)
                dve.tensor_copy(sidx[:, u:u + 1], scat_i[:, bass.ds(s, 1)]).then_inc(sidx_ready, 1)

            for s in range(GB):
                gather_index(s, s)
            dve.wait_ge(hid_zero, 1)
            rows_in(0, 0)
            rows_in(1, 1)
            product(0, 0)

            def slot_tiles(s, u, last):
                if not (last and u + 2 >= GB):
                    rows_in(s + 2, (u + 2) % GB)
                if not (last and u + 1 >= GB):
                    product(s + 1, (u + 1) % GB)
                hidden_in(s, u)
                scatter_index(s, u)
                if not last:
                    gather_index(s + GB, u)

            in_groups(slot_tiles, dve)

            with dve.Fori(0, NSEQ // YB) as g:
                for u in range(YB):
                    n = g * YB + u
                    dve.wait_ge(y_loaded[u], g * 16 + 16)
                    for j, gate, done in ((0, gate1, part_ready), (1, gate2, sum_ready)):
                        for t in range(TS):
                            last = dve.scalar_tensor_tensor(x_tile(n, t), yl[:, u, t, j, :],
                                                            gate[:, bass.ds(n * TS + t, 1)], x_tile(n, t),
                                                            ALU.mult, ALU.add)
                        last.then_inc(done, 1)
                        if j == 0:
                            dve.wait_ge(part_ready, n + 1)




def kernel(**inputs):
    import numpy as np
    import concourse.bacc as bacc
    from concourse.bass_utils import run_bass_kernel_spmd

    def flat(name):
        return np.ascontiguousarray(inputs[name])

    def turned(name, axes=None):
        return np.ascontiguousarray(np.transpose(inputs[name], axes))

    def by_partition(name):
        return np.ascontiguousarray(inputs[name].reshape(-1, P).T)

    arrays = {
        "x": flat("x"),
        "ctxT": turned("ctx_1024", (0, 2, 1)),
        "WqT": turned("L0_attn_Wq"),
        "WkT": turned("L0_attn_Wk"),
        "Wv": flat("L0_attn_Wv"),
        "Wo": flat("L0_attn_Wo"),
        "omegaT": turned("L0_attn_omega"),
        "W1": flat("L0_attn_W1"),
        "b1": by_partition("L0_attn_b1"),
        "W2": flat("L0_attn_W2"),
        "b2": flat("L0_attn_b2"),
        "gamma": by_partition("L0_attn_gamma"),
        "beta": by_partition("L0_attn_beta"),
        "xWqT": turned("L0_xattn_Wq"),
        "xbq": by_partition("L0_xattn_bq"),
        "xWkT": turned("L0_xattn_Wk"),
        "xbk": by_partition("L0_xattn_bk"),
        "xWvT": turned("L0_xattn_Wv"),
        "xbv": flat("L0_xattn_bv"),
        "WgT": turned("L0_ffn_Wg"),
        "E1": flat("L0_ffn_W1"),
        "E3": flat("L0_ffn_W3"),
        "E2": flat("L0_ffn_W2"),
    }
    nc = bacc.Bacc("TRN2", target_bir_lowering=False, num_devices=1)
    aps = {n: nc.dram_tensor(f"in_{n}", a.shape, mybir.dt.from_np(a.dtype), kind="ExternalInput").ap()
           for n, a in arrays.items()}
    out = nc.dram_tensor("out", inputs["x"].shape, F32, kind="ExternalOutput").ap()
    decoder(nc, **aps, out=out)
    r = run_bass_kernel_spmd(nc, [{f"in_{n}": a for n, a in arrays.items()}], core_ids=[0])
    return r.results[0]["out"]
```
